# Optimizing a Trainium2 kernel written in Bass

```python
import numpy as np
import jax
import jax.numpy as jnp

def _softmax(x, axis=-1):
    return jax.nn.softmax(x, axis=axis)

def _gelu(x):
    return jax.nn.gelu(x, approximate=True)

def _silu(x):
    return jax.nn.silu(x)

def _sigmoid(x):
    return jax.nn.sigmoid(x)

def _layernorm(x, axis=-1, eps=1e-05):
    m = jnp.mean(x, axis=axis, keepdims=True)
    v = jnp.var(x, axis=axis, keepdims=True)
    return (x - m) / jnp.sqrt(v + eps)

def _scatter_add(tgt, idx, src, axis=0):
    return tgt.at[idx].add(src)

def _segment_sum(src, seg, n):
    return jax.ops.segment_sum(src, seg, n)
kernel_name = 'mk_gnn_ffn_d1_gnn_r32_1714d9'

def setup_inputs(seed: int=0):
    np.random.seed(seed)
    _w = jnp.asarray

    def _rec_inputs():
        import jax
        import jax.numpy as jnp
        _gk = jax.random.key(seed)
        x = 7.22e-05 + 1 * jax.random.normal(jax.random.fold_in(_gk, 1), (3125, 256), jnp.float32)
        _s = jax.random.randint(jax.random.fold_in(_gk, 2), (25000,), 0, 3125, jnp.int32)
        _d = jax.random.randint(jax.random.fold_in(_gk, 3), (25000,), 0, 3125, jnp.int32)
        _loop = jnp.arange(3125, dtype=jnp.int32)
        src = jnp.concatenate([_s, _d, _loop])
        dst = jnp.concatenate([_d, _s, _loop])
        _o = jnp.argsort(dst, stable=True)
        src = src[_o]
        dst = dst[_o]
        edge_attr_5 = jax.random.uniform(jax.random.fold_in(_gk, 11), (53125, 5), jnp.float32, 0.0, 99.9996)
        node_type_19 = jax.random.randint(jax.random.fold_in(_gk, 13), (3125,), 0, 19, jnp.int32)
        return (x, src, dst, edge_attr_5, node_type_19)
    x, src, dst, edge_attr_5, node_type_19 = _rec_inputs()

    def _L0_gnn_setup():
        import jax, jax.numpy as jnp
        import numpy as np
        N = 1024
        E = 4096
        IN = 256
        OUT = 256
        TD = 32
        H = 4
        T = 19
        PROJ = OUT - 2 * TD
        DK = (OUT - TD) // H
        SQRT_DK = float(np.sqrt(DK))
        LN_EPS = 1e-05

        def time_emb(t, w, b):
            return jnp.cos(jnp.log(t + 1.0)[:, None] * w[None, :] + b[None, :])

        def typed_linear(x, W, b, node_type):
            out = jnp.zeros((x.shape[0], W.shape[2]), x.dtype)
            for t in range(W.shape[0]):
                out = jnp.where((node_type == t)[:, None], x @ W[t] + b[t], out)
            return out

        def seg_softmax(att, idx, n):
            m = jax.ops.segment_max(att, idx, num_segments=n)
            e = jnp.exp(att - m[idx])
            s = jax.ops.segment_sum(e, idx, num_segments=n)
            return e / (s[idx] + 1e-16)
        key = jax.random.key(seed)
        ks = jax.random.split(key, 8)
        x = jax.random.normal(ks[0], (N, IN), jnp.float32)
        node_type = jax.random.randint(ks[1], (N,), 0, T, jnp.int32)
        edge_index = jax.random.randint(ks[2], (2, E), 0, N, jnp.int32)
        times = jax.random.uniform(ks[3], (E, 3), jnp.float32, 0.0, 100.0)
        edge_attr = jnp.concatenate([times, node_type[edge_index[0]][:, None].astype(jnp.float32), node_type[edge_index[1]][:, None].astype(jnp.float32)], axis=1)
        s = 0.02
        Wk = jax.random.normal(ks[4], (T, IN, PROJ), jnp.float32) * s
        Wq = jax.random.normal(ks[5], (T, IN, PROJ), jnp.float32) * s
        Wv = jax.random.normal(ks[6], (T, IN, PROJ), jnp.float32) * s
        bk = jnp.zeros((T, PROJ), jnp.float32)
        bq = jnp.zeros((T, PROJ), jnp.float32)
        bv = jnp.zeros((T, PROJ), jnp.float32)
        Wa = jax.random.normal(ks[7], (T, 2 * OUT, IN), jnp.float32) * s
        ba = jnp.zeros((T, IN), jnp.float32)
        gamma = jnp.ones((T, IN), jnp.float32)
        beta = jnp.zeros((T, IN), jnp.float32)
        w_time = jnp.asarray(1.0 / 10 ** np.linspace(0, 1.5, TD), jnp.float32)
        b_time = jnp.zeros((TD,), jnp.float32)
        return dict(x=x, node_type=node_type, edge_index=edge_index, edge_attr=edge_attr, Wk=Wk, bk=bk, Wq=Wq, bq=bq, Wv=Wv, bv=bv, Wa=Wa, ba=ba, gamma=gamma, beta=beta, w_time=w_time, b_time=b_time)
    _L0_gnn_all = _L0_gnn_setup()
    _L0_gnn_in = {k: v for k, v in _L0_gnn_all.items() if k in ('Wk', 'bk', 'Wq', 'bq', 'Wv', 'bv', 'Wa', 'ba', 'gamma', 'beta', 'w_time', 'b_time')}
    del _L0_gnn_all

    def _L0_ffn_setup():
        import jax, jax.numpy as jnp
        import numpy as np
        TOP_K = 2
        LN_EPS = 1e-05
        key = jax.random.key(seed)
        ks = jax.random.split(key, 8)
        B, S, D, E, H = (16, 1024, 256, 8, 1024)
        x = jax.random.normal(ks[0], (B, S, D), dtype=jnp.float32)
        Wr = jax.random.normal(ks[1], (D, E), dtype=jnp.float32) * 0.1
        br = jnp.zeros((E,), dtype=jnp.float32)
        ln_g = jnp.ones((E, D), dtype=jnp.float32)
        ln_b = jnp.zeros((E, D), dtype=jnp.float32)
        W1 = jax.random.normal(ks[2], (E, D, H), dtype=jnp.float32) * (1.0 / np.sqrt(D))
        b1 = jnp.zeros((E, H), dtype=jnp.float32)
        W2 = jax.random.normal(ks[3], (E, H, D), dtype=jnp.float32) * (1.0 / np.sqrt(H))
        b2 = jnp.zeros((E, D), dtype=jnp.float32)
        return {'x': x, 'Wr': Wr, 'br': br, 'ln_g': ln_g, 'ln_b': ln_b, 'W1': W1, 'b1': b1, 'W2': W2, 'b2': b2}
    _L0_ffn_all = _L0_ffn_setup()
    _L0_ffn_in = {k: v for k, v in _L0_ffn_all.items() if k in ('Wr', 'br', 'ln_g', 'ln_b', 'W1', 'b1', 'W2', 'b2')}
    del _L0_ffn_all
    return {'x': x, 'src': src, 'dst': dst, 'edge_attr_5': edge_attr_5, 'node_type_19': node_type_19, 'L0_gnn_Wk': _L0_gnn_in['Wk'], 'L0_gnn_bk': _L0_gnn_in['bk'], 'L0_gnn_Wq': _L0_gnn_in['Wq'], 'L0_gnn_bq': _L0_gnn_in['bq'], 'L0_gnn_Wv': _L0_gnn_in['Wv'], 'L0_gnn_bv': _L0_gnn_in['bv'], 'L0_gnn_Wa': _L0_gnn_in['Wa'], 'L0_gnn_ba': _L0_gnn_in['ba'], 'L0_gnn_gamma': _L0_gnn_in['gamma'], 'L0_gnn_beta': _L0_gnn_in['beta'], 'L0_gnn_w_time': _L0_gnn_in['w_time'], 'L0_gnn_b_time': _L0_gnn_in['b_time'], 'L0_ffn_Wr': _L0_ffn_in['Wr'], 'L0_ffn_br': _L0_ffn_in['br'], 'L0_ffn_ln_g': _L0_ffn_in['ln_g'], 'L0_ffn_ln_b': _L0_ffn_in['ln_b'], 'L0_ffn_W1': _L0_ffn_in['W1'], 'L0_ffn_b1': _L0_ffn_in['b1'], 'L0_ffn_W2': _L0_ffn_in['W2'], 'L0_ffn_b2': _L0_ffn_in['b2']}

def reference(x, src, dst, edge_attr_5, node_type_19, L0_gnn_Wk, L0_gnn_bk, L0_gnn_Wq, L0_gnn_bq, L0_gnn_Wv, L0_gnn_bv, L0_gnn_Wa, L0_gnn_ba, L0_gnn_gamma, L0_gnn_beta, L0_gnn_w_time, L0_gnn_b_time, L0_ffn_Wr, L0_ffn_br, L0_ffn_ln_g, L0_ffn_ln_b, L0_ffn_W1, L0_ffn_b1, L0_ffn_W2, L0_ffn_b2):
    import jax
    import jax.numpy as jnp

    def _L0_gnn_ref(x, node_type, edge_index, edge_attr, Wk, bk, Wq, bq, Wv, bv, Wa, ba, gamma, beta, w_time, b_time):
        import jax, jax.numpy as jnp
        import numpy as np
        N = 1024
        E = 4096
        IN = 256
        OUT = 256
        TD = 32
        H = 4
        T = 19
        PROJ = OUT - 2 * TD
        DK = (OUT - TD) // H
        SQRT_DK = float(np.sqrt(DK))
        LN_EPS = 1e-05

        def time_emb(t, w, b):
            return jnp.cos(jnp.log(t + 1.0)[:, None] * w[None, :] + b[None, :])

        def typed_linear(x, W, b, node_type):
            out = jnp.zeros((x.shape[0], W.shape[2]), x.dtype)
            for t in range(W.shape[0]):
                out = jnp.where((node_type == t)[:, None], x @ W[t] + b[t], out)
            return out

        def seg_softmax(att, idx, n):
            m = jax.ops.segment_max(att, idx, num_segments=n)
            e = jnp.exp(att - m[idx])
            s = jax.ops.segment_sum(e, idx, num_segments=n)
            return e / (s[idx] + 1e-16)
        row, col = (edge_index[0], edge_index[1])
        n = x.shape[0]
        K = typed_linear(x, Wk, bk, node_type)
        Q = typed_linear(x, Wq, bq, node_type)
        V = typed_linear(x, Wv, bv, node_type)
        e0 = time_emb(edge_attr[:, 0], w_time, b_time)
        e1 = time_emb(edge_attr[:, 1], w_time, b_time)
        e2 = time_emb(edge_attr[:, 2], w_time, b_time)

        def edge_msgs(Kn, Qn, Vn, ek, eq):
            k = jnp.concatenate([Kn, ek], axis=1).reshape(-1, H, DK)
            q = jnp.concatenate([Qn, eq], axis=1).reshape(-1, H, DK)
            att = jnp.einsum('ehd,ed->eh', k, q.sum(axis=1)) / SQRT_DK
            v = jnp.concatenate([Vn, ek], axis=1).reshape(-1, H, DK)
            return (att, v)
        att, v = edge_msgs(K[row], Q[col], V[row], e1, e2)
        att_i, v_i = edge_msgs(K[col], Q[row], V[col], e2, e1)
        att = seg_softmax(att, col, n)
        att_i = seg_softmax(att_i, row, n)
        res = (v * att[:, :, None]).reshape(-1, H * DK)
        res = jnp.concatenate([res, e0], axis=1)
        res_i = (v_i * att_i[:, :, None]).reshape(-1, H * DK)
        res_i = jnp.concatenate([res_i, e0], axis=1)
        agg = jax.ops.segment_sum(res, col, num_segments=n) + jax.ops.segment_sum(res_i, row, num_segments=n)
        h = jnp.concatenate([agg, agg], axis=1)
        o = typed_linear(h, Wa, ba, node_type)
        y = o + x
        mu = y.mean(axis=-1, keepdims=True)
        var = y.var(axis=-1, keepdims=True)
        yn = (y - mu) / jnp.sqrt(var + LN_EPS)
        return yn * gamma[node_type] + beta[node_type]

    def _L0_ffn_ref(x, Wr, br, ln_g, ln_b, W1, b1, W2, b2):
        import jax, jax.numpy as jnp
        import numpy as np
        TOP_K = 2
        LN_EPS = 1e-05
        B, S, D = x.shape
        N = B * S
        xt = x.reshape(N, D)
        logits = xt @ Wr + br
        probs = jax.nn.softmax(logits, axis=-1)
        top_p, top_idx = jax.lax.top_k(probs, TOP_K)
        weights = top_p / top_p.sum(axis=-1, keepdims=True)
        mu = xt.mean(axis=-1, keepdims=True)
        var = ((xt - mu) ** 2).mean(axis=-1, keepdims=True)
        xn = (xt - mu) * jax.lax.rsqrt(var + LN_EPS)
        xe = xn[None, :, :] * ln_g[:, None, :] + ln_b[:, None, :]
        h = jax.nn.gelu(jnp.einsum('end,edh->enh', xe, W1) + b1[:, None, :], approximate=False)
        y = jnp.einsum('enh,ehd->end', h, W2) + b2[:, None, :]
        y_tok = jnp.transpose(y, (1, 0, 2))
        sel = jnp.take_along_axis(y_tok, top_idx[:, :, None], axis=1)
        out = (weights[:, :, None] * sel).sum(axis=1)
        return out.reshape(B, S, D)
    edge_index = jnp.stack([src, dst])
    x = x + _L0_gnn_ref(_layernorm(x, axis=-1), node_type_19, edge_index, edge_attr_5, L0_gnn_Wk, L0_gnn_bk, L0_gnn_Wq, L0_gnn_bq, L0_gnn_Wv, L0_gnn_bv, L0_gnn_Wa, L0_gnn_ba, L0_gnn_gamma, L0_gnn_beta, L0_gnn_w_time, L0_gnn_b_time)
    x = x + _L0_ffn_ref(_layernorm(x, axis=-1)[None], L0_ffn_Wr, L0_ffn_br, L0_ffn_ln_g, L0_ffn_ln_b, L0_ffn_W1, L0_ffn_b1, L0_ffn_W2, L0_ffn_b2)[0]
    return x

_drawn_inputs = setup_inputs


def setup_inputs(seed=0):
    import zlib

    import numpy as np

    out = dict(_drawn_inputs(seed))
    spreads = {'L0_gnn_bk': (0.0, 0.8),
     'L0_gnn_bq': (0.0, 0.8),
     'L0_gnn_bv': (0.0, 0.599),
     'L0_gnn_ba': (0.0, 0.1),
     'L0_gnn_gamma': (1.0, 0.2),
     'L0_gnn_beta': (0.0, 0.1),
     'L0_gnn_b_time': (0.0, 0.1),
     'L0_ffn_br': (0.0, 0.1),
     'L0_ffn_ln_g': (1.0, 0.2),
     'L0_ffn_ln_b': (0.0, 0.1),
     'L0_ffn_b1': (0.0, 0.1),
     'L0_ffn_b2': (0.0, 0.1)}
    factors = {'L0_gnn_Wk': 6.44, 'L0_gnn_Wq': 8.0, 'L0_gnn_Wv': 2.78}
    for name, (base, spread) in spreads.items():
        noise = np.random.default_rng([zlib.crc32(name.encode()), seed]).standard_normal(out[name].shape)
        drawn = base * np.exp(spread * noise) if base else spread * noise
        out[name] = jnp.asarray(drawn.astype(out[name].dtype))
    for name, factor in factors.items():
        out[name] = (out[name] * factor).astype(out[name].dtype)
    return out
```

```python
from contextlib import ExitStack

import concourse.bass as bass
from concourse import mybir

F32 = mybir.dt.float32
I32 = mybir.dt.int32
BF16 = mybir.dt.bfloat16
ALU = mybir.AluOpType
ACT = mybir.ActivationFunctionType
AX = mybir.AxisListType.X

P = 128
TWO_PI = 6.283185307179586
SIN_SCALE = 6.283185
MAGIC = 12582912.0
BIG = 1.0e30
RESET = -2.0e38
LN_EPS = 1e-5


class Chain:

    def __init__(self, eng, sem, base=0):
        self.eng, self.sem, self.base, self.n = eng, sem, base, 0

    def __call__(self, ins):
        self.n += 1
        ins.then_inc(self.sem, 1)
        self.eng.wait_ge(self.sem, self.base + self.n)


class At:

    def __init__(self, i, c):
        self.i, self.c, self.t = i, c, i * 4 + c

    def slot(self, k):
        return self.c % k

    def turn(self, k):
        return self.i * (4 // k) + self.c // k

    def __add__(self, n):
        return At(self.i, self.c + n)


def walk(eng, steps, step):
    step(At(0, 0))
    step(At(0, 1))
    loops = (steps - 2) // 4
    with eng.Fori(0, loops) as i:
        for u in range(4):
            step(At(i, 2 + u))
    for t in range(2 + 4 * loops, steps):
        step(At(0, t))


def wait_done(eng, sem, a, back=0):
    if a.c >= back:
        eng.wait_ge(sem, a.t + (1 - back))


class Dims:

    def __init__(self, x, src, Wk, Wa, w_time, W1):
        self.N, self.D = x.shape
        self.E = src.shape[0]
        self.T, _, self.PROJ = Wk.shape
        self.TD = w_time.shape[0]
        self.KD = self.D // P
        self.H = 4
        self.DK = (self.D - self.TD) // self.H
        self.LAST = self.PROJ - 3 * self.DK
        self.NB = -(-self.N // P)
        self.NP = self.NB * P
        self.FULL = self.N // P
        self.TAIL = self.N - self.FULL * P
        self.C = 8
        self.EC = -(-self.E // (P * self.C)) * self.C
        self.EFULL = self.E // self.EC
        self.ETAIL = self.E - self.EFULL * self.EC
        self.KB = 2 * self.NB
        self.G = 4
        self.R = 4
        rows = 2 * self.EC * P // self.G + self.KB * P
        self.RT = -(-rows // (P * self.R)) * self.R
        self.NR = self.RT * P
        self.QKV = 2 * self.PROJ + self.DK
        self.MSG = self.D + self.H
        self.X, _, self.HID = W1.shape


def gnn_ffn_kernel(nc, x, src, dst, edge_attr, node_type, Wk, bk, Wq, bq, Wv, bv, Wa, ba, gamma, beta,
                   w_time, b_time, Wr, br, ln_g, ln_b, W1, b1, W2, b2, out):
    d = Dims(x, src, Wk, Wa, w_time, W1)
    N, D, E, T, KD, NB, NPAD = d.N, d.D, d.E, d.T, d.KD, d.NB, d.NP
    PROJ, TD, H, DK, LAST = d.PROJ, d.TD, d.H, d.DK, d.LAST
    G, R, RT, NR, KB, EC, C = d.G, d.R, d.RT, d.NR, d.KB, d.EC, d.C
    ds = bass.ds

    kv_dram = nc.dram_tensor("kv_table", (1 + NPAD, 2 * PROJ), F32).ap()
    q_dram = nc.dram_tensor("q_table", (NPAD, DK), F32).ap()
    keyrow_dram = nc.dram_tensor("key_rows", (2 * EC, P), F32).ap()
    lorow_dram = nc.dram_tensor("lo_rows", (2 * EC, P), F32).ap()
    rec_dram = nc.dram_tensor("edge_records", (NR * G, 4), F32).ap()
    marks_dram = nc.dram_tensor("row_marks", (NR + P, 1), F32).ap()
    part_dram = nc.dram_tensor("row_messages", (NR, d.MSG), F32).ap()
    wk_dram = nc.dram_tensor("row_weights", (NR, H + 1), F32).ap()

    top = ExitStack()
    with top:
        def sbuf(ctx, name, shape, dt=F32):
            return ctx.enter_context(nc.sbuf_tensor(name, shape, dt))

        def psum(ctx, name, shape, dt=F32):
            return ctx.enter_context(nc.psum_tensor(name, shape, dt))

        def sems(*names):
            return [top.enter_context(nc.semaphore(n)) for n in names]

        pool_turn, = sems("pool_turn")

        xn = sbuf(top, "xn", [P, NB, D])
        res = sbuf(top, "res", [P, NB, D])
        ident = sbuf(top, "ident", [P, P])
        ones = sbuf(top, "ones", [P, P])
        before = sbuf(top, "before", [P, P])
        after = sbuf(top, "after", [P, P])
        lane = sbuf(top, "lane", [P, 2 * P])
        lane_col = sbuf(top, "lane_col", [P, 1])
        magic = sbuf(top, "magic", [P, 1])
        type_onehot = sbuf(top, "type_onehot", [T, NPAD])
        type_bc = sbuf(top, "type_bc", [P, NPAD], I32)
        stats = sbuf(top, "stats", [P, NB, 6])
        mean = sbuf(top, "mean", [P, NB])
        rstd = sbuf(top, "rstd", [P, NB])
        tmp_a = sbuf(top, "tmp_a", [P, NB])
        tmp_b = sbuf(top, "tmp_b", [P, NB])

        def layer_norm_stats(dve, act_in, act_out, link, source, turn):
            for b in range(NB):
                last = dve.bn_stats(stats[:, b, :], source[:, b, :])
            link(last)
            link(dve.tensor_tensor(mean[:], stats[:, :, 1], stats[:, :, 4], ALU.add))
            link(dve.tensor_tensor(tmp_a[:], stats[:, :, 1], stats[:, :, 4], ALU.subtract))
            link(dve.tensor_tensor(tmp_b[:], stats[:, :, 2], stats[:, :, 5], ALU.add))
            link(dve.tensor_scalar(mean[:], mean[:], 0.5, None, ALU.mult))
            link(dve.tensor_tensor(tmp_a[:], tmp_a[:], tmp_a[:], ALU.mult))
            link(dve.tensor_scalar(tmp_a[:], tmp_a[:], 0.25, LN_EPS, ALU.mult, ALU.add))
            dve.scalar_tensor_tensor(tmp_b[:], tmp_b[:], 1.0 / D, tmp_a[:], ALU.mult, ALU.add).then_inc(act_in, 1)
            dve.wait_ge(act_out, turn)
            link(dve.reciprocal(rstd[:], rstd[:]))

        def normalize(dve, dst_t, source):
            for b in range(NB):
                last = dve.tensor_scalar(dst_t[:, b, :], source[:, b, :], mean[:, b:b + 1], rstd[:, b:b + 1],
                                         ALU.subtract, ALU.mult)
            return last

        with ExitStack() as ctx:
            wcat = sbuf(ctx, "wcat", [P, T * KD, d.QKV])
            wq_st = sbuf(ctx, "wq_st", [P, T * KD, PROJ])
            bcat = sbuf(ctx, "bcat", [T, d.QKV])
            bq_st = sbuf(ctx, "bq_st", [T, PROJ])
            x_sb = xn
            xT = res[:].rearrange("p b c -> p (b c)").rearrange("p (k n) -> p k n", k=KD)
            masked = sbuf(ctx, "masked", [P, 4, KD, P])
            qkv = sbuf(ctx, "qkv", [P, d.QKV])
            onehot_st = sbuf(ctx, "onehot_st", [T, P])
            zero_row = sbuf(ctx, "zero_row", [1, 2 * PROJ])
            ps_t = psum(ctx, "ps_t", [P, 2, 512])
            ps_qkv = psum(ctx, "ps_qkv", [P, 512])
            x_in, type_in, wq_in, w_in = sems("x_in", "type_in", "wq_in", "w_in")
            zeroed, consts, var_ready, std_ready = sems("zeroed", "consts", "var_ready", "std_ready")
            dve_chain, xn_ready, tp_ready, xT_ready = sems("dve_chain", "xn_ready", "tp_ready", "xT_ready")
            mask_ready, mask_used, qkv_ready, qkv_copied = sems("mask_ready", "mask_used", "qkv_ready", "qkv_copied")
            stored, zero_out, q_folded, const_chain = sems("stored", "zero_out", "q_folded", "const_chain")
            block = ctx.enter_context(nc.Block())

            @block.sync
            def _(sp):
                sp.wait_ge(zeroed, 3)
                sp.dma_start(x_sb[:, 0:d.FULL, :], x[0:d.FULL * P, :].rearrange("(b p) c -> p b c", p=P)).then_inc(x_in, 16)
                sp.dma_start(x_sb[0:d.TAIL, d.FULL, :], x[d.FULL * P:N, :]).then_inc(x_in, 16)
                sp.dma_start(type_bc[:, 0:N], node_type.rearrange("(o n) -> o n", o=1).broadcast_to([P, N])).then_inc(type_in, 16)
                sp.dma_start(wq_st[:], Wq.rearrange("t (k p) c -> p (t k) c", p=P)).then_inc(wq_in, 16)
                sp.dma_start(bq_st[:], bq).then_inc(wq_in, 16)
                sp.dma_start(wcat[:, :, 0:PROJ], Wk.rearrange("t (k p) c -> p (t k) c", p=P)).then_inc(w_in, 16)
                sp.dma_start(wcat[:, :, PROJ:2 * PROJ], Wv.rearrange("t (k p) c -> p (t k) c", p=P)).then_inc(w_in, 16)
                sp.dma_start(bcat[:, 0:PROJ], bk).then_inc(w_in, 16)
                sp.dma_start(bcat[:, PROJ:2 * PROJ], bv).then_inc(w_in, 16)
                sp.dma_start(kv_dram[0:1, :], zero_row[:]).then_inc(zero_out, 16)
                with sp.Fori(0, NB) as b:
                    sp.wait_ge(qkv_copied, b + 1)
                    sp.dma_start(kv_dram[ds(b * P + 1, P), :], qkv[:, 0:2 * PROJ]).then_inc(stored, 16)
                    sp.dma_start(q_dram[ds(b * P, P), :], qkv[:, 2 * PROJ:d.QKV]).then_inc(stored, 16)
                sp.wait_ge(stored, 32 * NB)
                sp.wait_ge(zero_out, 16)

            @block.gpsimd
            def _(pool):
                pool.memset(x_sb[:, d.FULL:NB, :], 0.0).then_inc(zeroed, 1)
                pool.memset(type_bc[:, N:NPAD], 0).then_inc(zeroed, 1)
                pool.memset(zero_row[:], 0.0).then_inc(zeroed, 1)
                pool.memset(magic[:], MAGIC)
                pool.memset(ones[:], 1.0).then_inc(const_chain, 1)
                pool.iota(lane[:], [[1, 2 * P]], base=0, channel_multiplier=0,
                          allow_small_or_imprecise_dtypes=True).then_inc(const_chain, 1)
                pool.iota(lane_col[:], [[0, 1]], base=0, channel_multiplier=1,
                          allow_small_or_imprecise_dtypes=True).then_inc(const_chain, 1)
                pool.wait_ge(const_chain, 3)
                pool.tensor_scalar(ident[:], lane[:, 0:P], lane_col[:, 0:1], None, ALU.is_equal).then_inc(consts, 1)
                pool.tensor_scalar(before[:], lane[:, 0:P], lane_col[:, 0:1], None, ALU.is_gt).then_inc(consts, 1)
                pool.tensor_scalar(after[:], lane[:, 0:P], lane_col[:, 0:1], None, ALU.is_lt).then_inc(consts, 1)

            @block.vector
            def _(dve):
                link = Chain(dve, dve_chain)
                dve.wait_ge(x_in, 32)
                layer_norm_stats(dve, var_ready, std_ready, link, x_sb, 1)
                normalize(dve, xn, x_sb).then_inc(xn_ready, 1)
                dve.wait_ge(wq_in, 32)
                for wt, wst in ((wcat[:, :, 2 * PROJ:d.QKV], wq_st[:, :, :]),
                                (bcat[:, 2 * PROJ:d.QKV], bq_st[:, :])):
                    cut = (lambda t, a, b: t[:, :, a:b]) if len(wt.shape) == 3 else (lambda t, a, b: t[:, a:b])
                    link(dve.tensor_tensor(wt, cut(wst, 0, DK), cut(wst, DK, 2 * DK), ALU.add))
                    link(dve.tensor_tensor(wt, wt, cut(wst, 2 * DK, 3 * DK), ALU.add))
                    link(dve.tensor_tensor(cut(wt, 0, LAST), cut(wt, 0, LAST), cut(wst, 3 * DK, PROJ), ALU.add))
                dve.wait_ge(type_in, 16)
                dve.wait_ge(consts, 3)
                link(dve.tensor_scalar(type_onehot[:], type_bc[0:T, :], lane_col[0:T, 0:1], None, ALU.is_equal))
                dve.sem_inc(q_folded, 1)
                with dve.Fori(0, NB) as b:
                    dve.wait_ge(xT_ready, b * KD + KD)
                    for t in range(T):
                        dve.wait_ge(mask_used, b * T if t < 4 else b * T + t - 3)
                        dve.scalar_tensor_tensor(masked[:, t % 4, :, :],
                                                 type_bc[:, ds(b * P, P)].unsqueeze(1).broadcast_to([P, KD, P]), float(t),
                                                 xT[:, :, ds(b * P, P)], ALU.is_equal, ALU.mult).then_inc(mask_ready, 1)
                    dve.wait_ge(qkv_ready, b)
                    dve.tensor_copy(onehot_st[:], type_onehot[:, ds(b * P, P)]).then_inc(mask_ready, 1)

            @block.scalar
            def _(act):
                act.wait_ge(var_ready, 1)
                act.activation(rstd[:], tmp_b[:], ACT.Sqrt).then_inc(std_ready, 1)
                with act.Fori(0, NB) as b:
                    for k in range(KD):
                        act.wait_ge(tp_ready, b * KD + k + 1)
                        act.copy(xT[:, k, ds(b * P, P)], ps_t[:, k, 0:P]).then_inc(xT_ready, 1)
                with act.Fori(0, NB) as b:
                    act.wait_ge(qkv_ready, b + 1)
                    act.wait_ge(stored, b * 32)
                    act.copy(qkv[:], ps_qkv[:, 0:d.QKV]).then_inc(qkv_copied, 1)

            @block.tensor
            def _(pe):
                pe.wait_ge(consts, 3)
                pe.wait_ge(xn_ready, 1)
                for b in range(NB):
                    for k in range(KD):
                        if b:
                            pe.wait_ge(xT_ready, b * KD + k - KD + 1)
                        pe.transpose(ps_t[:, k, 0:P], xn[:, b, k * P:(k + 1) * P], ident[:]).then_inc(tp_ready, 1)
                pe.wait_ge(w_in, 64)
                pe.wait_ge(q_folded, 1)
                with pe.Fori(0, NB) as b:
                    pe.wait_ge(qkv_copied, b)
                    for t in range(T):
                        pe.wait_ge(mask_ready, b * (T + 1) + t + 1)
                        for k in range(KD):
                            last = pe.matmul(ps_qkv[:, 0:d.QKV], masked[:, t % 4, k, :], wcat[:, t * KD + k, :],
                                             start=(t == 0 and k == 0), stop=False)
                        last.then_inc(mask_used, 1)
                    pe.wait_ge(mask_ready, (b + 1) * (T + 1))
                    pe.matmul(ps_qkv[:, 0:d.QKV], onehot_st[:], bcat[:], start=False, stop=True).then_inc(qkv_ready, 1)


        row_base = sbuf(top, "row_base", [P, KB])

        NC = 2 * EC // C
        edges = ExitStack()
        with edges:
            rec = sbuf(edges, "rec", [P, 2 * EC, 4])
            key_f = sbuf(edges, "key_f", [P, 2 * EC])
            lo_f = sbuf(edges, "lo_f", [P, 2 * EC])
            hi_f = sbuf(edges, "hi_f", [P, 2 * EC])

            with ExitStack() as ctx:
                ends = [sbuf(ctx, "src_i", [P, EC], I32), sbuf(ctx, "dst_i", [P, EC], I32)]
                attr = sbuf(ctx, "attr", [P, EC, edge_attr.shape[1]])
                key_i = sbuf(ctx, "key_i", [P, 2 * EC], I32)
                lo_i = sbuf(ctx, "lo_i", [P, 2 * EC], I32)
                hi_i = sbuf(ctx, "hi_i", [P, 2 * EC], I32)
                zeros = sbuf(ctx, "zeros", [P, NR * G * 4 // P])
                zeros_b = sbuf(ctx, "zeros_b", [P, P], BF16)
                TC = 104
                NTC = 2 * EC // TC
                rows_sb = sbuf(ctx, "rows_sb", [TC, 2, NTC, P])
                lane_b = sbuf(ctx, "lane_b", [P, P], BF16)
                lo_hot = sbuf(ctx, "lo_hot", [P, 2, C, P], BF16)
                hi_hot = sbuf(ctx, "hi_hot", [P, 2, C, KB], BF16)
                cnt_i = sbuf(ctx, "cnt_i", [P, KB], I32)
                rows_f = sbuf(ctx, "rows_f", [P, KB])
                totals = sbuf(ctx, "totals", [P, KB])
                upto = sbuf(ctx, "upto", [P, KB])
                within = sbuf(ctx, "within", [P, KB])
                ps_row = psum(ctx, "ps_row", [P, 2, 512])
                ps_cnt = psum(ctx, "ps_cnt", [P, 512])
                ps_pre = psum(ctx, "ps_pre", [P, 2, 512])
                e_clear, e_in, keys_ready, lanes_ready, e_chain = sems("e_clear", "e_in", "keys_ready", "lanes_ready", "e_chain")
                row_tp, row_copied, rows_out, zeros_out = sems("row_tp", "row_copied", "rows_out", "zeros_out")
                hot_ready, cnt_ready, rows_ready, pre_ready = sems("hot_ready", "cnt_ready", "rows_ready", "pre_ready")
                hot_used = sems("hot_used0", "hot_used1")
                block = ctx.enter_context(nc.Block())

                @block.sync
                def _(sp):
                    sp.wait_ge(e_clear, 3)
                    for t, a in ((ends[0][:], src.rearrange("(n o) -> n o", o=1)),
                                 (ends[1][:], dst.rearrange("(n o) -> n o", o=1)),
                                 (attr[:].rearrange("p c a -> p (c a)"), edge_attr)):
                        sp.dma_start(t[0:d.EFULL, :], a[0:d.EFULL * EC, :].rearrange("(p c) a -> p (c a)", p=d.EFULL)).then_inc(e_in, 16)
                        sp.dma_start(t[d.EFULL:P, 0:d.ETAIL * a.shape[1]],
                                     a[d.EFULL * EC:E, :].rearrange("(p c) a -> p (c a)", p=1)).then_inc(e_in, 16)
                    sp.wait_ge(e_clear, 4)
                    sp.dma_start(rec_dram.rearrange("(p c) w -> p (c w)", p=P), zeros[:]).then_inc(zeros_out, 16)
                    sp.dma_start(marks_dram.rearrange("(p c) w -> p (c w)", p=P), zeros[:, 0:NR // P + 1]).then_inc(zeros_out, 16)
                    sp.wait_ge(row_copied, 2 * NTC)
                    for n, t in enumerate((keyrow_dram, lorow_dram)):
                        sp.dma_start(t.rearrange("(b r) c -> r b c", r=TC), rows_sb[:, n, :, :]).then_inc(rows_out, 16)
                    sp.wait_ge(zeros_out, 32)
                    sp.wait_ge(rows_out, 32)

                @block.gpsimd
                def _(pool):
                    pool.memset(ends[0][:], N).then_inc(e_clear, 1)
                    pool.memset(ends[1][:], N).then_inc(e_clear, 1)
                    pool.memset(attr[:], 0.0).then_inc(e_clear, 1)
                    pool.memset(zeros[:], 0.0).then_inc(e_clear, 1)

                @block.vector
                def _(dve):
                    link = Chain(dve, e_chain)
                    link(dve.memset(zeros_b[:], 0.0))
                    link(dve.tensor_copy(lane_b[:], lane[:, 0:P]))
                    dve.wait_ge(e_in, 96)
                    for way in range(2):
                        cols = slice(way * EC, (way + 1) * EC)
                        link(dve.tensor_scalar(rec[:, cols, 0], ends[way][:], 1.0, None, ALU.add))
                        link(dve.tensor_scalar(key_i[:, cols], ends[1 - way][:], float(way * NPAD), None, ALU.add))
                    dve.tensor_copy(key_f[:], key_i[:]).then_inc(keys_ready, 1)
                    link(dve.tensor_scalar(lo_i[:], key_i[:], P - 1, None, ALU.bitwise_and))
                    link(dve.tensor_scalar(hi_i[:], key_i[:], 7, None, ALU.arith_shift_right))
                    dve.tensor_copy(lo_f[:], lo_i[:]).then_inc(lanes_ready, 1)
                    link(dve.tensor_copy(hi_f[:], hi_i[:]))
                    dve.wait_ge(lanes_ready, 1)
                    with dve.Fori(0, NC // 2) as i:
                        for s in range(2):
                            c = i * 2 + s
                            dve.wait_ge(hot_used[s], i)
                            dve.tensor_tensor(lo_hot[:, s], lane_b[:].unsqueeze(1).broadcast_to([P, C, P]),
                                              lo_f[:, ds(c * C, C)].unsqueeze(2).broadcast_to([P, C, P]),
                                              ALU.is_equal).then_inc(hot_ready, 1)
                            dve.tensor_tensor(hi_hot[:, s], lane_b[:, 0:KB].unsqueeze(1).broadcast_to([P, C, KB]),
                                              hi_f[:, ds(c * C, C)].unsqueeze(2).broadcast_to([P, C, KB]),
                                              ALU.is_equal).then_inc(hot_ready, 1)
                    dve.wait_ge(cnt_ready, 1)
                    link(dve.tensor_copy(cnt_i[:], ps_cnt[:, 0:KB]))
                    link(dve.tensor_scalar(cnt_i[:], cnt_i[:], float(G - 1), None, ALU.add))
                    link(dve.tensor_scalar(cnt_i[:], cnt_i[:], G.bit_length() - 1, None, ALU.arith_shift_right))
                    dve.tensor_scalar(rows_f[:], cnt_i[:], 1.0, None, ALU.max).then_inc(rows_ready, 1)
                    dve.wait_ge(pre_ready, 1)
                    link(dve.tensor_copy(totals[:], ps_pre[:, 1, 0:KB]))
                    link(dve.tensor_copy(within[:], ps_pre[:, 0, 0:KB]))
                    link(dve.tensor_tensor_scan(upto[:], ones[:, 0:KB], totals[:], 0.0, ALU.mult, ALU.add))
                    link(dve.tensor_tensor(upto[:], upto[:], totals[:], ALU.subtract))
                    link(dve.tensor_tensor(row_base[:], upto[:], within[:], ALU.add))

                @block.scalar
                def _(act):
                    act.wait_ge(e_in, 96)
                    for way, words in enumerate(((0, 1, 2), (0, 2, 1))):
                        for w, a in enumerate(words):
                            act.activation(rec[:, way * EC:(way + 1) * EC, 1 + w], attr[:, :, a], ACT.Ln, bias=1.0)
                    for n in range(2 * NTC):
                        act.wait_ge(row_tp, n + 1)
                        act.copy(rows_sb[:, n // NTC, n % NTC, :], ps_row[0:TC, n % 2, 0:P]).then_inc(row_copied, 1)

                @block.tensor
                def _(pe):
                    pe.wait_ge(keys_ready, 1)
                    pe.wait_ge(lanes_ready, 1)
                    for n in range(2 * NTC):
                        if n >= 2:
                            pe.wait_ge(row_copied, n - 1)
                        t = (key_f, lo_f)[n // NTC]
                        pe.transpose(ps_row[0:TC, n % 2, 0:P], t[:, n % NTC * TC:(n % NTC + 1) * TC], ident[:]).then_inc(row_tp, 1)
                    pe.wait_ge(hot_ready, 1)
                    pe.matmul(ps_cnt[:, 0:KB], zeros_b[:], lane_b[:, 0:KB], start=True, stop=False, skip_group_check=True)
                    with pe.Fori(0, NC // 2) as i:
                        for s in range(2):
                            pe.wait_ge(hot_ready, i * 4 + s * 2 + 2)
                            for j in range(C):
                                last = pe.matmul(ps_cnt[:, 0:KB], lo_hot[:, s, j, :], hi_hot[:, s, j, :], start=False,
                                                 stop=False, skip_group_check=True)
                            last.then_inc(hot_used[s], 1)
                    pe.matmul(ps_cnt[:, 0:KB], zeros_b[:], lane_b[:, 0:KB], start=False, stop=True,
                              skip_group_check=True).then_inc(cnt_ready, 1)
                    pe.wait_ge(rows_ready, 1)
                    pe.matmul(ps_pre[:, 0, 0:KB], before[:], rows_f[:], start=True, stop=True)
                    pe.matmul(ps_pre[:, 1, 0:KB], ones[:], rows_f[:], start=True, stop=True).then_inc(pre_ready, 1)

            with ExitStack() as ctx:
                key_row = sbuf(ctx, "key_row", [P, 2, C, P])
                lo_row = sbuf(ctx, "lo_row", [P, 2, C, P])
                lo_hot_t = sbuf(ctx, "lo_hot_t", [P, 2, C, P])
                lo_hot = sbuf(ctx, "lo_hot2", [P, 2, C, P])
                hi_hot = sbuf(ctx, "hi_hot2", [P, 2, C, KB])
                same = sbuf(ctx, "same", [P, C, P])
                picked = sbuf(ctx, "picked", [P, C, KB])
                rank = sbuf(ctx, "rank", [P, 2, C])
                seen = sbuf(ctx, "seen", [P, C])
                place = sbuf(ctx, "place", [P, 2, C], I32)
                rec_st = sbuf(ctx, "rec_st", [P, 2, C, 4])
                base_g = sbuf(ctx, "base_g", [P, KB])
                so_far = sbuf(ctx, "so_far", [P, 2, KB])
                base_i = sbuf(ctx, "base_i", [P, KB], I32)
                MK = 10
                mark_st = sbuf(ctx, "mark_st", [P, MK], I32)
                ps_sofar = psum(ctx, "ps_sofar", [P, 512])
                ps_pick = psum(ctx, "ps_pick", [P, 2, 512])
                row_in = sems("row_in0", "row_in1")
                rows_used = sems("rows_used0", "rows_used1")
                pick_ready = sems("pick_ready0", "pick_ready1")
                place_ready = sems("place_ready0", "place_ready1")
                sent = sems("sent0", "sent1")
                hots_ready, base_ready, added, sofar_ready, p_chain, rec_staged = sems(
                    "hots_ready", "base_ready", "added", "sofar_ready", "p_chain", "rec_staged")
                mark_staged, marks_out, base_i_ready = sems("mark_staged", "marks_out", "base_i_ready")
                block = ctx.enter_context(nc.Block())

                @block.sync
                def _(sp):
                    with sp.Fori(0, NC // 2) as i:
                        for s in range(2):
                            sp.wait_ge(rows_used[s], i * C)
                            for t, a in ((key_row, keyrow_dram), (lo_row, lorow_dram)):
                                sp.dma_start(t[:, s].rearrange("p j e -> p (j e)"),
                                             a[ds((i * 2 + s) * C, C), :].rearrange("(o j) e -> o (j e)", o=1)
                                             .broadcast_to([P, C * P])).then_inc(row_in[s], 16)

                @block.gpsimd
                def _(pool):
                    with pool.Fori(0, KB // MK) as i:
                        pool.wait_ge(mark_staged, i + 1)
                        pool.sem_inc(pool_turn, 1)
                        for n in range(MK):
                            pool.indirect_dma_start(marks_dram[:, :], bass.IndirectOffsetOnAxis(ap=mark_st[:, n:n + 1], axis=0),
                                                    ones[:, 0:1], None).then_inc(marks_out, 16)
                    with pool.Fori(0, NC // 2) as i:
                        for s in range(2):
                            pool.wait_ge(place_ready[s], i + 1)
                            pool.wait_ge(rec_staged, i * 2 + s + 1)
                            pool.sem_inc(pool_turn, 1)
                            for j in range(C):
                                pool.indirect_dma_start(rec_dram[:, :], bass.IndirectOffsetOnAxis(ap=place[:, s, j:j + 1], axis=0),
                                                        rec_st[:, s, j, :], None).then_inc(sent[s], 16)
                    for s in range(2):
                        pool.wait_ge(sent[s], 16 * C * (NC // 2))
                    pool.wait_ge(marks_out, 16 * KB)

                @block.vector
                def _(dve):
                    dve.tensor_scalar(base_g[:], row_base[:], float(G), None, ALU.mult).then_inc(base_ready, 1)
                    dve.tensor_copy(base_i[:], row_base[:]).then_inc(base_i_ready, 1)
                    dve.wait_ge(base_i_ready, 1)
                    with dve.Fori(0, KB // MK) as i:
                        dve.wait_ge(marks_out, i * MK * 16)
                        dve.tensor_copy(mark_st[:], base_i[:, ds(i * MK, MK)]).then_inc(mark_staged, 1)

                    def compare(c, s, turn):
                        dve.wait_ge(row_in[s], turn * 32 + 32)
                        dve.wait_ge(pick_ready[s], turn)
                        dve.tensor_scalar(lo_hot_t[:, s], lo_row[:, s], lane_col[:, 0:1], None, ALU.is_equal).then_inc(hots_ready, 1)
                        dve.tensor_tensor(lo_hot[:, s], lane[:, 0:P].unsqueeze(1).broadcast_to([P, C, P]),
                                          lo_f[:, ds(c * C, C)].unsqueeze(2).broadcast_to([P, C, P]),
                                          ALU.is_equal).then_inc(hots_ready, 1)
                        dve.tensor_tensor(hi_hot[:, s], lane[:, 0:KB].unsqueeze(1).broadcast_to([P, C, KB]),
                                          hi_f[:, ds(c * C, C)].unsqueeze(2).broadcast_to([P, C, KB]),
                                          ALU.is_equal).then_inc(hots_ready, 1)
                        dve.wait_ge(rows_used[1 - s], (turn + s) * C)
                        dve.wait_ge(place_ready[s], turn)
                        for j in range(C):
                            dve.scalar_tensor_tensor(same[:, j], key_row[:, s, j, :], key_f[:, ds(c * C + j, 1)], after[:],
                                                     ALU.is_equal, ALU.mult, accum_out=rank[:, s, j:j + 1]).then_inc(rows_used[s], 1)

                    def settle(c, s, turn, start):
                        link = Chain(dve, p_chain, start)
                        dve.wait_ge(pick_ready[s], turn + 1)
                        link(dve.tensor_tensor(picked[:], ps_pick[:, s, 0:C * KB].rearrange("p (j b) -> p j b", j=C), hi_hot[:, s], ALU.mult))
                        dve.wait_ge(place_ready[1 - s], turn + s)
                        link(dve.tensor_reduce(seen[:], picked[:], AX, ALU.add))
                        dve.wait_ge(rows_used[s], (turn + 1) * C)
                        dve.wait_ge(sent[s], turn * 16 * C)
                        dve.tensor_tensor(place[:, s], seen[:], rank[:, s], ALU.add).then_inc(place_ready[s], 1)

                    compare(0, 0, 0)
                    with dve.Fori(0, NC // 2 - 1) as i:
                        compare(i * 2 + 1, 1, i)
                        settle(i * 2, 0, i, i * 4)
                        compare(i * 2 + 2, 0, i + 1)
                        settle(i * 2 + 1, 1, i, i * 4 + 2)
                    compare(NC - 1, 1, NC // 2 - 1)
                    settle(NC - 2, 0, NC // 2 - 1, 2 * NC - 4)
                    settle(NC - 1, 1, NC // 2 - 1, 2 * NC - 2)

                @block.scalar
                def _(act):
                    act.wait_ge(added, 1)
                    act.copy(so_far[:, 0, :], ps_sofar[:, 0:KB]).then_inc(sofar_ready, 1)
                    with act.Fori(0, NC // 2) as i:
                        for s in range(2):
                            c = i * 2 + s
                            act.wait_ge(sent[s], i * 16 * C)
                            act.copy(rec_st[:, s], rec[:, ds(c * C, C), :]).then_inc(rec_staged, 1)
                            for j in range(C):
                                act.wait_ge(added, c * C + j + 2)
                                act.copy(so_far[:, (j + 1) % 2, :], ps_sofar[:, 0:KB]).then_inc(sofar_ready, 1)

                @block.tensor
                def _(pe):
                    pe.wait_ge(base_ready, 1)
                    pe.matmul(ps_sofar[:, 0:KB], ident[:], base_g[:], start=True, stop=False, skip_group_check=True).then_inc(added, 1)
                    with pe.Fori(0, NC // 2) as i:
                        for s in range(2):
                            c = i * 2 + s
                            pe.wait_ge(hots_ready, c * 3 + 3)
                            pe.wait_ge(place_ready[s], i)
                            for j in range(C):
                                pe.wait_ge(sofar_ready, c * C + j + 1)
                                pe.matmul(ps_sofar[:, 0:KB], lo_hot[:, s, j, :], hi_hot[:, s, j, :], start=False, stop=False,
                                          skip_group_check=True).then_inc(added, 1)
                                last = pe.matmul(ps_pick[:, s, j * KB:(j + 1) * KB], lo_hot_t[:, s, j, :], so_far[:, j % 2, :],
                                                 start=True, stop=True)
                            last.then_inc(pick_ready[s], 1)

        rows = ExitStack()
        with rows:
            marks = sbuf(rows, "marks", [P, RT])
            marks_next = sbuf(rows, "marks_next", [P, RT])
            key_of = sbuf(rows, "key_of", [P, RT])
            row_max = sbuf(rows, "row_max", [P, RT, H])
            with ExitStack() as ctx:
                AHEAD = 4
                rec = sbuf(ctx, "rec_rows", [P, RT + AHEAD, G * 4])
                gidx = sbuf(ctx, "gidx", [P, RT + AHEAD, G + 1], I32)
                valid = sbuf(ctx, "valid", [P, RT, G])
                mask = sbuf(ctx, "mask", [P, RT, G])
                target_f = sbuf(ctx, "target_f", [P, RT])
                low_rows = sbuf(ctx, "low_rows", [P, 1])
                w_row = sbuf(ctx, "w_row", [1, TD])
                b_row = sbuf(ctx, "b_row", [1, 3, TD])
                time_w = sbuf(ctx, "time_w", [G * 4, G * 3 * TD])
                idx_st = sbuf(ctx, "idx_st", [P, R, G + 1], I32)
                rec_st = sbuf(ctx, "rec_row_st", [P, R, G * 4])
                rec_t = sbuf(ctx, "rec_t", [G * 4, 2, P])
                turns = sbuf(ctx, "turns", [P, 2, G * 3 * TD])
                phase = sbuf(ctx, "phase", [P, 2, G * 3 * TD])
                emb = sbuf(ctx, "emb", [P, R, G, 3, TD])
                kv = sbuf(ctx, "kv", [P, R, G, 2 * PROJ])
                q = sbuf(ctx, "q", [P, R, DK])
                prod = sbuf(ctx, "prod", [P, G, H * DK])
                q_sum = sbuf(ctx, "q_sum", [P, G, DK])
                att = sbuf(ctx, "att", [P, G, H])
                att_m = sbuf(ctx, "att_m", [P, G, H])
                drop = sbuf(ctx, "drop", [P, 2, G, H])
                weight = sbuf(ctx, "weight", [P, 2, G, H])
                msg = sbuf(ctx, "msg", [P, 2, G, d.MSG])
                msg_out = sbuf(ctx, "msg_out", [P, 2, d.MSG])
                ps_rt = psum(ctx, "ps_rt", [P, 2, 512])
                ps_low = psum(ctx, "ps_low", [P, 512])
                ps_turns = psum(ctx, "ps_turns", [P, 2, 512])
                ps_sum = psum(ctx, "ps_sum", [P, 2, 512])
                r_clear, r_in, r_chain, w_in2, w_scaled, w_clear, w_placed = sems(
                    "r_clear", "r_in", "r_chain", "w_in2", "w_scaled", "w_clear", "w_placed")
                counted, low_ready, rows_set = sems("counted", "low_ready", "rows_set")
                staged, rt_turned, rt_copied, turns_ready, rounded, phase_ready = sems(
                    "staged", "rt_turned", "rt_copied", "turns_ready", "rounded", "phase_ready")
                emb_ready, drop_ready, weight_ready, sum_ready, sum_copied, att_chain, msg_chain = sems(
                    "emb_ready", "drop_ready", "weight_ready", "sum_ready", "sum_copied", "att_chain", "msg_chain")
                msg_ready = sems(*[f"msg_ready{n}" for n in range(R)])
                kv_in = sems(*[f"kv_in{n}" for n in range(R)])
                msg_stored = sems("msg_stored0", "msg_stored1")
                block = ctx.enter_context(nc.Block())

                @block.sync
                def _(sp):
                    sp.dma_start(rec[:, 0:RT, :].rearrange("p i w -> p (i w)"),
                                 rec_dram.rearrange("(p i) w -> p (i w)", p=P)).then_inc(r_in, 16)
                    sp.dma_start(marks[:], marks_dram[0:NR, :].rearrange("(p i) o -> p (i o)", p=P)).then_inc(r_in, 16)
                    sp.dma_start(marks_next[:], marks_dram[1:NR + 1, :].rearrange("(p i) o -> p (i o)", p=P)).then_inc(r_in, 16)
                    sp.dma_start(w_row[:], w_time.rearrange("(o n) -> o n", o=1)).then_inc(w_in2, 16)
                    for n in range(3):
                        sp.dma_start(b_row[:, n, :], b_time.rearrange("(o n) -> o n", o=1)).then_inc(w_in2, 16)
                    sp.wait_ge(w_scaled, 2)
                    sp.wait_ge(w_clear, 1)
                    for g in range(G):
                        at = g * 3 * TD
                        sp.dma_start(time_w[g * 4:g * 4 + 1, at:at + 3 * TD], b_row[:].rearrange("p n t -> p (n t)")).then_inc(w_placed, 16)
                        for n in range(3):
                            sp.dma_start(time_w[g * 4 + 1 + n:g * 4 + 2 + n, at + n * TD:at + (n + 1) * TD], w_row[:]).then_inc(w_placed, 16)

                    def store(a):
                        sp.wait_ge(sum_copied, a.t + 1)
                        sp.dma_start(part_dram.rearrange("(p i) c -> p i c", p=P)[:, ds(a.t, 1), :].rearrange("p i c -> p (i c)"),
                                     msg_out[:, a.slot(2), :]).then_inc(msg_stored[a.slot(2)], 16)

                    walk(sp, RT, store)
                    for n in range(2):
                        sp.wait_ge(msg_stored[n], 16 * (RT // 2))

                @block.gpsimd
                def _(pool):
                    pool.memset(rec[:, RT:, :], 0.0).then_inc(r_clear, 1)
                    pool.memset(gidx[:, RT:, :], 0).then_inc(r_clear, 1)
                    pool.memset(time_w[:], 0.0).then_inc(w_clear, 1)

                    def gather(a):
                        s = a.slot(R)
                        pool.wait_ge(staged, a.t + 1)
                        pool.wait_ge(msg_ready[s], a.turn(R))
                        pool.sem_inc(pool_turn, 1)
                        for g in range(G):
                            pool.indirect_dma_start(kv[:, s, g, :], None, kv_dram[:, :],
                                                    bass.IndirectOffsetOnAxis(ap=idx_st[:, s, g:g + 1], axis=0)).then_inc(kv_in[s], 16)
                        pool.indirect_dma_start(q[:, s, :], None, q_dram[:, :],
                                                bass.IndirectOffsetOnAxis(ap=idx_st[:, s, G:G + 1], axis=0)).then_inc(kv_in[s], 16)

                    walk(pool, RT, gather)

                @block.vector
                def _(dve):
                    link = Chain(dve, r_chain)
                    dve.wait_ge(w_in2, 64)
                    dve.tensor_scalar(w_row[:], w_row[:], 1.0 / TWO_PI, None, ALU.mult).then_inc(w_scaled, 1)
                    dve.tensor_scalar(b_row[:], b_row[:], 1.0 / TWO_PI, 0.25, ALU.mult, ALU.add).then_inc(w_scaled, 1)
                    dve.wait_ge(r_in, 48)
                    dve.wait_ge(r_clear, 2)
                    link(dve.tensor_tensor_scan(key_of[:], ones[:, 0:1].broadcast_to([P, RT]), marks[:], 0.0, ALU.mult, ALU.add))
                    dve.tensor_copy(low_rows[:], key_of[:, RT - 1:RT]).then_inc(counted, 1)
                    dve.wait_ge(low_ready, 1)
                    dve.wait_ge(counted, 1)
                    link(dve.tensor_scalar(low_rows[:], ps_low[:, 0:1], -1.0, None, ALU.add))
                    link(dve.tensor_scalar(key_of[:], key_of[:], low_rows[:, 0:1], None, ALU.add))
                    link(dve.tensor_scalar(target_f[:], key_of[:], float(NPAD), float(-NPAD), ALU.is_ge, ALU.mult))
                    link(dve.tensor_tensor(gidx[:, 0:RT, G], target_f[:], key_of[:], ALU.add))
                    words = rec[:, 0:RT, :].rearrange("p i (g w) -> p i g w", w=4)[:, :, :, 0]
                    link(dve.tensor_copy(gidx[:, 0:RT, 0:G], words))
                    link(dve.tensor_scalar(valid[:], words, 1.0, None, ALU.min))
                    link(dve.tensor_scalar(mask[:], valid[:], -1.0, BIG, ALU.add, ALU.mult))
                    dve.memset(words, 1.0).then_inc(rows_set, 1)

                    def find_phase(a):
                        wait_done(dve, rounded, a)
                        wait_done(dve, emb_ready, a, 2)
                        h = a.slot(2)
                        dve.scalar_tensor_tensor(phase[:, h], turns[:, h], MAGIC, ps_turns[:, h, 0:G * 3 * TD],
                                                 ALU.subtract, ALU.subtract).then_inc(phase_ready, 1)

                    def attend(a):
                        s, h = a.slot(R), a.slot(2)
                        link = Chain(dve, att_chain, a.t * 5)
                        dve.wait_ge(kv_in[s], (a.turn(R) + 1) * 16 * (G + 1))
                        dve.wait_ge(emb_ready, a.t + 1)
                        dve.tensor_copy(q_sum[:, :, 0:LAST], q[:, s, 0:LAST].unsqueeze(1).broadcast_to([P, G, LAST]))
                        link(dve.tensor_tensor(q_sum[:, :, LAST:], emb[:, s, :, 2, :], q[:, s, LAST:DK].unsqueeze(1).broadcast_to([P, G, TD]), ALU.add))
                        dve.tensor_tensor(prod[:, :, 0:3 * DK].rearrange("p g (h c) -> p g h c", h=3),
                                          kv[:, s, :, 0:3 * DK].rearrange("p g (h c) -> p g h c", h=3),
                                          q_sum[:].unsqueeze(2).broadcast_to([P, G, 3, DK]), ALU.mult)
                        dve.tensor_tensor(prod[:, :, 3 * DK:PROJ], kv[:, s, :, 3 * DK:PROJ], q_sum[:, :, 0:LAST], ALU.mult)
                        link(dve.tensor_tensor(prod[:, :, PROJ:], emb[:, s, :, 1, :], q_sum[:, :, LAST:], ALU.mult))
                        link(dve.tensor_reduce(att[:], prod[:].rearrange("p g (h c) -> p g h c", h=H), AX, ALU.add))
                        link(dve.tensor_tensor(att_m[:], att[:], mask[:, ds(a.t, 1), :].rearrange("p i g -> p (i g)").unsqueeze(2).broadcast_to([P, G, H]), ALU.add))
                        top_of = row_max[:, ds(a.t, 1), :].rearrange("p i h -> p (i h)")
                        link(dve.tensor_reduce(top_of, att_m[:].rearrange("p g h -> p h g"), AX, ALU.max))
                        wait_done(dve, weight_ready, a, 2)
                        dve.tensor_tensor(drop[:, h], att_m[:], top_of.unsqueeze(1).broadcast_to([P, G, H]), ALU.subtract).then_inc(drop_ready, 1)

                    def weigh(a):
                        s, h = a.slot(R), a.slot(2)
                        link = Chain(dve, msg_chain, a.t * 4)
                        dve.wait_ge(weight_ready, a.t + 1)
                        wait_done(dve, sum_ready, a, 2)
                        real = valid[:, ds(a.t, 1), :].rearrange("p i g -> p (i g)").unsqueeze(2)
                        link(dve.tensor_tensor(msg[:, h, :, D:], weight[:, h], real.broadcast_to([P, G, H]), ALU.mult))
                        link(dve.tensor_tensor(msg[:, h, :, 0:3 * DK].rearrange("p g (h c) -> p g h c", h=3),
                                          kv[:, s, :, PROJ:PROJ + 3 * DK].rearrange("p g (h c) -> p g h c", h=3),
                                          msg[:, h, :, D:D + 3].unsqueeze(3).broadcast_to([P, G, 3, DK]), ALU.mult))
                        last_w = msg[:, h, :, D + 3:D + 4]
                        link(dve.tensor_tensor(msg[:, h, :, PROJ:PROJ + TD], emb[:, s, :, 1, :], last_w.broadcast_to([P, G, TD]), ALU.mult))
                        link(dve.tensor_tensor(msg[:, h, :, PROJ + TD:D], emb[:, s, :, 0, :], real.broadcast_to([P, G, TD]), ALU.mult))
                        dve.tensor_tensor(msg[:, h, :, 3 * DK:PROJ], kv[:, s, :, PROJ + 3 * DK:], last_w.broadcast_to([P, G, LAST]),
                                          ALU.mult).then_inc(msg_ready[s], 1)

                    def step(a):
                        find_phase(a + 1)
                        attend(a)
                        if a.c:
                            weigh(a + -1)

                    find_phase(At(0, 0))
                    walk(dve, RT, step)
                    weigh(At(0, RT - 1))

                @block.scalar
                def _(act):
                    def stage(a):
                        act.wait_ge(kv_in[a.slot(R)], a.turn(R) * 16 * (G + 1))
                        wait_done(act, rt_turned, a, R)
                        act.copy(idx_st[:, a.slot(R), :], gidx[:, ds(a.t, 1), :].rearrange("p i g -> p (i g)"))
                        act.copy(rec_st[:, a.slot(R), :], rec[:, ds(a.t, 1), :].rearrange("p i g -> p (i g)")).then_inc(staged, 1)

                    def copy_rt(a):
                        wait_done(act, rt_turned, a)
                        wait_done(act, turns_ready, a, 2)
                        act.copy(rec_t[:, a.slot(2), :], ps_rt[0:G * 4, a.slot(2), 0:P]).then_inc(rt_copied, 1)

                    def round_turns(a):
                        wait_done(act, turns_ready, a)
                        wait_done(act, phase_ready, a, 2)
                        act.activation(turns[:, a.slot(2)], ps_turns[:, a.slot(2), 0:G * 3 * TD], ACT.Identity,
                                       bias=magic[:, 0:1]).then_inc(rounded, 1)

                    def sines(a):
                        wait_done(act, phase_ready, a)
                        act.wait_ge(msg_ready[a.slot(R)], a.turn(R))
                        act.activation(emb[:, a.slot(R)].rearrange("p g n t -> p (g n t)"), phase[:, a.slot(2)], ACT.Sin,
                                       scale=-SIN_SCALE).then_inc(emb_ready, 1)

                    def exps(a):
                        wait_done(act, drop_ready, a)
                        if a.c >= 2:
                            act.wait_ge(msg_ready[(a + -2).slot(R)], (a + -2).turn(R) + 1)
                        act.activation(weight[:, a.slot(2)], drop[:, a.slot(2)], ACT.Exp, scale=float(DK) ** -0.5).then_inc(weight_ready, 1)

                    def copy_sum(a):
                        wait_done(act, sum_ready, a)
                        act.wait_ge(msg_stored[a.slot(2)], a.turn(2) * 16)
                        act.copy(msg_out[:, a.slot(2), :], ps_sum[:, a.slot(2), 0:d.MSG]).then_inc(sum_copied, 1)

                    def step(a):
                        copy_rt(a + 3)
                        round_turns(a + 2)
                        sines(a + 1)
                        exps(a)
                        stage(a + 4)
                        if a.c:
                            copy_sum(a + -1)

                    act.wait_ge(rows_set, 1)
                    for t in range(4):
                        stage(At(0, t))
                    for t in range(3):
                        copy_rt(At(0, t))
                    for t in range(2):
                        round_turns(At(0, t))
                    sines(At(0, 0))
                    walk(act, RT, step)
                    copy_sum(At(0, RT - 1))

                @block.tensor
                def _(pe):
                    pe.wait_ge(counted, 1)
                    pe.matmul(ps_low[:, 0:1], before[:], low_rows[:], start=True, stop=True).then_inc(low_ready, 1)
                    pe.wait_ge(w_placed, 16 * G * 4)

                    def turn_rec(a):
                        wait_done(pe, staged, a)
                        wait_done(pe, rt_copied, a, 2)
                        pe.transpose(ps_rt[0:G * 4, a.slot(2), 0:P], rec_st[:, a.slot(R), :], ident[:]).then_inc(rt_turned, 1)

                    def multiply(a):
                        wait_done(pe, rt_copied, a)
                        wait_done(pe, phase_ready, a, 2)
                        pe.matmul(ps_turns[:, a.slot(2), 0:G * 3 * TD], rec_t[:, a.slot(2), :], time_w[:], start=True,
                                  stop=True).then_inc(turns_ready, 1)

                    def add_up(a):
                        pe.wait_ge(msg_ready[a.slot(R)], a.turn(R) + 1)
                        wait_done(pe, sum_copied, a, 2)
                        for g in range(G):
                            last = pe.matmul(ps_sum[:, a.slot(2), 0:d.MSG], ident[:], msg[:, a.slot(2), g, :], start=(g == 0), stop=(g == G - 1))
                        last.then_inc(sum_ready, 1)

                    def step(a):
                        turn_rec(a + 3)
                        multiply(a + 2)
                        if a.c:
                            add_up(a + -1)

                    for t in range(3):
                        turn_rec(At(0, t))
                    for t in range(2):
                        multiply(At(0, t))
                    walk(pe, RT, step)
                    add_up(At(0, RT - 1))

            with ExitStack() as ctx:
                fall = sbuf(ctx, "fall", [P, 2, RT])
                lane_fall = sbuf(ctx, "lane_fall", [P, 2])
                flow = sbuf(ctx, "flow", [P, 2, H, RT])
                ends_of = sbuf(ctx, "ends_of", [P, 2, 2, H])
                across = sbuf(ctx, "across", [H, 2, P + 1])
                across_in = sbuf(ctx, "across_in", [H, 2, 2, P])
                carry = sbuf(ctx, "carry", [P, 2, H])
                below = sbuf(ctx, "below", [P, RT, H])
                share = sbuf(ctx, "share", [P, RT, H + 1])
                ps_lane = psum(ctx, "ps_lane", [P, 4, 512])
                s_chain, lanes_set, lanes_turned, carry_set, carry_turned, below_ready, share_ready, share_out = sems(
                    "s_chain", "lanes_set", "lanes_turned", "carry_set", "carry_turned", "below_ready", "share_ready", "share_out")
                block = ctx.enter_context(nc.Block())

                @block.vector
                def _(dve):
                    link = Chain(dve, s_chain)
                    link(dve.tensor_scalar(fall[:, 0], marks[:], RESET, None, ALU.mult))
                    link(dve.tensor_scalar(fall[:, 1], marks_next[:], RESET, None, ALU.mult))
                    link(dve.tensor_reduce(lane_fall[:], fall[:], AX, ALU.min))
                    link(dve.memset(across[:], RESET / 2))
                    for n in range(2):
                        order = slice(None, None, -1) if n else slice(None)
                        edge = 0 if n else RT - 1

                        def scan(start):
                            for h in range(H):
                                src_t = flow[:, 0, h, order] if n else row_max[:, :, h]
                                last = dve.tensor_tensor_scan(flow[:, n, h, order], fall[:, n, order], src_t, start(h), ALU.add, ALU.max)
                            link(last)

                        scan(lambda h: RESET / 2)
                        link(dve.tensor_copy(ends_of[:, n, 0, :], flow[:, n, :, edge]))
                        dve.tensor_copy(ends_of[:, n, 1, :], lane_fall[:, n:n + 1].broadcast_to([P, H])).then_inc(lanes_set, 1)
                        dve.wait_ge(lanes_turned, n + 1)
                        for w in range(2):
                            link(dve.tensor_copy(across_in[:, n, w, :], ps_lane[0:H, w, 0:P]))
                        kept = across[:, n, 0:P][:, order] if n else across[:, n, 1:P + 1]
                        dve.tensor_tensor_scan(kept, across_in[:, n, 1, order], across_in[:, n, 0, order], RESET / 2,
                                               ALU.add, ALU.max).then_inc(carry_set, 1)
                        dve.wait_ge(carry_turned, n + 1)
                        link(dve.tensor_copy(carry[:, n, :], ps_lane[:, 2, 0:H]))
                        scan(lambda h: carry[:, n, h:h + 1])
                    dve.tensor_tensor(below[:], row_max[:], flow[:, 1].rearrange("p h i -> p i h"), ALU.subtract).then_inc(below_ready, 1)
                    dve.tensor_copy(share[:, :, H], key_of[:]).then_inc(share_ready, 1)

                @block.tensor
                def _(pe):
                    for n in range(2):
                        pe.wait_ge(lanes_set, n + 1)
                        for w in range(2):
                            last = pe.transpose(ps_lane[0:H, w, 0:P], ends_of[:, n, w, :], ident[:])
                        last.then_inc(lanes_turned, 1)
                        pe.wait_ge(carry_set, n + 1)
                        pe.transpose(ps_lane[:, 2, 0:H], across[:, n, 1:P + 1] if n else across[:, n, 0:P], ident[0:H, 0:H]).then_inc(carry_turned, 1)

                @block.scalar
                def _(act):
                    act.wait_ge(below_ready, 1)
                    act.activation(share[:, :, 0:H], below[:], ACT.Exp, scale=float(DK) ** -0.5).then_inc(share_ready, 1)

                @block.sync
                def _(sp):
                    sp.wait_ge(share_ready, 2)
                    sp.dma_start(wk_dram.rearrange("(p i) c -> p (i c)", p=P), share[:].rearrange("p i c -> p (i c)")).then_inc(share_out, 16)
                    sp.wait_ge(share_out, 16)

        nodes = ExitStack()
        with nodes:
            agg = sbuf(nodes, "agg", [P, NB, D])
            with ExitStack() as ctx:
                acc = sbuf(ctx, "acc", [P, KB + 1, d.MSG])
                first_key = sbuf(ctx, "first_key", [1, RT])
                first_i = sbuf(ctx, "first_i", [1, RT], I32)
                block_i = sbuf(ctx, "block_i", [1, RT], I32)
                block_key = sbuf(ctx, "block_key", [1, RT])
                block_key_bc = sbuf(ctx, "block_key_bc", [P, RT])
                part = sbuf(ctx, "part", [P, 4, d.MSG])
                wk = sbuf(ctx, "wk", [P, 4, H + 1])
                key_hot = sbuf(ctx, "key_hot", [P, 4, 2 * P])
                total = sbuf(ctx, "total", [P, KB, H])
                ps_bc = psum(ctx, "ps_bc", [P, 512])
                ps_key = psum(ctx, "ps_key", [P, 2, 2, 512])
                k_in, k_chain, first_ready, bc_ready, acc_clear = sems("k_in", "k_chain", "first_ready", "bc_ready", "acc_clear")
                part_in = sems(*[f"part_in{n}" for n in range(4)])
                part_ready, key_summed, key_added, tile_chain = sems("part_ready", "key_summed", "key_added", "tile_chain")
                block = ctx.enter_context(nc.Block())

                @block.sync
                def _(sp):
                    sp.dma_start(first_key[:], wk_dram.rearrange("(i p) c -> c p i", p=P)[H:H + 1, 0, :],
                                 allow_slow_non_contiguous=True).then_inc(k_in, 16)

                    def load(a):
                        s = a.slot(4)
                        if a.c >= 4:
                            sp.wait_ge(key_summed, a.t - 3)
                        sp.dma_start(part[:, s, :], part_dram[ds(a.t * P, P), :]).then_inc(part_in[s], 16)
                        sp.dma_start(wk[:, s, :], wk_dram[ds(a.t * P, P), :]).then_inc(part_in[s], 16)

                    for t in range(4):
                        load(At(0, t))
                    with sp.Fori(0, RT // 4 - 1) as i:
                        for u in range(4):
                            load(At(i, 4 + u))

                @block.gpsimd
                def _(pool):
                    pool.memset(acc[:], 0.0).then_inc(acc_clear, 1)

                @block.vector
                def _(dve):
                    link = Chain(dve, k_chain)
                    dve.wait_ge(k_in, 16)
                    link(dve.tensor_copy(first_i[:], first_key[:]))
                    link(dve.tensor_scalar(block_i[:], first_i[:], 7, None, ALU.arith_shift_right))
                    dve.tensor_scalar(block_key[:], block_i[:], float(P), None, ALU.mult).then_inc(first_ready, 1)
                    dve.wait_ge(bc_ready, 1)
                    link(dve.tensor_copy(block_key_bc[:], ps_bc[:, 0:RT]))
                    dve.wait_ge(acc_clear, 1)

                    def prepare(a):
                        s = a.slot(4)
                        dve.wait_ge(part_in[s], (a.turn(4) + 1) * 32)
                        if a.c >= 4:
                            dve.wait_ge(key_summed, a.t - 3)
                        heads = part[:, s, 0:3 * DK].rearrange("p (h c) -> p h c", h=3)
                        dve.tensor_tensor(heads, heads, wk[:, s, 0:3].unsqueeze(2).broadcast_to([P, 3, DK]), ALU.mult)
                        dve.tensor_tensor(part[:, s, 3 * DK:H * DK], part[:, s, 3 * DK:H * DK],
                                          wk[:, s, 3:4].broadcast_to([P, DK]), ALU.mult)
                        dve.tensor_tensor(part[:, s, D:], part[:, s, D:], wk[:, s, 0:H], ALU.mult)
                        dve.tensor_scalar(key_hot[:, s], lane[:], block_key_bc[:, ds(a.t, 1)], wk[:, s, H:H + 1],
                                          ALU.add, ALU.is_equal).then_inc(part_ready, 1)

                    def add(a):
                        at = dve.value_load(block_i[0:1, ds(a.t, 1)], min_val=0, max_val=KB - 1)
                        wait_done(dve, key_summed, a)
                        if a.c:
                            dve.wait_ge(key_added, a.t)
                        dve.tensor_tensor(acc[:, ds(at, 2), :], acc[:, ds(at, 2), :], ps_key[:, a.slot(2), :, 0:d.MSG],
                                          ALU.add).then_inc(key_added, 1)

                    for t in range(4):
                        prepare(At(0, t))
                    for t in range(2):
                        add(At(0, t))
                    with dve.Fori(0, RT // 4 - 1) as i:
                        for u in range(4):
                            prepare(At(i, 4 + u))
                            add(At(i, 2 + u))
                    for t in range(RT - 2, RT):
                        add(At(0, t))
                    dve.wait_ge(key_added, RT)
                    link(dve.tensor_scalar(total[:], acc[:, 0:KB, D:], 1e-16, None, ALU.add))
                    link(dve.reciprocal(total[:], total[:]))
                    heads = acc[:, 0:KB, 0:3 * DK].rearrange("p b (h c) -> p b h c", h=3)
                    link(dve.tensor_tensor(heads, heads, total[:, :, 0:3].unsqueeze(3).broadcast_to([P, KB, 3, DK]), ALU.mult))
                    link(dve.tensor_tensor(acc[:, 0:KB, 3 * DK:H * DK], acc[:, 0:KB, 3 * DK:H * DK],
                                           total[:, :, 3:4].broadcast_to([P, KB, DK]), ALU.mult))
                    link(dve.tensor_tensor(agg[:], acc[:, 0:NB, 0:D], acc[:, NB:KB, 0:D], ALU.add))

                @block.tensor
                def _(pe):
                    pe.wait_ge(first_ready, 1)
                    pe.matmul(ps_bc[:, 0:RT], ones[0:1, :], block_key[:], start=True, stop=True).then_inc(bc_ready, 1)

                    def sum_rows(a):
                        s, h = a.slot(4), a.slot(2)
                        wait_done(pe, part_ready, a)
                        wait_done(pe, key_added, a, 2)
                        for n in range(2):
                            last = pe.matmul(ps_key[:, h, n, 0:d.MSG], key_hot[:, s, n * P:(n + 1) * P], part[:, s, :], start=True, stop=True)
                        last.then_inc(key_summed, 1)

                    walk(pe, RT, sum_rows)

            with ExitStack() as ctx:
                wa = sbuf(ctx, "wa", [P, T * KD, D])
                wa2 = sbuf(ctx, "wa2", [P, T * KD, D])
                vecs = sbuf(ctx, "vecs", [T, 3, D])
                aT = res[:].rearrange("p b c -> p (b c)").rearrange("p (k n) -> p k n", k=KD)
                masked = sbuf(ctx, "masked_a", [P, 4, KD, P])
                onehot_st = sbuf(ctx, "onehot_a", [T, P])
                ps_t = psum(ctx, "ps_ta", [P, 2, 512])
                ps_o = psum(ctx, "ps_o", [P, 512])
                ps_v = psum(ctx, "ps_v", [P, 512])
                res_clear, res_in, wa_in, vecs_in, wa_ready = sems("res_clear", "res_in", "wa_in", "vecs_in", "wa_ready")
                a_turned, a_copied, a_mask_ready, a_mask_used, o_ready, o_used = sems(
                    "a_turned", "a_copied", "a_mask_ready", "a_mask_used", "o_ready", "o_used")
                a_chain, a_var, a_std, v_hot, v_ready, v_used = sems("a_chain", "a_var", "a_std", "v_hot", "v_ready", "v_used")
                block = ctx.enter_context(nc.Block())

                @block.gpsimd
                def _(pool):
                    pool.wait_ge(o_ready, NB)
                    pool.memset(res[:, d.FULL:NB, :], 0.0).then_inc(res_clear, 1)

                @block.sync
                def _(sp):
                    for half, t in enumerate((wa, wa2)):
                        for k in range(KD):
                            sp.dma_start(t[:].rearrange("p (t k) c -> p t k c", k=KD)[:, :, k, :],
                                         Wa[:, half * D + k * P:half * D + (k + 1) * P, :].rearrange("t p c -> p t c")).then_inc(wa_in, 16)
                    for n, v in enumerate((ba, gamma, beta)):
                        sp.dma_start(vecs[:, n, :], v).then_inc(vecs_in, 16)
                    sp.wait_ge(res_clear, 1)
                    sp.dma_start(res[:, 0:d.FULL, :], x[0:d.FULL * P, :].rearrange("(b p) c -> p b c", p=P)).then_inc(res_in, 16)
                    sp.dma_start(res[0:d.TAIL, d.FULL, :], x[d.FULL * P:N, :]).then_inc(res_in, 16)

                @block.scalar
                def _(act):
                    with act.Fori(0, NB) as b:
                        for k in range(KD):
                            act.wait_ge(a_turned, b * KD + k + 1)
                            act.copy(aT[:, k, ds(b * P, P)], ps_t[:, k, 0:P]).then_inc(a_copied, 1)
                    act.wait_ge(a_var, 1)
                    act.activation(rstd[:], tmp_b[:], ACT.Sqrt).then_inc(a_std, 1)

                @block.vector
                def _(dve):
                    link = Chain(dve, a_chain)
                    dve.wait_ge(wa_in, 64)
                    dve.tensor_tensor(wa[:], wa[:], wa2[:], ALU.add).then_inc(wa_ready, 1)
                    with dve.Fori(0, NB) as b:
                        dve.wait_ge(a_copied, b * KD + KD)
                        for t in range(T):
                            dve.wait_ge(a_mask_used, b * T if t < 4 else b * T + t - 3)
                            dve.scalar_tensor_tensor(masked[:, t % 4, :, :],
                                                     type_bc[:, ds(b * P, P)].unsqueeze(1).broadcast_to([P, KD, P]), float(t),
                                                     aT[:, :, ds(b * P, P)], ALU.is_equal, ALU.mult).then_inc(a_mask_ready, 1)
                        dve.wait_ge(o_used, b)
                        dve.tensor_copy(onehot_st[:], type_onehot[:, ds(b * P, P)]).then_inc(a_mask_ready, 1)
                        dve.wait_ge(o_ready, b + 1)
                        dve.tensor_tensor(agg[:, ds(b, 1), :].rearrange("p b c -> p (b c)"), ps_o[:, 0:D],
                                          xn[:, ds(b, 1), :].rearrange("p b c -> p (b c)"), ALU.add).then_inc(o_used, 1)
                    dve.wait_ge(o_used, NB)
                    layer_norm_stats(dve, a_var, a_std, link, agg, 1)
                    link(normalize(dve, agg, agg))
                    dve.wait_ge(res_in, 32)
                    with dve.Fori(0, NB) as b:
                        dve.tensor_copy(onehot_st[:], type_onehot[:, ds(b * P, P)]).then_inc(v_hot, 1)
                        dve.wait_ge(v_ready, b + 1)
                        row = agg[:, ds(b, 1), :].rearrange("p b c -> p (b c)")
                        out_row = res[:, ds(b, 1), :].rearrange("p b c -> p (b c)")
                        step = Chain(dve, v_used, b * 3)
                        step(dve.tensor_tensor(row, row, ps_v[:, 0:D], ALU.mult))
                        step(dve.tensor_tensor(row, row, ps_v[:, D:2 * D], ALU.add))
                        step(dve.tensor_tensor(out_row, out_row, row, ALU.add))

                @block.tensor
                def _(pe):
                    for b in range(NB):
                        for k in range(KD):
                            if b:
                                pe.wait_ge(a_copied, b * KD + k - KD + 1)
                            pe.transpose(ps_t[:, k, 0:P], agg[:, b, k * P:(k + 1) * P], ident[:]).then_inc(a_turned, 1)
                    pe.wait_ge(wa_ready, 1)
                    pe.wait_ge(vecs_in, 48)
                    with pe.Fori(0, NB) as b:
                        pe.wait_ge(o_used, b)
                        for t in range(T):
                            pe.wait_ge(a_mask_ready, b * (T + 1) + t + 1)
                            for k in range(KD):
                                last = pe.matmul(ps_o[:, 0:D], masked[:, t % 4, k, :], wa[:, t * KD + k, :],
                                                 start=(t == 0 and k == 0), stop=False)
                            last.then_inc(a_mask_used, 1)
                        pe.wait_ge(a_mask_ready, (b + 1) * (T + 1))
                        pe.matmul(ps_o[:, 0:D], onehot_st[:], vecs[:, 0, :], start=False, stop=True).then_inc(o_ready, 1)
                    with pe.Fori(0, NB) as b:
                        pe.wait_ge(v_hot, b + 1)
                        pe.wait_ge(v_used, b * 3)
                        pe.matmul(ps_v[:, 0:2 * D], onehot_st[:], vecs[:, 1:3, :], start=True, stop=True).then_inc(v_ready, 1)

        X, HID = d.X, d.HID
        FH = HID // P
        with ExitStack() as ctx:
            tok_t = sbuf(ctx, "tok_t", [P, KD, NPAD])
            wr = sbuf(ctx, "wr", [P, KD, X])
            br_row = sbuf(ctx, "br_row", [1, X])
            logits = sbuf(ctx, "logits", [P, NB, X])
            higher = sbuf(ctx, "higher", [P, NB, X, X])
            equal = sbuf(ctx, "equal", [P, NB, X, X])
            earlier = sbuf(ctx, "earlier", [P, X, X])
            order = sbuf(ctx, "order", [P, NB, X])
            best = sbuf(ctx, "best", [P, NB])
            gate = sbuf(ctx, "gate", [P, NB * X])
            gate3 = gate[:].rearrange("p (b e) -> p b e", e=X)
            b1_rows = sbuf(ctx, "b1_rows", [X * FH, P])
            ln_rows = sbuf(ctx, "ln_rows", [X * KD, 2, P])
            b1_t = sbuf(ctx, "b1_t", [P, X * FH])
            ln_t = sbuf(ctx, "ln_t", [P, 2, X * KD])
            b2_row = sbuf(ctx, "b2_row", [1, X, D])
            w1 = sbuf(ctx, "w1", [P, 2, KD, HID])
            w2 = sbuf(ctx, "w2", [P, 2, FH, D])
            x_e = sbuf(ctx, "x_e", [P, KD, P])
            hid = sbuf(ctx, "hid", [P, FH, P])
            ps_t = psum(ctx, "ps_tf", [P, 2, 512])
            ps_l = psum(ctx, "ps_l", [P, 512])
            ps_h = psum(ctx, "ps_h", [P, 2, 512])
            ps_y = psum(ctx, "ps_y", [P, 512])
            f_chain, f_var, f_std, xf_ready, f_turned, f_copied, logits_ready = sems(
                "f_chain", "f_var", "f_std", "xf_ready", "f_turned", "f_copied", "logits_ready")
            f_in, earlier_set, ex_in, ex_ready, small_turned, small_ready = sems(
                "f_in", "earlier_set", "ex_in", "ex_ready", "small_turned", "small_ready")
            exp_in = sems("exp_in0", "exp_in1")
            xe_ready, h_ready, hid_ready, y_ready, y_used, out_done = sems(
                "xe_ready", "h_ready", "hid_ready", "y_ready", "y_used", "out_done")
            block = ctx.enter_context(nc.Block())

            @block.sync
            def _(sp):
                sp.dma_start(wr[:], Wr.rearrange("(k p) e -> p k e", p=P)).then_inc(f_in, 16)
                sp.dma_start(br_row[:], br.rearrange("(o e) -> o e", o=1)).then_inc(f_in, 16)
                sp.dma_start(b1_rows[:], b1.rearrange("e (f p) -> (e f) p", p=P)).then_inc(f_in, 16)
                sp.dma_start(ln_rows[:, 0, :], ln_g.rearrange("e (k p) -> (e k) p", p=P)).then_inc(f_in, 16)
                sp.dma_start(ln_rows[:, 1, :], ln_b.rearrange("e (k p) -> (e k) p", p=P)).then_inc(f_in, 16)
                sp.dma_start(b2_row[:], b2.rearrange("(o e) c -> o e c", o=1)).then_inc(f_in, 16)

                def load(e, s):
                    sp.dma_start(w1[:, s], W1[ds(e, 1), :, :].rearrange("o (k p) h -> p (o k) h", p=P)).then_inc(exp_in[s], 16)
                    sp.dma_start(w2[:, s], W2[ds(e, 1), :, :].rearrange("o (k p) h -> p (o k) h", p=P)).then_inc(exp_in[s], 16)

                load(0, 0)
                load(1, 1)
                with sp.Fori(0, X // 2 - 1) as i:
                    for s in range(2):
                        sp.wait_ge(y_ready, (i * 2 + (s + 1)) * NB)
                        load(i * 2 + (s + 2), s)
                sp.wait_ge(y_used, X * NB)
                sp.dma_start(out[0:d.FULL * P, :].rearrange("(b p) c -> p b c", p=P), res[:, 0:d.FULL, :]).then_inc(out_done, 16)
                sp.dma_start(out[d.FULL * P:N, :], res[0:d.TAIL, d.FULL, :]).then_inc(out_done, 16)
                sp.wait_ge(out_done, 32)

            @block.gpsimd
            def _(pool):
                pool.iota(equal[:, 0], [[1, X], [-1, X]], base=0, channel_multiplier=0,
                          allow_small_or_imprecise_dtypes=True).then_inc(earlier_set, 1)
                pool.wait_ge(earlier_set, 1)
                pool.tensor_scalar(earlier[:], equal[:, 0], 0.0, None, ALU.is_gt).then_inc(earlier_set, 1)

            @block.vector
            def _(dve):
                link = Chain(dve, f_chain)
                layer_norm_stats(dve, f_var, f_std, link, res, 1)
                normalize(dve, xn, res).then_inc(xf_ready, 1)
                dve.wait_ge(xf_ready, 1)
                layer_norm_stats(dve, f_var, f_std, link, xn, 2)
                dve.wait_ge(logits_ready, 1)
                normalize(dve, xn, xn).then_inc(xf_ready, 1)
                link(dve.tensor_copy(logits[:].rearrange("p b e -> p (b e)"), ps_l[:, 0:NB * X]))
                dve.wait_ge(earlier_set, 2)
                mine = logits[:].unsqueeze(3).broadcast_to([P, NB, X, X])
                other = logits[:].unsqueeze(2).broadcast_to([P, NB, X, X])
                link(dve.tensor_tensor(higher[:], other, mine, ALU.is_gt))
                link(dve.tensor_tensor(equal[:], other, mine, ALU.is_equal))
                link(dve.tensor_tensor(equal[:], equal[:], earlier[:].unsqueeze(1).broadcast_to([P, NB, X, X]), ALU.mult))
                link(dve.tensor_tensor(higher[:], higher[:], equal[:], ALU.add))
                link(dve.tensor_reduce(order[:], higher[:], AX, ALU.add))
                link(dve.tensor_scalar(order[:], order[:], 2.0, None, ALU.is_lt))
                link(dve.tensor_reduce(best[:], logits[:], AX, ALU.max))
                dve.tensor_tensor(logits[:], logits[:], best[:].unsqueeze(2).broadcast_to([P, NB, X]), ALU.subtract).then_inc(ex_in, 1)
                dve.wait_ge(ex_ready, 1)
                link(dve.tensor_tensor(gate3, gate3, order[:], ALU.mult))
                link(dve.tensor_reduce(best[:], gate3, AX, ALU.add))
                link(dve.reciprocal(best[:], best[:]))
                link(dve.tensor_tensor(gate3, gate3, best[:].unsqueeze(2).broadcast_to([P, NB, X]), ALU.mult))
                for n in range(2):
                    dve.wait_ge(small_turned, 3)
                    link(dve.tensor_copy(ln_t[:, n, :], ps_h[:, n, 0:X * KD]))
                dve.tensor_copy(b1_t[:], ps_y[:, 0:X * FH]).then_inc(small_ready, 1)
                dve.wait_ge(small_ready, 1)
                dve.wait_ge(f_copied, 4 * NB)
                with dve.Fori(0, X) as e:
                    with dve.Fori(0, NB) as b:
                        n = e * NB + b
                        dve.wait_ge(h_ready, n * 2)
                        for k in range(KD):
                            dve.tensor_scalar(x_e[:, k, :], tok_t[:, k, ds(b * P, P)], ln_t[:, 0, ds(e * KD + k, 1)],
                                              ln_t[:, 1, ds(e * KD + k, 1)], ALU.mult, ALU.add).then_inc(xe_ready, 1)
                        dve.wait_ge(y_ready, n + 1)
                        dve.wait_ge(y_used, n)
                        row = res[:, ds(b, 1), :].rearrange("p b c -> p (b c)")
                        dve.scalar_tensor_tensor(row, ps_y[:, 0:D], gate[:, ds(b * X + e, 1)], row, ALU.mult, ALU.add).then_inc(y_used, 1)

            @block.scalar
            def _(act):
                for n in range(2):
                    act.wait_ge(f_var, n + 1)
                    act.activation(rstd[:], tmp_b[:], ACT.Sqrt).then_inc(f_std, 1)
                    if n == 0:
                        with act.Fori(0, NB) as b:
                            for k in range(KD):
                                act.wait_ge(f_turned, b * KD + k + 1)
                                act.copy(tok_t[:, k, ds(b * P, P)], ps_t[:, k, 0:P]).then_inc(f_copied, 1)
                act.wait_ge(ex_in, 1)
                act.activation(gate3, logits[:], ACT.Exp).then_inc(ex_ready, 1)
                with act.Fori(0, NB) as b:
                    for k in range(KD):
                        act.wait_ge(f_turned, b * KD + (k + 1 + NB * KD))
                        act.copy(tok_t[:, k, ds(b * P, P)], ps_t[:, k, 0:P]).then_inc(f_copied, 1)
                act.wait_ge(small_ready, 1)
                with act.Fori(0, X) as e:
                    with act.Fori(0, NB) as b:
                        n = e * NB + b
                        act.wait_ge(y_ready, n)
                        for f in range(FH):
                            if f % 4 == 0:
                                act.wait_ge(h_ready, n * 2 + f // 4 + 1)
                            act.activation(hid[:, f, :], ps_h[:, f // 4, f % 4 * P:(f % 4 + 1) * P], ACT.Gelu,
                                           bias=b1_t[:, ds(e * FH + f, 1)]).then_inc(hid_ready, 1)

            @block.tensor
            def _(pe):
                pe.wait_ge(f_in, 96)
                pe.wait_ge(xf_ready, 1)
                for n in range(2):
                    if n:
                        pe.wait_ge(xf_ready, 2)
                    for b in range(NB):
                        for k in range(KD):
                            if b or n:
                                pe.wait_ge(f_copied, (n * NB + b - 1) * KD + k + 1)
                            pe.transpose(ps_t[:, k, 0:P], xn[:, b, k * P:(k + 1) * P], ident[:]).then_inc(f_turned, 1)
                    if n == 0:
                        pe.wait_ge(f_copied, NB * KD)
                        for b in range(NB):
                            for k in range(KD):
                                pe.matmul(ps_l[:, b * X:(b + 1) * X], tok_t[:, k, b * P:(b + 1) * P], wr[:, k, :], start=(k == 0), stop=False)
                            last = pe.matmul(ps_l[:, b * X:(b + 1) * X], ones[0:1, :], br_row[:], start=False, stop=True)
                        last.then_inc(logits_ready, 1)
                        for m in range(2):
                            pe.transpose(ps_h[:, m, 0:X * KD], ln_rows[:, m, :], ident[0:X * KD, 0:X * KD]).then_inc(small_turned, 1)
                        pe.transpose(ps_y[:, 0:X * FH], b1_rows[:], ident[0:X * FH, 0:X * FH]).then_inc(small_turned, 1)
                pe.wait_ge(small_ready, 1)
                with pe.Fori(0, X // 2) as i:
                    for s in range(2):
                        with pe.Fori(0, NB) as b:
                            n = i * 2 * NB + s * NB + b
                            pe.wait_ge(exp_in[s], (i + 1) * 32)
                            pe.wait_ge(xe_ready, (n + 1) * KD)
                            pe.wait_ge(hid_ready, n * FH)
                            for f in range(FH):
                                for k in range(KD):
                                    last = pe.matmul(ps_h[:, f // 4, f % 4 * P:(f % 4 + 1) * P], w1[:, s, k, f * P:(f + 1) * P], x_e[:, k, :],
                                                     start=(k == 0), stop=(k == KD - 1))
                                if f % 4 == 3:
                                    last.then_inc(h_ready, 1)
                            pe.wait_ge(y_used, n)
                            for f in range(FH):
                                pe.wait_ge(hid_ready, n * FH + f + 1)
                                pe.matmul(ps_y[:, 0:D], hid[:, f, :], w2[:, s, f, :], start=(f == 0), stop=False)
                            pe.matmul(ps_y[:, 0:D], ones[0:1, :], b2_row[:, ds(i * 2 + s, 1), :].rearrange("o e c -> o (e c)"), start=False,
                                      stop=True).then_inc(y_ready, 1)


_INS = ['x', 'src', 'dst', 'edge_attr_5', 'node_type_19', 'L0_gnn_Wk', 'L0_gnn_bk', 'L0_gnn_Wq', 'L0_gnn_bq',
        'L0_gnn_Wv', 'L0_gnn_bv', 'L0_gnn_Wa', 'L0_gnn_ba', 'L0_gnn_gamma', 'L0_gnn_beta', 'L0_gnn_w_time',
        'L0_gnn_b_time', 'L0_ffn_Wr', 'L0_ffn_br', 'L0_ffn_ln_g', 'L0_ffn_ln_b', 'L0_ffn_W1', 'L0_ffn_b1',
        'L0_ffn_W2', 'L0_ffn_b2']


def kernel(**inputs):
    import numpy as _np
    import concourse.bacc as _bacc
    from concourse import mybir as _mybir
    from concourse.bass_utils import run_bass_kernel_spmd as _run

    nc = _bacc.Bacc("TRN2", target_bir_lowering=False, num_devices=1)
    arrays, args = {}, []
    for name in _INS:
        a = _np.ascontiguousarray(inputs[name])
        arrays[f"in_{name}"] = a
        args.append(nc.dram_tensor(f"in_{name}", a.shape, _mybir.dt.from_np(a.dtype), kind="ExternalInput").ap())
    args.append(nc.dram_tensor("out_x", inputs["x"].shape, _mybir.dt.float32, kind="ExternalOutput").ap())
    gnn_ffn_kernel(nc, *args)
    r = _run(nc, [arrays], core_ids=[0])
    return r.results[0]["out_x"]
```

```python
from contextlib import ExitStack

import concourse.bass as bass
from concourse import mybir

F32 = mybir.dt.float32
I32 = mybir.dt.int32
BF16 = mybir.dt.bfloat16
ALU = mybir.AluOpType
ACT = mybir.ActivationFunctionType
AX = mybir.AxisListType.X

P = 128
TWO_PI = 6.283185307179586
SIN_SCALE = 6.283185
MAGIC = 12582912.0
BIG = 1.0e30
RESET = -2.0e38
LN_EPS = 1e-5


class Chain:

    def __init__(self, eng, sem, base=0):
        self.eng, self.sem, self.base, self.n = eng, sem, base, 0

    def __call__(self, ins):
        self.n += 1
        ins.then_inc(self.sem, 1)
        self.eng.wait_ge(self.sem, self.base + self.n)


class At:

    def __init__(self, i, c):
        self.i, self.c, self.t = i, c, i * 4 + c

    def slot(self, k):
        return self.c % k

    def turn(self, k):
        return self.i * (4 // k) + self.c // k

    def __add__(self, n):
        return At(self.i, self.c + n)


def walk(eng, steps, step):
    for t in range(min(4, steps)):
        step(At(0, t))
    loops = (steps - 5) // 4
    with eng.Fori(0, loops) as i:
        for u in range(4):
            step(At(i, 4 + u))
    for t in range(4 + 4 * loops, steps):
        step(At(0, t))


def wait_slot(eng, sem, a, slots, by=1):
    if a.c >= slots:
        eng.wait_ge(sem, a.turn(slots) * by)


def wait_done(eng, sem, a, back=0):
    if a.c >= back:
        eng.wait_ge(sem, a.t + (1 - back))


class Dims:

    def __init__(self, x, src, Wk, Wa, w_time, W1):
        self.N, self.D = x.shape
        self.E = src.shape[0]
        self.T, _, self.PROJ = Wk.shape
        self.TD = w_time.shape[0]
        self.KD = self.D // P
        self.H = 4
        self.DK = (self.D - self.TD) // self.H
        self.LAST = self.PROJ - 3 * self.DK
        self.NB = -(-self.N // P)
        self.NP = self.NB * P
        self.FULL = self.N // P
        self.TAIL = self.N - self.FULL * P
        self.C = 8
        self.EC = -(-self.E // (P * self.C)) * self.C
        self.EFULL = self.E // self.EC
        self.ETAIL = self.E - self.EFULL * self.EC
        self.KB = 2 * self.NB
        self.G = 4
        self.R = 4
        rows = 2 * self.EC * P // self.G + self.KB * P
        self.RT = -(-rows // (P * self.R)) * self.R
        self.NR = self.RT * P
        self.QKV = 2 * self.PROJ + self.DK
        self.MSG = self.D + self.H
        self.X, _, self.HID = W1.shape
        self.TOP = 2
        self.XT = self.TOP * self.NB + self.X - 1


def gnn_ffn_kernel(nc, x, src, dst, edge_attr, node_type, Wk, bk, Wq, bq, Wv, bv, Wa, ba, gamma, beta,
                   w_time, b_time, Wr, br, ln_g, ln_b, W1, b1, W2, b2, out):
    d = Dims(x, src, Wk, Wa, w_time, W1)
    N, D, E, T, KD, NB, NPAD = d.N, d.D, d.E, d.T, d.KD, d.NB, d.NP
    PROJ, TD, H, DK, LAST = d.PROJ, d.TD, d.H, d.DK, d.LAST
    G, R, RT, NR, KB, EC, C = d.G, d.R, d.RT, d.NR, d.KB, d.EC, d.C
    ds = bass.ds

    KVW = 2 * PROJ + TD
    kv_dram = nc.dram_tensor("kv_table", (1 + NPAD, KVW), F32).ap()
    q_dram = nc.dram_tensor("q_table", (NPAD, DK), F32).ap()
    keyrow_dram = nc.dram_tensor("key_rows", (2 * EC, P), F32).ap()
    lorow_dram = nc.dram_tensor("lo_rows", (2 * EC, P), F32).ap()
    rec_dram = nc.dram_tensor("edge_records", (NR * G, 4), F32).ap()
    marks_dram = nc.dram_tensor("row_marks", (NR + P, 1), F32).ap()
    part_dram = nc.dram_tensor("row_messages", (NR, d.MSG), F32).ap()
    sorted_dram = nc.dram_tensor("tokens_by_expert", (d.XT * P, D), F32).ap()
    expert_out_dram = nc.dram_tensor("expert_out", (d.XT * P, D), F32).ap()
    wk_dram = nc.dram_tensor("row_weights", (NR, H + 1), F32).ap()

    top = ExitStack()
    with top:
        def sbuf(ctx, name, shape, dt=F32):
            return ctx.enter_context(nc.sbuf_tensor(name, shape, dt))

        def psum(ctx, name, shape, dt=F32):
            return ctx.enter_context(nc.psum_tensor(name, shape, dt))

        in_use = []

        def sems(*names):
            made = [nc.alloc_semaphore(name=n) for n in names]
            in_use.extend(made)
            return made

        def clear_sems():
            nc.clear_and_free_semaphores(list(in_use))
            in_use.clear()
            nc.all_engine_barrier()

        pool_turn = nc.alloc_semaphore(name="pool_turn")

        xn = sbuf(top, "xn", [P, NB, D])
        res = sbuf(top, "res", [P, NB, D])
        ident = sbuf(top, "ident", [P, P])
        ones = sbuf(top, "ones", [P, P])
        before = sbuf(top, "before", [P, P])
        after = sbuf(top, "after", [P, P])
        lane = sbuf(top, "lane", [P, 2 * P])
        lane_col = sbuf(top, "lane_col", [P, 1])
        magic = sbuf(top, "magic", [P, 1])
        type_onehot = sbuf(top, "type_onehot", [T, NPAD])
        type_bc = sbuf(top, "type_bc", [P, NPAD], I32)
        stats = sbuf(top, "stats", [P, NB, 6])
        mean = sbuf(top, "mean", [P, NB])
        rstd = sbuf(top, "rstd", [P, NB])
        tmp_a = sbuf(top, "tmp_a", [P, NB])
        tmp_b = sbuf(top, "tmp_b", [P, NB])

        def layer_norm_stats(dve, act_in, act_out, link, source, turn):
            for b in range(NB):
                last = dve.bn_stats(stats[:, b, :], source[:, b, :])
            link(last)
            link(dve.tensor_tensor(mean[:], stats[:, :, 1], stats[:, :, 4], ALU.add))
            link(dve.tensor_tensor(tmp_a[:], stats[:, :, 1], stats[:, :, 4], ALU.subtract))
            link(dve.tensor_tensor(tmp_b[:], stats[:, :, 2], stats[:, :, 5], ALU.add))
            link(dve.tensor_scalar(mean[:], mean[:], 0.5, None, ALU.mult))
            link(dve.tensor_tensor(tmp_a[:], tmp_a[:], tmp_a[:], ALU.mult))
            link(dve.tensor_scalar(tmp_a[:], tmp_a[:], 0.25, LN_EPS, ALU.mult, ALU.add))
            dve.scalar_tensor_tensor(tmp_b[:], tmp_b[:], 1.0 / D, tmp_a[:], ALU.mult, ALU.add).then_inc(act_in, 1)
            dve.wait_ge(act_out, turn)
            link(dve.reciprocal(rstd[:], rstd[:]))

        def normalize(dve, dst_t, source):
            for b in range(NB):
                last = dve.tensor_scalar(dst_t[:, b, :], source[:, b, :], mean[:, b:b + 1], rstd[:, b:b + 1],
                                         ALU.subtract, ALU.mult)
            return last

        with ExitStack() as ctx:
            wcat = sbuf(ctx, "wcat", [P, T * KD, d.QKV])
            wq_st = sbuf(ctx, "wq_st", [P, T * KD, PROJ])
            bcat = sbuf(ctx, "bcat", [T, d.QKV])
            bq_st = sbuf(ctx, "bq_st", [T, PROJ])
            x_sb = xn
            xT = res[:].rearrange("p b c -> p (b c)").rearrange("p (k n) -> p k n", k=KD)
            masked = sbuf(ctx, "masked", [P, 4, KD, P])
            qkv = sbuf(ctx, "qkv", [P, KVW + DK])
            onehot_st = sbuf(ctx, "onehot_st", [T, P])
            zero_row = sbuf(ctx, "zero_row", [1, KVW])
            ps_t = psum(ctx, "ps_t", [P, 2, 512])
            ps_qkv = psum(ctx, "ps_qkv", [P, 512])
            x_in, type_in, wq_in, w_in = sems("x_in", "type_in", "wq_in", "w_in")
            zeroed, consts, var_ready, std_ready = sems("zeroed", "consts", "var_ready", "std_ready")
            dve_chain, xn_ready, tp_ready, xT_ready = sems("dve_chain", "xn_ready", "tp_ready", "xT_ready")
            mask_ready, mask_used, qkv_ready, qkv_copied = sems("mask_ready", "mask_used", "qkv_ready", "qkv_copied")
            stored, zero_out, q_folded, const_chain = sems("stored", "zero_out", "q_folded", "const_chain")
            block = ctx.enter_context(nc.Block())

            @block.sync
            def _(sp):
                sp.wait_ge(zeroed, 3)
                sp.dma_start(x_sb[:, 0:d.FULL, :], x[0:d.FULL * P, :].rearrange("(b p) c -> p b c", p=P)).then_inc(x_in, 16)
                sp.dma_start(x_sb[0:d.TAIL, d.FULL, :], x[d.FULL * P:N, :]).then_inc(x_in, 16)
                sp.dma_start(type_bc[:, 0:N], node_type.rearrange("(o n) -> o n", o=1).broadcast_to([P, N])).then_inc(type_in, 16)
                sp.dma_start(wq_st[:], Wq.rearrange("t (k p) c -> p (t k) c", p=P)).then_inc(wq_in, 16)
                sp.dma_start(bq_st[:], bq).then_inc(wq_in, 16)
                sp.dma_start(wcat[:, :, 0:PROJ], Wk.rearrange("t (k p) c -> p (t k) c", p=P)).then_inc(w_in, 16)
                sp.dma_start(wcat[:, :, PROJ:2 * PROJ], Wv.rearrange("t (k p) c -> p (t k) c", p=P)).then_inc(w_in, 16)
                sp.dma_start(bcat[:, 0:PROJ], bk).then_inc(w_in, 16)
                sp.dma_start(bcat[:, PROJ:2 * PROJ], bv).then_inc(w_in, 16)
                sp.dma_start(kv_dram[0:1, :], zero_row[:]).then_inc(zero_out, 16)
                with sp.Fori(0, NB) as b:
                    sp.wait_ge(qkv_copied, b + 1)
                    sp.dma_start(kv_dram[ds(b * P + 1, P), :], qkv[:, 0:KVW]).then_inc(stored, 16)
                    sp.dma_start(q_dram[ds(b * P, P), :], qkv[:, KVW:]).then_inc(stored, 16)
                sp.wait_ge(stored, 32 * NB)
                sp.wait_ge(zero_out, 16)

            @block.gpsimd
            def _(pool):
                pool.memset(x_sb[:, d.FULL:NB, :], 0.0).then_inc(zeroed, 1)
                pool.memset(type_bc[:, N:NPAD], 0).then_inc(zeroed, 1)
                pool.memset(qkv[:, PROJ:PROJ + TD], 0.0)
                pool.memset(zero_row[:], 0.0).then_inc(zeroed, 1)
                pool.memset(magic[:], MAGIC)
                pool.memset(ones[:], 1.0).then_inc(const_chain, 1)
                pool.iota(lane[:], [[1, 2 * P]], base=0, channel_multiplier=0,
                          allow_small_or_imprecise_dtypes=True).then_inc(const_chain, 1)
                pool.iota(lane_col[:], [[0, 1]], base=0, channel_multiplier=1,
                          allow_small_or_imprecise_dtypes=True).then_inc(const_chain, 1)
                pool.wait_ge(const_chain, 3)
                pool.tensor_scalar(ident[:], lane[:, 0:P], lane_col[:, 0:1], None, ALU.is_equal).then_inc(consts, 1)
                pool.tensor_scalar(before[:], lane[:, 0:P], lane_col[:, 0:1], None, ALU.is_gt).then_inc(consts, 1)
                pool.tensor_scalar(after[:], lane[:, 0:P], lane_col[:, 0:1], None, ALU.is_lt).then_inc(consts, 1)

            @block.vector
            def _(dve):
                link = Chain(dve, dve_chain)
                dve.wait_ge(x_in, 32)
                layer_norm_stats(dve, var_ready, std_ready, link, x_sb, 1)
                normalize(dve, xn, x_sb).then_inc(xn_ready, 1)
                dve.wait_ge(wq_in, 32)
                for wt, wst in ((wcat[:, :, 2 * PROJ:d.QKV], wq_st[:, :, :]),
                                (bcat[:, 2 * PROJ:d.QKV], bq_st[:, :])):
                    cut = (lambda t, a, b: t[:, :, a:b]) if len(wt.shape) == 3 else (lambda t, a, b: t[:, a:b])
                    link(dve.tensor_tensor(wt, cut(wst, 0, DK), cut(wst, DK, 2 * DK), ALU.add))
                    link(dve.tensor_tensor(wt, wt, cut(wst, 2 * DK, 3 * DK), ALU.add))
                    link(dve.tensor_tensor(cut(wt, 0, LAST), cut(wt, 0, LAST), cut(wst, 3 * DK, PROJ), ALU.add))
                dve.wait_ge(type_in, 16)
                dve.wait_ge(consts, 3)
                link(dve.tensor_scalar(type_onehot[:], type_bc[0:T, :], lane_col[0:T, 0:1], None, ALU.is_equal))
                dve.sem_inc(q_folded, 1)
                with dve.Fori(0, NB) as b:
                    dve.wait_ge(xT_ready, b * KD + KD)
                    for t in range(T):
                        dve.wait_ge(mask_used, b * T if t < 4 else b * T + t - 3)
                        dve.scalar_tensor_tensor(masked[:, t % 4, :, :],
                                                 type_bc[:, ds(b * P, P)].unsqueeze(1).broadcast_to([P, KD, P]), float(t),
                                                 xT[:, :, ds(b * P, P)], ALU.is_equal, ALU.mult).then_inc(mask_ready, 1)
                    dve.wait_ge(qkv_ready, b)
                    dve.tensor_copy(onehot_st[:], type_onehot[:, ds(b * P, P)]).then_inc(mask_ready, 1)

            @block.scalar
            def _(act):
                act.wait_ge(var_ready, 1)
                act.activation(rstd[:], tmp_b[:], ACT.Sqrt).then_inc(std_ready, 1)
                with act.Fori(0, NB) as b:
                    for k in range(KD):
                        act.wait_ge(tp_ready, b * KD + k + 1)
                        act.copy(xT[:, k, ds(b * P, P)], ps_t[:, k, 0:P]).then_inc(xT_ready, 1)
                with act.Fori(0, NB) as b:
                    act.wait_ge(qkv_ready, b + 1)
                    act.wait_ge(stored, b * 32)
                    act.copy(qkv[:, 0:PROJ], ps_qkv[:, 0:PROJ])
                    act.copy(qkv[:, PROJ + TD:], ps_qkv[:, PROJ:d.QKV]).then_inc(qkv_copied, 1)

            @block.tensor
            def _(pe):
                pe.wait_ge(consts, 3)
                pe.wait_ge(xn_ready, 1)
                for b in range(NB):
                    for k in range(KD):
                        if b:
                            pe.wait_ge(xT_ready, b * KD + k - KD + 1)
                        pe.transpose(ps_t[:, k, 0:P], xn[:, b, k * P:(k + 1) * P], ident[:]).then_inc(tp_ready, 1)
                pe.wait_ge(w_in, 64)
                pe.wait_ge(q_folded, 1)
                with pe.Fori(0, NB) as b:
                    pe.wait_ge(qkv_copied, b)
                    for t in range(T):
                        pe.wait_ge(mask_ready, b * (T + 1) + t + 1)
                        for k in range(KD):
                            last = pe.matmul(ps_qkv[:, 0:d.QKV], masked[:, t % 4, k, :], wcat[:, t * KD + k, :],
                                             start=(t == 0 and k == 0), stop=False)
                        last.then_inc(mask_used, 1)
                    pe.wait_ge(mask_ready, (b + 1) * (T + 1))
                    pe.matmul(ps_qkv[:, 0:d.QKV], onehot_st[:], bcat[:], start=False, stop=True).then_inc(qkv_ready, 1)


        row_base = sbuf(top, "row_base", [P, KB])

        NC = 2 * EC // C
        edges = ExitStack()
        with edges:
            rec = sbuf(edges, "rec", [P, 2 * EC, 4])
            key_f = sbuf(edges, "key_f", [P, 2 * EC])
            lo_f = sbuf(edges, "lo_f", [P, 2 * EC])
            hi_f = sbuf(edges, "hi_f", [P, 2 * EC])

            with ExitStack() as ctx:
                ends = [sbuf(ctx, "src_i", [P, EC], I32), sbuf(ctx, "dst_i", [P, EC], I32)]
                attr = sbuf(ctx, "attr", [P, EC, edge_attr.shape[1]])
                key_i = sbuf(ctx, "key_i", [P, 2 * EC], I32)
                lo_i = sbuf(ctx, "lo_i", [P, 2 * EC], I32)
                hi_i = sbuf(ctx, "hi_i", [P, 2 * EC], I32)
                zeros = sbuf(ctx, "zeros", [P, NR * G * 4 // P])
                zeros_b = sbuf(ctx, "zeros_b", [P, P], BF16)
                TC = 104
                NTC = 2 * EC // TC
                rows_sb = sbuf(ctx, "rows_sb", [TC, 2, NTC, P])
                lane_b = sbuf(ctx, "lane_b", [P, P], BF16)
                lo_hot = sbuf(ctx, "lo_hot", [P, 2, C, P], BF16)
                hi_hot = sbuf(ctx, "hi_hot", [P, 2, C, KB], BF16)
                cnt_i = sbuf(ctx, "cnt_i", [P, KB], I32)
                rows_f = sbuf(ctx, "rows_f", [P, KB])
                totals = sbuf(ctx, "totals", [P, KB])
                upto = sbuf(ctx, "upto", [P, KB])
                within = sbuf(ctx, "within", [P, KB])
                ps_row = psum(ctx, "ps_row", [P, 2, 512])
                ps_cnt = psum(ctx, "ps_cnt", [P, 512])
                ps_pre = psum(ctx, "ps_pre", [P, 2, 512])
                e_clear, e_in, keys_ready, lanes_ready, e_chain = sems("e_clear", "e_in", "keys_ready", "lanes_ready", "e_chain")
                row_tp, row_copied, rows_out, zeros_out = sems("row_tp", "row_copied", "rows_out", "zeros_out")
                hot_ready, cnt_ready, rows_ready, pre_ready = sems("hot_ready", "cnt_ready", "rows_ready", "pre_ready")
                hot_used = sems("hot_used0", "hot_used1")
                block = ctx.enter_context(nc.Block())

                @block.sync
                def _(sp):
                    sp.wait_ge(e_clear, 3)
                    for t, a in ((ends[0][:], src.rearrange("(n o) -> n o", o=1)),
                                 (ends[1][:], dst.rearrange("(n o) -> n o", o=1)),
                                 (attr[:].rearrange("p c a -> p (c a)"), edge_attr)):
                        sp.dma_start(t[0:d.EFULL, :], a[0:d.EFULL * EC, :].rearrange("(p c) a -> p (c a)", p=d.EFULL)).then_inc(e_in, 16)
                        sp.dma_start(t[d.EFULL:P, 0:d.ETAIL * a.shape[1]],
                                     a[d.EFULL * EC:E, :].rearrange("(p c) a -> p (c a)", p=1)).then_inc(e_in, 16)
                    sp.wait_ge(e_clear, 4)
                    sp.dma_start(rec_dram.rearrange("(p c) w -> p (c w)", p=P), zeros[:]).then_inc(zeros_out, 16)
                    sp.dma_start(marks_dram.rearrange("(p c) w -> p (c w)", p=P), zeros[:, 0:NR // P + 1]).then_inc(zeros_out, 16)
                    fill = sorted_dram.rearrange("(p c) w -> p (c w)", p=P)
                    FC = d.XT * D // 4
                    for n in range(4):
                        sp.dma_start(fill[:, n * FC:(n + 1) * FC], zeros[:, 0:FC]).then_inc(zeros_out, 16)
                    sp.wait_ge(row_copied, 2 * NTC)
                    for n, t in enumerate((keyrow_dram, lorow_dram)):
                        sp.dma_start(t.rearrange("(b r) c -> r b c", r=TC), rows_sb[:, n, :, :]).then_inc(rows_out, 16)
                    sp.wait_ge(zeros_out, 96)
                    sp.wait_ge(rows_out, 32)

                @block.gpsimd
                def _(pool):
                    pool.memset(ends[0][:], N).then_inc(e_clear, 1)
                    pool.memset(ends[1][:], N).then_inc(e_clear, 1)
                    pool.memset(attr[:], 0.0).then_inc(e_clear, 1)
                    pool.memset(zeros[:], 0.0).then_inc(e_clear, 1)

                @block.vector
                def _(dve):
                    link = Chain(dve, e_chain)
                    link(dve.memset(zeros_b[:], 0.0))
                    link(dve.tensor_copy(lane_b[:], lane[:, 0:P]))
                    dve.wait_ge(e_in, 96)
                    for way in range(2):
                        cols = slice(way * EC, (way + 1) * EC)
                        link(dve.tensor_scalar(rec[:, cols, 0], ends[way][:], 1.0, None, ALU.add))
                        link(dve.tensor_scalar(key_i[:, cols], ends[1 - way][:], float(way * NPAD), None, ALU.add))
                    dve.tensor_copy(key_f[:], key_i[:]).then_inc(keys_ready, 1)
                    link(dve.tensor_scalar(lo_i[:], key_i[:], P - 1, None, ALU.bitwise_and))
                    link(dve.tensor_scalar(hi_i[:], key_i[:], 7, None, ALU.arith_shift_right))
                    dve.tensor_copy(lo_f[:], lo_i[:]).then_inc(lanes_ready, 1)
                    link(dve.tensor_copy(hi_f[:], hi_i[:]))
                    dve.wait_ge(lanes_ready, 1)
                    with dve.Fori(0, NC // 2) as i:
                        for s in range(2):
                            c = i * 2 + s
                            dve.wait_ge(hot_used[s], i)
                            dve.tensor_tensor(lo_hot[:, s], lane_b[:].unsqueeze(1).broadcast_to([P, C, P]),
                                              lo_f[:, ds(c * C, C)].unsqueeze(2).broadcast_to([P, C, P]),
                                              ALU.is_equal).then_inc(hot_ready, 1)
                            dve.tensor_tensor(hi_hot[:, s], lane_b[:, 0:KB].unsqueeze(1).broadcast_to([P, C, KB]),
                                              hi_f[:, ds(c * C, C)].unsqueeze(2).broadcast_to([P, C, KB]),
                                              ALU.is_equal).then_inc(hot_ready, 1)
                    dve.wait_ge(cnt_ready, 1)
                    link(dve.tensor_copy(cnt_i[:], ps_cnt[:, 0:KB]))
                    link(dve.tensor_scalar(cnt_i[:], cnt_i[:], float(G - 1), None, ALU.add))
                    link(dve.tensor_scalar(cnt_i[:], cnt_i[:], G.bit_length() - 1, None, ALU.arith_shift_right))
                    dve.tensor_scalar(rows_f[:], cnt_i[:], 1.0, None, ALU.max).then_inc(rows_ready, 1)
                    dve.wait_ge(pre_ready, 1)
                    link(dve.tensor_copy(totals[:], ps_pre[:, 1, 0:KB]))
                    link(dve.tensor_copy(within[:], ps_pre[:, 0, 0:KB]))
                    link(dve.tensor_tensor_scan(upto[:], ones[:, 0:KB], totals[:], 0.0, ALU.mult, ALU.add))
                    link(dve.tensor_tensor(upto[:], upto[:], totals[:], ALU.subtract))
                    link(dve.tensor_tensor(row_base[:], upto[:], within[:], ALU.add))

                @block.scalar
                def _(act):
                    act.wait_ge(e_in, 96)
                    for way, words in enumerate(((0, 1, 2), (0, 2, 1))):
                        for w, a in enumerate(words):
                            act.activation(rec[:, way * EC:(way + 1) * EC, 1 + w], attr[:, :, a], ACT.Ln, bias=1.0)
                    for n in range(2 * NTC):
                        act.wait_ge(row_tp, n + 1)
                        act.copy(rows_sb[:, n // NTC, n % NTC, :], ps_row[0:TC, n % 2, 0:P]).then_inc(row_copied, 1)

                @block.tensor
                def _(pe):
                    pe.wait_ge(keys_ready, 1)
                    pe.wait_ge(lanes_ready, 1)
                    for n in range(2 * NTC):
                        if n >= 2:
                            pe.wait_ge(row_copied, n - 1)
                        t = (key_f, lo_f)[n // NTC]
                        pe.transpose(ps_row[0:TC, n % 2, 0:P], t[:, n % NTC * TC:(n % NTC + 1) * TC], ident[:]).then_inc(row_tp, 1)
                    pe.wait_ge(hot_ready, 1)
                    pe.matmul(ps_cnt[:, 0:KB], zeros_b[:], lane_b[:, 0:KB], start=True, stop=False, skip_group_check=True)
                    with pe.Fori(0, NC // 2) as i:
                        for s in range(2):
                            pe.wait_ge(hot_ready, i * 4 + s * 2 + 2)
                            for j in range(C):
                                last = pe.matmul(ps_cnt[:, 0:KB], lo_hot[:, s, j, :], hi_hot[:, s, j, :], start=False,
                                                 stop=False, skip_group_check=True)
                            last.then_inc(hot_used[s], 1)
                    pe.matmul(ps_cnt[:, 0:KB], zeros_b[:], lane_b[:, 0:KB], start=False, stop=True,
                              skip_group_check=True).then_inc(cnt_ready, 1)
                    pe.wait_ge(rows_ready, 1)
                    pe.matmul(ps_pre[:, 0, 0:KB], before[:], rows_f[:], start=True, stop=True)
                    pe.matmul(ps_pre[:, 1, 0:KB], ones[:], rows_f[:], start=True, stop=True).then_inc(pre_ready, 1)

            with ExitStack() as ctx:
                key_row = sbuf(ctx, "key_row", [P, 2, C, P])
                lo_row = sbuf(ctx, "lo_row", [P, 2, C, P])
                lo_hot_t = sbuf(ctx, "lo_hot_t", [P, 2, C, P])
                lo_hot = sbuf(ctx, "lo_hot2", [P, 2, C, P])
                hi_hot = sbuf(ctx, "hi_hot2", [P, 2, C, KB])
                same = sbuf(ctx, "same", [P, C, P])
                picked = sbuf(ctx, "picked", [P, C, KB])
                rank = sbuf(ctx, "rank", [P, 2, C])
                seen = sbuf(ctx, "seen", [P, C])
                place = sbuf(ctx, "place", [P, 2, C], I32)
                rec_st = sbuf(ctx, "rec_st", [P, 2, C, 4])
                base_g = sbuf(ctx, "base_g", [P, KB])
                so_far = sbuf(ctx, "so_far", [P, 2, KB])
                base_i = sbuf(ctx, "base_i", [P, KB], I32)
                MK = 10
                mark_st = sbuf(ctx, "mark_st", [P, MK], I32)
                ps_sofar = psum(ctx, "ps_sofar", [P, 512])
                ps_pick = psum(ctx, "ps_pick", [P, 2, 512])
                row_in = sems("row_in0", "row_in1")
                rows_used = sems("rows_used0", "rows_used1")
                pick_ready = sems("pick_ready0", "pick_ready1")
                place_ready = sems("place_ready0", "place_ready1")
                sent = sems("sent0", "sent1")
                hots_ready, base_ready, added, sofar_ready, p_chain, rec_staged = sems(
                    "hots_ready", "base_ready", "added", "sofar_ready", "p_chain", "rec_staged")
                mark_staged, marks_out, base_i_ready = sems("mark_staged", "marks_out", "base_i_ready")
                block = ctx.enter_context(nc.Block())

                @block.sync
                def _(sp):
                    with sp.Fori(0, NC // 2) as i:
                        for s in range(2):
                            sp.wait_ge(rows_used[s], i * C)
                            for t, a in ((key_row, keyrow_dram), (lo_row, lorow_dram)):
                                sp.dma_start(t[:, s].rearrange("p j e -> p (j e)"),
                                             a[ds((i * 2 + s) * C, C), :].rearrange("(o j) e -> o (j e)", o=1)
                                             .broadcast_to([P, C * P])).then_inc(row_in[s], 16)

                @block.gpsimd
                def _(pool):
                    with pool.Fori(0, KB // MK) as i:
                        pool.wait_ge(mark_staged, i + 1)
                        pool.sem_inc(pool_turn, 1)
                        for n in range(MK):
                            pool.indirect_dma_start(marks_dram[:, :], bass.IndirectOffsetOnAxis(ap=mark_st[:, n:n + 1], axis=0),
                                                    ones[:, 0:1], None).then_inc(marks_out, 16)
                    with pool.Fori(0, NC // 2) as i:
                        for s in range(2):
                            pool.wait_ge(place_ready[s], i + 1)
                            pool.wait_ge(rec_staged, i * 2 + s + 1)
                            pool.sem_inc(pool_turn, 1)
                            for j in range(C):
                                pool.indirect_dma_start(rec_dram[:, :], bass.IndirectOffsetOnAxis(ap=place[:, s, j:j + 1], axis=0),
                                                        rec_st[:, s, j, :], None).then_inc(sent[s], 16)
                    for s in range(2):
                        pool.wait_ge(sent[s], 16 * C * (NC // 2))
                    pool.wait_ge(marks_out, 16 * KB)

                @block.vector
                def _(dve):
                    dve.tensor_scalar(base_g[:], row_base[:], float(G), None, ALU.mult).then_inc(base_ready, 1)
                    dve.tensor_copy(base_i[:], row_base[:]).then_inc(base_i_ready, 1)
                    dve.wait_ge(base_i_ready, 1)
                    with dve.Fori(0, KB // MK) as i:
                        dve.wait_ge(marks_out, i * MK * 16)
                        dve.tensor_copy(mark_st[:], base_i[:, ds(i * MK, MK)]).then_inc(mark_staged, 1)

                    def compare(c, s, turn):
                        dve.wait_ge(row_in[s], turn * 32 + 32)
                        dve.wait_ge(pick_ready[s], turn)
                        dve.tensor_scalar(lo_hot_t[:, s], lo_row[:, s], lane_col[:, 0:1], None, ALU.is_equal).then_inc(hots_ready, 1)
                        dve.tensor_tensor(lo_hot[:, s], lane[:, 0:P].unsqueeze(1).broadcast_to([P, C, P]),
                                          lo_f[:, ds(c * C, C)].unsqueeze(2).broadcast_to([P, C, P]),
                                          ALU.is_equal).then_inc(hots_ready, 1)
                        dve.tensor_tensor(hi_hot[:, s], lane[:, 0:KB].unsqueeze(1).broadcast_to([P, C, KB]),
                                          hi_f[:, ds(c * C, C)].unsqueeze(2).broadcast_to([P, C, KB]),
                                          ALU.is_equal).then_inc(hots_ready, 1)
                        dve.wait_ge(rows_used[1 - s], (turn + s) * C)
                        dve.wait_ge(place_ready[s], turn)
                        for j in range(C):
                            dve.scalar_tensor_tensor(same[:, j], key_row[:, s, j, :], key_f[:, ds(c * C + j, 1)], after[:],
                                                     ALU.is_equal, ALU.mult, accum_out=rank[:, s, j:j + 1]).then_inc(rows_used[s], 1)

                    def settle(c, s, turn, start):
                        link = Chain(dve, p_chain, start)
                        dve.wait_ge(pick_ready[s], turn + 1)
                        link(dve.tensor_tensor(picked[:], ps_pick[:, s, 0:C * KB].rearrange("p (j b) -> p j b", j=C), hi_hot[:, s], ALU.mult))
                        dve.wait_ge(place_ready[1 - s], turn + s)
                        link(dve.tensor_reduce(seen[:], picked[:], AX, ALU.add))
                        dve.wait_ge(rows_used[s], (turn + 1) * C)
                        dve.wait_ge(sent[s], turn * 16 * C)
                        dve.tensor_tensor(place[:, s], seen[:], rank[:, s], ALU.add).then_inc(place_ready[s], 1)

                    compare(0, 0, 0)
                    with dve.Fori(0, NC // 2 - 1) as i:
                        compare(i * 2 + 1, 1, i)
                        settle(i * 2, 0, i, i * 4)
                        compare(i * 2 + 2, 0, i + 1)
                        settle(i * 2 + 1, 1, i, i * 4 + 2)
                    compare(NC - 1, 1, NC // 2 - 1)
                    settle(NC - 2, 0, NC // 2 - 1, 2 * NC - 4)
                    settle(NC - 1, 1, NC // 2 - 1, 2 * NC - 2)

                @block.scalar
                def _(act):
                    act.wait_ge(added, 1)
                    act.copy(so_far[:, 0, :], ps_sofar[:, 0:KB]).then_inc(sofar_ready, 1)
                    with act.Fori(0, NC // 2) as i:
                        for s in range(2):
                            c = i * 2 + s
                            act.wait_ge(sent[s], i * 16 * C)
                            act.copy(rec_st[:, s], rec[:, ds(c * C, C), :]).then_inc(rec_staged, 1)
                            for j in range(C):
                                act.wait_ge(added, c * C + j + 2)
                                act.copy(so_far[:, (j + 1) % 2, :], ps_sofar[:, 0:KB]).then_inc(sofar_ready, 1)

                @block.tensor
                def _(pe):
                    pe.wait_ge(base_ready, 1)
                    pe.matmul(ps_sofar[:, 0:KB], ident[:], base_g[:], start=True, stop=False, skip_group_check=True).then_inc(added, 1)
                    with pe.Fori(0, NC // 2) as i:
                        for s in range(2):
                            c = i * 2 + s
                            pe.wait_ge(hots_ready, c * 3 + 3)
                            pe.wait_ge(place_ready[s], i)
                            for j in range(C):
                                pe.wait_ge(sofar_ready, c * C + j + 1)
                                pe.matmul(ps_sofar[:, 0:KB], lo_hot[:, s, j, :], hi_hot[:, s, j, :], start=False, stop=False,
                                          skip_group_check=True).then_inc(added, 1)
                                last = pe.matmul(ps_pick[:, s, j * KB:(j + 1) * KB], lo_hot_t[:, s, j, :], so_far[:, j % 2, :],
                                                 start=True, stop=True)
                            last.then_inc(pick_ready[s], 1)

        rows = ExitStack()
        with rows:
            marks = sbuf(rows, "marks", [P, RT])
            marks_next = sbuf(rows, "marks_next", [P, RT])
            key_of = sbuf(rows, "key_of", [P, RT])
            row_max = sbuf(rows, "row_max", [P, RT, H])
            with ExitStack() as ctx:
                AHEAD = 4
                rec = sbuf(ctx, "rec_rows", [P, RT + AHEAD, G * 4])
                gidx = sbuf(ctx, "gidx", [P, RT + AHEAD, G + 1], I32)
                valid = sbuf(ctx, "valid", [P, RT, G])
                mask = sbuf(ctx, "mask", [P, RT, G])
                target_f = sbuf(ctx, "target_f", [P, RT])
                low_rows = sbuf(ctx, "low_rows", [P, 1])
                w_row = sbuf(ctx, "w_row", [1, TD])
                b_row = sbuf(ctx, "b_row", [1, 3, TD])
                time_w = sbuf(ctx, "time_w", [G * 4, G * 3 * TD])
                idx_st = sbuf(ctx, "idx_st", [P, R, G + 1], I32)
                rec_st = sbuf(ctx, "rec_row_st", [P, R, G * 4])
                rec_t = sbuf(ctx, "rec_t", [G * 4, 2, P])
                turns = sbuf(ctx, "turns", [P, 2, G * 3 * TD])
                phase = sbuf(ctx, "phase", [P, 2, G * 3 * TD])
                kv = sbuf(ctx, "kv", [P, R, G, 2 * H * DK])
                q_emb = sbuf(ctx, "q_emb", [P, 2, G, DK])
                q = sbuf(ctx, "q", [P, R, DK])
                prod = sbuf(ctx, "prod", [P, G, H * DK])
                q_sum = sbuf(ctx, "q_sum", [P, G, DK])
                att = sbuf(ctx, "att", [P, G, H])
                att_m = sbuf(ctx, "att_m", [P, G + 1, H])
                drop = sbuf(ctx, "drop", [P, 2, G, H])
                msg = sbuf(ctx, "msg", [P, R, G, d.MSG])
                msg_out = sbuf(ctx, "msg_out", [P, 2, d.MSG])
                ps_rt = psum(ctx, "ps_rt", [P, 2, 512])
                ps_low = psum(ctx, "ps_low", [P, 512])
                ps_turns = psum(ctx, "ps_turns", [P, 2, 512])
                ps_sum = psum(ctx, "ps_sum", [P, 2, 512])
                r_clear, r_in, r_chain, w_in2, w_scaled, w_clear, w_placed = sems(
                    "r_clear", "r_in", "r_chain", "w_in2", "w_scaled", "w_clear", "w_placed")
                counted, low_ready, rows_set = sems("counted", "low_ready", "rows_set")
                staged, rt_turned, rt_copied, turns_ready, rounded, phase_ready = sems(
                    "staged", "rt_turned", "rt_copied", "turns_ready", "rounded", "phase_ready")
                emb_ready, weight_ready, sum_ready, sum_copied, att_chain = sems(
                    "emb_ready", "weight_ready", "sum_ready", "sum_copied", "att_chain")
                msg_ready = sems(*[f"msg_ready{n}" for n in range(R)])
                kv_in = sems(*[f"kv_in{n}" for n in range(R)])
                msg_stored = sems("msg_stored0", "msg_stored1")
                block = ctx.enter_context(nc.Block())

                @block.sync
                def _(sp):
                    sp.dma_start(rec[:, 0:RT, :].rearrange("p i w -> p (i w)"),
                                 rec_dram.rearrange("(p i) w -> p (i w)", p=P)).then_inc(r_in, 16)
                    sp.dma_start(marks[:], marks_dram[0:NR, :].rearrange("(p i) o -> p (i o)", p=P)).then_inc(r_in, 16)
                    sp.dma_start(marks_next[:], marks_dram[1:NR + 1, :].rearrange("(p i) o -> p (i o)", p=P)).then_inc(r_in, 16)
                    sp.dma_start(w_row[:], w_time.rearrange("(o n) -> o n", o=1)).then_inc(w_in2, 16)
                    for n in range(3):
                        sp.dma_start(b_row[:, n, :], b_time.rearrange("(o n) -> o n", o=1)).then_inc(w_in2, 16)
                    sp.wait_ge(w_scaled, 2)
                    sp.wait_ge(w_clear, 1)
                    for g in range(G):
                        at = g * 3 * TD
                        sp.dma_start(time_w[g * 4:g * 4 + 1, at:at + 3 * TD], b_row[:].rearrange("p n t -> p (n t)")).then_inc(w_placed, 16)
                        for n in range(3):
                            sp.dma_start(time_w[g * 4 + 1 + n:g * 4 + 2 + n, at + n * TD:at + (n + 1) * TD], w_row[:]).then_inc(w_placed, 16)

                    def store(a):
                        sp.wait_ge(sum_copied, a.t + 1)
                        sp.dma_start(part_dram.rearrange("(p i) c -> p i c", p=P)[:, ds(a.t, 1), :].rearrange("p i c -> p (i c)"),
                                     msg_out[:, a.slot(2), :]).then_inc(msg_stored[a.slot(2)], 16)

                    walk(sp, RT, store)
                    for n in range(2):
                        sp.wait_ge(msg_stored[n], 16 * (RT // 2))

                @block.gpsimd
                def _(pool):
                    pool.memset(rec[:, RT:, :], 0.0).then_inc(r_clear, 1)
                    pool.memset(gidx[:, RT:, :], 0).then_inc(r_clear, 1)
                    pool.memset(time_w[:], 0.0).then_inc(w_clear, 1)
                    pool.memset(q_emb[:, :, :, 0:LAST], 0.0).then_inc(r_clear, 1)
                    pool.memset(att_m[:, G, :], -BIG / 10).then_inc(r_clear, 1)

                    def gather(a):
                        s = a.slot(R)
                        pool.wait_ge(staged, a.t + 1)
                        wait_slot(pool, msg_ready[s], a, R)
                        pool.sem_inc(pool_turn, 1)
                        for g in range(G):
                            pool.indirect_dma_start(kv[:, s, g, 0:KVW], None, kv_dram[:, :],
                                                    bass.IndirectOffsetOnAxis(ap=idx_st[:, s, g:g + 1], axis=0)).then_inc(kv_in[s], 16)
                        pool.indirect_dma_start(q[:, s, :], None, q_dram[:, :],
                                                bass.IndirectOffsetOnAxis(ap=idx_st[:, s, G:G + 1], axis=0)).then_inc(kv_in[s], 16)

                    walk(pool, RT, gather)

                @block.vector
                def _(dve):
                    link = Chain(dve, r_chain)
                    dve.wait_ge(w_in2, 64)
                    dve.tensor_scalar(w_row[:], w_row[:], 1.0 / TWO_PI, None, ALU.mult).then_inc(w_scaled, 1)
                    dve.tensor_scalar(b_row[:], b_row[:], 1.0 / TWO_PI, 0.25, ALU.mult, ALU.add).then_inc(w_scaled, 1)
                    dve.wait_ge(r_in, 48)
                    dve.wait_ge(r_clear, 4)
                    link(dve.tensor_tensor_scan(key_of[:], ones[:, 0:1].broadcast_to([P, RT]), marks[:], 0.0, ALU.mult, ALU.add))
                    dve.tensor_copy(low_rows[:], key_of[:, RT - 1:RT]).then_inc(counted, 1)
                    dve.wait_ge(low_ready, 1)
                    dve.wait_ge(counted, 1)
                    link(dve.tensor_scalar(low_rows[:], ps_low[:, 0:1], -1.0, None, ALU.add))
                    link(dve.tensor_scalar(key_of[:], key_of[:], low_rows[:, 0:1], None, ALU.add))
                    link(dve.tensor_scalar(target_f[:], key_of[:], float(NPAD), float(-NPAD), ALU.is_ge, ALU.mult))
                    link(dve.tensor_tensor(gidx[:, 0:RT, G], target_f[:], key_of[:], ALU.add))
                    words = rec[:, 0:RT, :].rearrange("p i (g w) -> p i g w", w=4)[:, :, :, 0]
                    link(dve.tensor_copy(gidx[:, 0:RT, 0:G], words))
                    link(dve.tensor_scalar(valid[:], words, 1.0, None, ALU.min))
                    link(dve.tensor_scalar(mask[:], valid[:], -1.0, BIG, ALU.add, ALU.mult))
                    dve.tensor_copy(words, valid[:]).then_inc(rows_set, 1)

                    def find_phase(a):
                        wait_done(dve, rounded, a)
                        wait_done(dve, emb_ready, a, 2)
                        h = a.slot(2)
                        dve.scalar_tensor_tensor(phase[:, h], turns[:, h], MAGIC, ps_turns[:, h, 0:G * 3 * TD],
                                                 ALU.subtract, ALU.subtract).then_inc(phase_ready, 1)

                    def signal(ins, sem=att_chain):
                        ins.then_inc(sem, 1)

                    def step(a):
                        find_phase(a + 1)
                        s, h = a.slot(R), a.slot(2)
                        n = a.t * 6

                        def done(k):
                            dve.wait_ge(att_chain, n + k)

                        dve.wait_ge(kv_in[s], (a.turn(R) + 1) * 16 * (G + 1))
                        dve.wait_ge(emb_ready, a.t + 1)
                        signal(dve.tensor_tensor(q_sum[:], q_emb[:, h], q[:, s, :].unsqueeze(1).broadcast_to([P, G, DK]), ALU.add))
                        done(1)
                        signal(dve.tensor_tensor(prod[:].rearrange("p g (h c) -> p g h c", h=H),
                                                 kv[:, s, :, 0:H * DK].rearrange("p g (h c) -> p g h c", h=H),
                                                 q_sum[:].unsqueeze(2).broadcast_to([P, G, H, DK]), ALU.mult))
                        if a.c:
                            weigh(a + -1)
                        done(2)
                        signal(dve.tensor_reduce(att[:], prod[:].rearrange("p g (h c) -> p g h c", h=H), AX, ALU.add))
                        done(3)
                        signal(dve.tensor_tensor(att_m[:, 0:G, :], att[:], mask[:, ds(a.t, 1), :].rearrange("p i g -> p (i g)").unsqueeze(2).broadcast_to([P, G, H]), ALU.add))
                        top_of = row_max[:, ds(a.t, 1), :].rearrange("p i h -> p (i h)")
                        done(4)
                        signal(dve.tensor_reduce(top_of, att_m[:].rearrange("p g h -> p h g"), AX, ALU.max))
                        done(5)
                        wait_done(dve, weight_ready, a, 2)
                        signal(dve.tensor_tensor(drop[:, h], att_m[:, 0:G, :], top_of.unsqueeze(1).broadcast_to([P, G, H]), ALU.subtract))

                    def weigh(a):
                        s = a.slot(R)
                        wait_done(dve, weight_ready, a)
                        dve.tensor_tensor(msg[:, s, :, 0:H * DK].rearrange("p g (h c) -> p g h c", h=H),
                                          kv[:, s, :, H * DK:].rearrange("p g (h c) -> p g h c", h=H),
                                          msg[:, s, :, D:].unsqueeze(3).broadcast_to([P, G, H, DK]), ALU.mult).then_inc(msg_ready[s], 1)

                    find_phase(At(0, 0))
                    walk(dve, RT, step)
                    weigh(At(0, RT - 1))

                @block.scalar
                def _(act):
                    def stage(a):
                        wait_slot(act, kv_in[a.slot(R)], a, R, 16 * (G + 1))
                        wait_done(act, rt_turned, a, R)
                        act.copy(idx_st[:, a.slot(R), :], gidx[:, ds(a.t, 1), :].rearrange("p i g -> p (i g)"))
                        act.copy(rec_st[:, a.slot(R), :], rec[:, ds(a.t, 1), :].rearrange("p i g -> p (i g)")).then_inc(staged, 1)

                    def copy_rt(a):
                        wait_done(act, rt_turned, a)
                        wait_done(act, turns_ready, a, 2)
                        act.copy(rec_t[:, a.slot(2), :], ps_rt[0:G * 4, a.slot(2), 0:P]).then_inc(rt_copied, 1)

                    def round_turns(a):
                        wait_done(act, turns_ready, a)
                        wait_done(act, phase_ready, a, 2)
                        act.activation(turns[:, a.slot(2)], ps_turns[:, a.slot(2), 0:G * 3 * TD], ACT.Identity,
                                       bias=magic[:, 0:1]).then_inc(rounded, 1)

                    def sines(a):
                        s, h = a.slot(R), a.slot(2)
                        wait_done(act, phase_ready, a)
                        wait_done(act, sum_ready, a, R)
                        act.wait_ge(kv_in[s], (a.turn(R) + 1) * 16 * (G + 1))
                        if a.c >= 2:
                            act.wait_ge(att_chain, a.t * 6 - 11)
                        at = phase[:, h].rearrange("p (g n t) -> p n g t", g=G, n=3)
                        for n, to in ((1, kv[:, s, :, PROJ:H * DK]), (1, kv[:, s, :, KVW:]), (2, q_emb[:, h, :, LAST:]),
                                      (0, msg[:, s, :, H * DK:D])):
                            last = act.activation(to, at[:, n], ACT.Sin, scale=-SIN_SCALE)
                        last.then_inc(emb_ready, 1)

                    def exps(a):
                        act.wait_ge(att_chain, a.t * 6 + 6)
                        act.activation(msg[:, a.slot(R), :, D:], drop[:, a.slot(2)], ACT.Exp, scale=float(DK) ** -0.5).then_inc(weight_ready, 1)

                    def copy_sum(a):
                        wait_done(act, sum_ready, a)
                        wait_slot(act, msg_stored[a.slot(2)], a, 2, 16)
                        act.copy(msg_out[:, a.slot(2), :], ps_sum[:, a.slot(2), 0:d.MSG]).then_inc(sum_copied, 1)

                    def step(a):
                        copy_rt(a + 3)
                        round_turns(a + 2)
                        if a.c + 1 < RT:
                            sines(a + 1)
                        exps(a)
                        stage(a + 4)
                        if a.c:
                            copy_sum(a + -1)

                    act.wait_ge(rows_set, 1)
                    for t in range(4):
                        stage(At(0, t))
                    for t in range(3):
                        copy_rt(At(0, t))
                    for t in range(2):
                        round_turns(At(0, t))
                    sines(At(0, 0))
                    walk(act, RT, step)
                    copy_sum(At(0, RT - 1))

                @block.tensor
                def _(pe):
                    pe.wait_ge(counted, 1)
                    pe.matmul(ps_low[:, 0:1], before[:], low_rows[:], start=True, stop=True).then_inc(low_ready, 1)
                    pe.wait_ge(w_placed, 16 * G * 4)

                    def turn_rec(a):
                        wait_done(pe, staged, a)
                        wait_done(pe, rt_copied, a, 2)
                        pe.transpose(ps_rt[0:G * 4, a.slot(2), 0:P], rec_st[:, a.slot(R), :], ident[:]).then_inc(rt_turned, 1)

                    def multiply(a):
                        wait_done(pe, rt_copied, a)
                        wait_done(pe, phase_ready, a, 2)
                        pe.matmul(ps_turns[:, a.slot(2), 0:G * 3 * TD], rec_t[:, a.slot(2), :], time_w[:], start=True,
                                  stop=True).then_inc(turns_ready, 1)

                    def add_up(a):
                        pe.wait_ge(msg_ready[a.slot(R)], a.turn(R) + 1)
                        wait_done(pe, sum_copied, a, 2)
                        for g in range(G):
                            last = pe.matmul(ps_sum[:, a.slot(2), 0:d.MSG], ident[:], msg[:, a.slot(R), g, :], start=(g == 0), stop=(g == G - 1))
                        last.then_inc(sum_ready, 1)

                    def step(a):
                        turn_rec(a + 3)
                        multiply(a + 2)
                        if a.c:
                            add_up(a + -1)

                    for t in range(3):
                        turn_rec(At(0, t))
                    for t in range(2):
                        multiply(At(0, t))
                    walk(pe, RT, step)
                    add_up(At(0, RT - 1))

            with ExitStack() as ctx:
                fall = sbuf(ctx, "fall", [P, 2, RT])
                lane_fall = sbuf(ctx, "lane_fall", [P, 2])
                flow = sbuf(ctx, "flow", [P, 2, H, RT])
                ends_of = sbuf(ctx, "ends_of", [P, 2, 2, H])
                across = sbuf(ctx, "across", [H, 2, P + 1])
                across_in = sbuf(ctx, "across_in", [H, 2, 2, P])
                carry = sbuf(ctx, "carry", [P, 2, H])
                below = sbuf(ctx, "below", [P, RT, H])
                share = sbuf(ctx, "share", [P, RT, H + 1])
                ps_lane = psum(ctx, "ps_lane", [P, 4, 512])
                s_chain, lanes_set, lanes_turned, carry_set, carry_turned, below_ready, share_ready, share_out = sems(
                    "s_chain", "lanes_set", "lanes_turned", "carry_set", "carry_turned", "below_ready", "share_ready", "share_out")
                block = ctx.enter_context(nc.Block())

                @block.vector
                def _(dve):
                    link = Chain(dve, s_chain)
                    link(dve.tensor_scalar(fall[:, 0], marks[:], RESET, None, ALU.mult))
                    link(dve.tensor_scalar(fall[:, 1], marks_next[:], RESET, None, ALU.mult))
                    link(dve.tensor_reduce(lane_fall[:], fall[:], AX, ALU.min))
                    link(dve.memset(across[:], RESET / 2))
                    for n in range(2):
                        order = slice(None, None, -1) if n else slice(None)
                        edge = 0 if n else RT - 1

                        def scan(start):
                            for h in range(H):
                                src_t = flow[:, 0, h, order] if n else row_max[:, :, h]
                                last = dve.tensor_tensor_scan(flow[:, n, h, order], fall[:, n, order], src_t, start(h), ALU.add, ALU.max)
                            link(last)

                        scan(lambda h: RESET / 2)
                        link(dve.tensor_copy(ends_of[:, n, 0, :], flow[:, n, :, edge]))
                        dve.tensor_copy(ends_of[:, n, 1, :], lane_fall[:, n:n + 1].broadcast_to([P, H])).then_inc(lanes_set, 1)
                        dve.wait_ge(lanes_turned, n + 1)
                        for w in range(2):
                            link(dve.tensor_copy(across_in[:, n, w, :], ps_lane[0:H, w, 0:P]))
                        kept = across[:, n, 0:P][:, order] if n else across[:, n, 1:P + 1]
                        dve.tensor_tensor_scan(kept, across_in[:, n, 1, order], across_in[:, n, 0, order], RESET / 2,
                                               ALU.add, ALU.max).then_inc(carry_set, 1)
                        dve.wait_ge(carry_turned, n + 1)
                        link(dve.tensor_copy(carry[:, n, :], ps_lane[:, 2, 0:H]))
                        scan(lambda h: carry[:, n, h:h + 1])
                    dve.tensor_tensor(below[:], row_max[:], flow[:, 1].rearrange("p h i -> p i h"), ALU.subtract).then_inc(below_ready, 1)
                    dve.tensor_copy(share[:, :, H], key_of[:]).then_inc(share_ready, 1)

                @block.tensor
                def _(pe):
                    for n in range(2):
                        pe.wait_ge(lanes_set, n + 1)
                        for w in range(2):
                            last = pe.transpose(ps_lane[0:H, w, 0:P], ends_of[:, n, w, :], ident[:])
                        last.then_inc(lanes_turned, 1)
                        pe.wait_ge(carry_set, n + 1)
                        pe.transpose(ps_lane[:, 2, 0:H], across[:, n, 1:P + 1] if n else across[:, n, 0:P], ident[0:H, 0:H]).then_inc(carry_turned, 1)

                @block.scalar
                def _(act):
                    act.wait_ge(below_ready, 1)
                    act.activation(share[:, :, 0:H], below[:], ACT.Exp, scale=float(DK) ** -0.5).then_inc(share_ready, 1)

                @block.sync
                def _(sp):
                    sp.wait_ge(share_ready, 2)
                    sp.dma_start(wk_dram.rearrange("(p i) c -> p (i c)", p=P), share[:].rearrange("p i c -> p (i c)")).then_inc(share_out, 16)
                    sp.wait_ge(share_out, 16)

        nodes = ExitStack()
        with nodes:
            agg = sbuf(nodes, "agg", [P, NB, D])
            with ExitStack() as ctx:
                acc = sbuf(ctx, "acc", [P, KB + 1, d.MSG])
                first_key = sbuf(ctx, "first_key", [1, RT])
                first_i = sbuf(ctx, "first_i", [1, RT], I32)
                block_i = sbuf(ctx, "block_i", [1, RT], I32)
                block_key = sbuf(ctx, "block_key", [1, RT])
                block_key_bc = sbuf(ctx, "block_key_bc", [P, RT])
                part = sbuf(ctx, "part", [P, 4, d.MSG])
                wk = sbuf(ctx, "wk", [P, 4, H + 1])
                key_hot = sbuf(ctx, "key_hot", [P, 4, 2 * P])
                total = sbuf(ctx, "total", [P, KB, H])
                ps_bc = psum(ctx, "ps_bc", [P, 512])
                ps_key = psum(ctx, "ps_key", [P, 2, 2, 512])
                k_in, k_chain, first_ready, bc_ready, acc_clear = sems("k_in", "k_chain", "first_ready", "bc_ready", "acc_clear")
                part_in = sems(*[f"part_in{n}" for n in range(4)])
                part_ready, key_summed, key_added, tile_chain = sems("part_ready", "key_summed", "key_added", "tile_chain")
                block = ctx.enter_context(nc.Block())

                @block.sync
                def _(sp):
                    sp.dma_start(first_key[:], wk_dram.rearrange("(i p) c -> c p i", p=P)[H:H + 1, 0, :],
                                 allow_slow_non_contiguous=True).then_inc(k_in, 16)

                    def load(a):
                        s = a.slot(4)
                        if a.c >= 4:
                            sp.wait_ge(key_summed, a.t - 3)
                        sp.dma_start(part[:, s, :], part_dram[ds(a.t * P, P), :]).then_inc(part_in[s], 16)
                        sp.dma_start(wk[:, s, :], wk_dram[ds(a.t * P, P), :]).then_inc(part_in[s], 16)

                    for t in range(4):
                        load(At(0, t))
                    with sp.Fori(0, RT // 4 - 1) as i:
                        for u in range(4):
                            load(At(i, 4 + u))

                @block.gpsimd
                def _(pool):
                    pool.memset(acc[:], 0.0).then_inc(acc_clear, 1)

                @block.vector
                def _(dve):
                    link = Chain(dve, k_chain)
                    dve.wait_ge(k_in, 16)
                    link(dve.tensor_copy(first_i[:], first_key[:]))
                    link(dve.tensor_scalar(block_i[:], first_i[:], 7, None, ALU.arith_shift_right))
                    dve.tensor_scalar(block_key[:], block_i[:], float(P), None, ALU.mult).then_inc(first_ready, 1)
                    dve.wait_ge(bc_ready, 1)
                    link(dve.tensor_copy(block_key_bc[:], ps_bc[:, 0:RT]))
                    dve.wait_ge(acc_clear, 1)

                    def prepare(a):
                        s = a.slot(4)
                        dve.wait_ge(part_in[s], (a.turn(4) + 1) * 32)
                        if a.c >= 4:
                            dve.wait_ge(key_summed, a.t - 3)
                        heads = part[:, s, 0:3 * DK].rearrange("p (h c) -> p h c", h=3)
                        dve.tensor_tensor(heads, heads, wk[:, s, 0:3].unsqueeze(2).broadcast_to([P, 3, DK]), ALU.mult)
                        dve.tensor_tensor(part[:, s, 3 * DK:H * DK], part[:, s, 3 * DK:H * DK],
                                          wk[:, s, 3:4].broadcast_to([P, DK]), ALU.mult)
                        dve.tensor_tensor(part[:, s, D:], part[:, s, D:], wk[:, s, 0:H], ALU.mult)
                        dve.tensor_scalar(key_hot[:, s], lane[:], block_key_bc[:, ds(a.t, 1)], wk[:, s, H:H + 1],
                                          ALU.add, ALU.is_equal).then_inc(part_ready, 1)

                    def add(a):
                        at = dve.value_load(block_i[0:1, ds(a.t, 1)], min_val=0, max_val=KB - 1)
                        wait_done(dve, key_summed, a)
                        if a.c:
                            dve.wait_ge(key_added, a.t)
                        dve.tensor_tensor(acc[:, ds(at, 2), :], acc[:, ds(at, 2), :], ps_key[:, a.slot(2), :, 0:d.MSG],
                                          ALU.add).then_inc(key_added, 1)

                    for t in range(4):
                        prepare(At(0, t))
                    for t in range(2):
                        add(At(0, t))
                    with dve.Fori(0, RT // 4 - 1) as i:
                        for u in range(4):
                            prepare(At(i, 4 + u))
                            add(At(i, 2 + u))
                    for t in range(RT - 2, RT):
                        add(At(0, t))
                    dve.wait_ge(key_added, RT)
                    link(dve.tensor_scalar(total[:], acc[:, 0:KB, D:], 1e-16, None, ALU.add))
                    link(dve.reciprocal(total[:], total[:]))
                    heads = acc[:, 0:KB, 0:3 * DK].rearrange("p b (h c) -> p b h c", h=3)
                    link(dve.tensor_tensor(heads, heads, total[:, :, 0:3].unsqueeze(3).broadcast_to([P, KB, 3, DK]), ALU.mult))
                    link(dve.tensor_tensor(acc[:, 0:KB, 3 * DK:H * DK], acc[:, 0:KB, 3 * DK:H * DK],
                                           total[:, :, 3:4].broadcast_to([P, KB, DK]), ALU.mult))
                    link(dve.tensor_tensor(agg[:], acc[:, 0:NB, 0:D], acc[:, NB:KB, 0:D], ALU.add))

                @block.tensor
                def _(pe):
                    pe.wait_ge(first_ready, 1)
                    pe.matmul(ps_bc[:, 0:RT], ones[0:1, :], block_key[:], start=True, stop=True).then_inc(bc_ready, 1)

                    def sum_rows(a):
                        s, h = a.slot(4), a.slot(2)
                        wait_done(pe, part_ready, a)
                        wait_done(pe, key_added, a, 2)
                        for n in range(2):
                            last = pe.matmul(ps_key[:, h, n, 0:d.MSG], key_hot[:, s, n * P:(n + 1) * P], part[:, s, :], start=True, stop=True)
                        last.then_inc(key_summed, 1)

                    walk(pe, RT, sum_rows)

            with ExitStack() as ctx:
                wa = sbuf(ctx, "wa", [P, T * KD, D])
                wa2 = sbuf(ctx, "wa2", [P, T * KD, D])
                vecs = sbuf(ctx, "vecs", [T, 3, D])
                aT = res[:].rearrange("p b c -> p (b c)").rearrange("p (k n) -> p k n", k=KD)
                masked = sbuf(ctx, "masked_a", [P, 4, KD, P])
                onehot_st = sbuf(ctx, "onehot_a", [T, P])
                ps_t = psum(ctx, "ps_ta", [P, 2, 512])
                ps_o = psum(ctx, "ps_o", [P, 512])
                ps_v = psum(ctx, "ps_v", [P, 512])
                res_clear, res_in, wa_in, vecs_in, wa_ready = sems("res_clear", "res_in", "wa_in", "vecs_in", "wa_ready")
                a_turned, a_copied, a_mask_ready, a_mask_used, o_ready, o_used = sems(
                    "a_turned", "a_copied", "a_mask_ready", "a_mask_used", "o_ready", "o_used")
                a_chain, a_var, a_std, v_hot, v_ready, v_used = sems("a_chain", "a_var", "a_std", "v_hot", "v_ready", "v_used")
                block = ctx.enter_context(nc.Block())

                @block.gpsimd
                def _(pool):
                    pool.wait_ge(o_ready, NB)
                    pool.memset(res[:, d.FULL:NB, :], 0.0).then_inc(res_clear, 1)

                @block.sync
                def _(sp):
                    for half, t in enumerate((wa, wa2)):
                        for k in range(KD):
                            sp.dma_start(t[:].rearrange("p (t k) c -> p t k c", k=KD)[:, :, k, :],
                                         Wa[:, half * D + k * P:half * D + (k + 1) * P, :].rearrange("t p c -> p t c")).then_inc(wa_in, 16)
                    for n, v in enumerate((ba, gamma, beta)):
                        sp.dma_start(vecs[:, n, :], v).then_inc(vecs_in, 16)
                    sp.wait_ge(res_clear, 1)
                    sp.dma_start(res[:, 0:d.FULL, :], x[0:d.FULL * P, :].rearrange("(b p) c -> p b c", p=P)).then_inc(res_in, 16)
                    sp.dma_start(res[0:d.TAIL, d.FULL, :], x[d.FULL * P:N, :]).then_inc(res_in, 16)

                @block.scalar
                def _(act):
                    with act.Fori(0, NB) as b:
                        for k in range(KD):
                            act.wait_ge(a_turned, b * KD + k + 1)
                            act.copy(aT[:, k, ds(b * P, P)], ps_t[:, k, 0:P]).then_inc(a_copied, 1)
                    act.wait_ge(a_var, 1)
                    act.activation(rstd[:], tmp_b[:], ACT.Sqrt).then_inc(a_std, 1)

                @block.vector
                def _(dve):
                    link = Chain(dve, a_chain)
                    dve.wait_ge(wa_in, 64)
                    dve.tensor_tensor(wa[:], wa[:], wa2[:], ALU.add).then_inc(wa_ready, 1)
                    with dve.Fori(0, NB) as b:
                        dve.wait_ge(a_copied, b * KD + KD)
                        for t in range(T):
                            dve.wait_ge(a_mask_used, b * T if t < 4 else b * T + t - 3)
                            dve.scalar_tensor_tensor(masked[:, t % 4, :, :],
                                                     type_bc[:, ds(b * P, P)].unsqueeze(1).broadcast_to([P, KD, P]), float(t),
                                                     aT[:, :, ds(b * P, P)], ALU.is_equal, ALU.mult).then_inc(a_mask_ready, 1)
                        dve.wait_ge(o_used, b)
                        dve.tensor_copy(onehot_st[:], type_onehot[:, ds(b * P, P)]).then_inc(a_mask_ready, 1)
                        dve.wait_ge(o_ready, b + 1)
                        dve.tensor_tensor(agg[:, ds(b, 1), :].rearrange("p b c -> p (b c)"), ps_o[:, 0:D],
                                          xn[:, ds(b, 1), :].rearrange("p b c -> p (b c)"), ALU.add).then_inc(o_used, 1)
                    dve.wait_ge(o_used, NB)
                    layer_norm_stats(dve, a_var, a_std, link, agg, 1)
                    link(normalize(dve, agg, agg))
                    dve.wait_ge(res_in, 32)
                    with dve.Fori(0, NB) as b:
                        dve.tensor_copy(onehot_st[:], type_onehot[:, ds(b * P, P)]).then_inc(v_hot, 1)
                        dve.wait_ge(v_ready, b + 1)
                        row = agg[:, ds(b, 1), :].rearrange("p b c -> p (b c)")
                        out_row = res[:, ds(b, 1), :].rearrange("p b c -> p (b c)")
                        step = Chain(dve, v_used, b * 3)
                        step(dve.tensor_tensor(row, row, ps_v[:, 0:D], ALU.mult))
                        step(dve.tensor_tensor(row, row, ps_v[:, D:2 * D], ALU.add))
                        step(dve.tensor_tensor(out_row, out_row, row, ALU.add))

                @block.tensor
                def _(pe):
                    for b in range(NB):
                        for k in range(KD):
                            if b:
                                pe.wait_ge(a_copied, b * KD + k - KD + 1)
                            pe.transpose(ps_t[:, k, 0:P], agg[:, b, k * P:(k + 1) * P], ident[:]).then_inc(a_turned, 1)
                    pe.wait_ge(wa_ready, 1)
                    pe.wait_ge(vecs_in, 48)
                    with pe.Fori(0, NB) as b:
                        pe.wait_ge(o_used, b)
                        for t in range(T):
                            pe.wait_ge(a_mask_ready, b * (T + 1) + t + 1)
                            for k in range(KD):
                                last = pe.matmul(ps_o[:, 0:D], masked[:, t % 4, k, :], wa[:, t * KD + k, :],
                                                 start=(t == 0 and k == 0), stop=False)
                            last.then_inc(a_mask_used, 1)
                        pe.wait_ge(a_mask_ready, (b + 1) * (T + 1))
                        pe.matmul(ps_o[:, 0:D], onehot_st[:], vecs[:, 0, :], start=False, stop=True).then_inc(o_ready, 1)
                    with pe.Fori(0, NB) as b:
                        pe.wait_ge(v_hot, b + 1)
                        pe.wait_ge(v_used, b * 3)
                        pe.matmul(ps_v[:, 0:2 * D], onehot_st[:], vecs[:, 1:3, :], start=True, stop=True).then_inc(v_ready, 1)

        clear_sems()
        X, HID, TOP, XT = d.X, d.HID, d.TOP, d.XT
        FH = HID // P
        ffn = ExitStack()
        with ffn:
            gate = sbuf(ffn, "gate", [P, TOP, NB])
            place_i = sbuf(ffn, "place_i", [P, NB + 4, TOP], I32)
            expert_i = sbuf(ffn, "expert_i", [P, XT], I32)
            b1_t = sbuf(ffn, "b1_t", [P, X * FH])
            ln_t = sbuf(ffn, "ln_t", [P, 2, X * KD])
            b2_row = sbuf(ffn, "b2_row", [1, X, D])
            w2 = sbuf(ffn, "w2", [P, X, FH, D])
            with ExitStack() as ctx:
                tok_t = sbuf(ctx, "tok_t", [P, KD, NPAD])
                wr = sbuf(ctx, "wr", [P, KD, X])
                br_row = sbuf(ctx, "br_row", [1, X])
                logits = sbuf(ctx, "logits", [P, NB, X])
                higher = sbuf(ctx, "higher", [P, NB, X, X])
                equal = sbuf(ctx, "equal", [P, NB, X, X])
                earlier = sbuf(ctx, "earlier", [P, X, X])
                order = sbuf(ctx, "order", [P, NB, X])
                chosen = sbuf(ctx, "chosen", [P, NB, X])
                best = sbuf(ctx, "best", [P, NB])
                block_tot = sbuf(ctx, "block_tot", [P, NB, X])
                block_upto = sbuf(ctx, "block_upto", [P, NB, X])
                row_of = sbuf(ctx, "row_of", [P, NB, X])
                tiles_i = sbuf(ctx, "tiles_i", [P, X], I32)
                tiles_f = sbuf(ctx, "tiles_f", [P, X])
                tiles_upto = sbuf(ctx, "tiles_upto", [P, X])
                first_row = sbuf(ctx, "first_row", [P, X])
                past = sbuf(ctx, "past", [P, XT, X])
                expert_f = sbuf(ctx, "expert_f", [P, XT])
                pick = sbuf(ctx, "pick", [P, NB, X])
                picked = sbuf(ctx, "picked_e", [P, TOP, NB, X])
                place_f = sbuf(ctx, "place_f", [P, TOP, NB])
                b1_rows = sbuf(ctx, "b1_rows", [X * FH, P])
                ln_rows = sbuf(ctx, "ln_rows", [X * KD, 2, P])
                tok_st = sbuf(ctx, "tok_st", [P, 2, D])
                place_st = sbuf(ctx, "place_st", [P, 2, TOP], I32)
                ps_t = psum(ctx, "ps_tf", [P, 2, 512])
                ps_l = psum(ctx, "ps_l", [P, 512])
                ps_s = psum(ctx, "ps_s", [P, 3, 512])
                ps_n = psum(ctx, "ps_n", [P, 2, 512])
                f_chain, f_var, f_std, xf_ready, f_turned, f_copied, logits_ready = sems(
                    "f_chain", "f_var", "f_std", "xf_ready", "f_turned", "f_copied", "logits_ready")
                f_in, earlier_set, ex_in, ex_ready, small_turned, chosen_ready, prefix_ready, w2_in = sems(
                    "f_in", "earlier_set", "ex_in", "ex_ready", "small_turned", "chosen_ready", "prefix_ready", "w2_in")
                tok_staged = sems("tok_staged0", "tok_staged1")
                tok_sent = sems("tok_sent0", "tok_sent1")
                block = ctx.enter_context(nc.Block())

                @block.sync
                def _(sp):
                    sp.dma_start(wr[:], Wr.rearrange("(k p) e -> p k e", p=P)).then_inc(f_in, 16)
                    sp.dma_start(br_row[:], br.rearrange("(o e) -> o e", o=1)).then_inc(f_in, 16)
                    sp.dma_start(b1_rows[:], b1.rearrange("e (f p) -> (e f) p", p=P)).then_inc(f_in, 16)
                    sp.dma_start(ln_rows[:, 0, :], ln_g.rearrange("e (k p) -> (e k) p", p=P)).then_inc(f_in, 16)
                    sp.dma_start(ln_rows[:, 1, :], ln_b.rearrange("e (k p) -> (e k) p", p=P)).then_inc(f_in, 16)
                    sp.dma_start(b2_row[:], b2.rearrange("(o e) c -> o e c", o=1)).then_inc(f_in, 16)
                    sp.dma_start(w2[:].rearrange("p e f c -> p (e f) c"), W2.rearrange("e (f p) c -> p (e f) c", p=P)).then_inc(w2_in, 16)
                    sp.wait_ge(w2_in, 16)

                @block.gpsimd
                def _(pool):
                    pool.iota(equal[:, 0], [[1, X], [-1, X]], base=0, channel_multiplier=0,
                              allow_small_or_imprecise_dtypes=True).then_inc(earlier_set, 1)
                    pool.wait_ge(earlier_set, 1)
                    pool.tensor_scalar(earlier[:], equal[:, 0], 0.0, None, ALU.is_gt).then_inc(earlier_set, 1)

                    def send(a):
                        s = a.slot(2)
                        pool.wait_ge(tok_staged[s], a.turn(2) + 1)
                        pool.sem_inc(pool_turn, 1)
                        for n in range(TOP):
                            pool.indirect_dma_start(sorted_dram[:, :], bass.IndirectOffsetOnAxis(ap=place_st[:, s, n:n + 1], axis=0),
                                                    tok_st[:, s, :], None).then_inc(tok_sent[s], 16)

                    walk(pool, NB, send)
                    pool.wait_ge(tok_sent[0], 16 * TOP * (NB - NB // 2))
                    pool.wait_ge(tok_sent[1], 16 * TOP * (NB // 2))

                @block.vector
                def _(dve):
                    link = Chain(dve, f_chain)
                    layer_norm_stats(dve, f_var, f_std, link, res, 1)
                    normalize(dve, xn, res).then_inc(xf_ready, 1)
                    dve.wait_ge(xf_ready, 1)
                    layer_norm_stats(dve, f_var, f_std, link, xn, 2)
                    dve.wait_ge(logits_ready, 1)
                    link(dve.tensor_copy(logits[:].rearrange("p b e -> p (b e)"), ps_l[:, 0:NB * X]))
                    dve.wait_ge(earlier_set, 2)
                    mine = logits[:].unsqueeze(3).broadcast_to([P, NB, X, X])
                    other = logits[:].unsqueeze(2).broadcast_to([P, NB, X, X])
                    link(dve.tensor_tensor(higher[:], other, mine, ALU.is_gt))
                    link(dve.tensor_tensor(equal[:], other, mine, ALU.is_equal))
                    link(dve.tensor_tensor(equal[:], equal[:], earlier[:].unsqueeze(1).broadcast_to([P, NB, X, X]), ALU.mult))
                    link(dve.tensor_tensor(higher[:], higher[:], equal[:], ALU.add))
                    link(dve.tensor_reduce(order[:], higher[:], AX, ALU.add))
                    dve.tensor_scalar(chosen[:], order[:], float(TOP), None, ALU.is_lt).then_inc(chosen_ready, 1)
                    link(dve.tensor_reduce(best[:], logits[:], AX, ALU.max))
                    dve.tensor_tensor(logits[:], logits[:], best[:].unsqueeze(2).broadcast_to([P, NB, X]), ALU.subtract).then_inc(ex_in, 1)
                    dve.wait_ge(prefix_ready, 1)
                    link(dve.tensor_copy(block_tot[:].rearrange("p b e -> p (b e)"), ps_n[:, 1, 0:NB * X]))
                    for e in range(X):
                        last = dve.tensor_tensor_scan(block_upto[:, :, e], ones[:, 0:NB], block_tot[:, :, e], 0.0, ALU.mult, ALU.add)
                    link(last)
                    link(dve.tensor_scalar(tiles_i[:], block_upto[:, NB - 1, :], float(P - 1), None, ALU.add))
                    link(dve.tensor_scalar(tiles_i[:], tiles_i[:], P.bit_length() - 1, None, ALU.arith_shift_right))
                    link(dve.tensor_copy(tiles_f[:], tiles_i[:]))
                    link(dve.tensor_tensor_scan(tiles_upto[:], ones[:, 0:X], tiles_f[:], 0.0, ALU.mult, ALU.add))
                    link(dve.tensor_tensor(first_row[:], tiles_upto[:], tiles_f[:], ALU.subtract))
                    link(dve.tensor_scalar(first_row[:], first_row[:], float(P), None, ALU.mult))
                    link(dve.tensor_tensor(row_of[:], block_upto[:], block_tot[:], ALU.subtract))
                    link(dve.tensor_tensor(row_of[:].rearrange("p b e -> p (b e)"), row_of[:].rearrange("p b e -> p (b e)"), ps_n[:, 0, 0:NB * X], ALU.add))
                    link(dve.tensor_tensor(row_of[:], row_of[:], first_row[:].unsqueeze(1).broadcast_to([P, NB, X]), ALU.add))
                    link(dve.tensor_tensor(past[:], lane[:, 0:XT].unsqueeze(2).broadcast_to([P, XT, X]),
                                           tiles_upto[:].unsqueeze(1).broadcast_to([P, XT, X]), ALU.is_ge))
                    link(dve.tensor_reduce(expert_f[:], past[:], AX, ALU.add))
                    link(dve.tensor_scalar(expert_i[:], expert_f[:], float(X - 1), None, ALU.min))
                    dve.wait_ge(ex_ready, 1)
                    for n in range(TOP):
                        link(dve.tensor_scalar(pick[:], order[:], float(n), None, ALU.is_equal))
                        link(dve.tensor_tensor(picked[:, n], pick[:], row_of[:], ALU.mult))
                        link(dve.tensor_reduce(place_f[:, n, :], picked[:, n], AX, ALU.add))
                        link(dve.tensor_tensor(pick[:], pick[:], logits[:], ALU.mult))
                        link(dve.tensor_reduce(gate[:, n, :], pick[:], AX, ALU.add))
                    link(dve.memset(place_i[:, NB:, :], 0))
                    link(dve.tensor_copy(place_i[:, 0:NB, :], place_f[:].rearrange("p n b -> p b n")))
                    link(dve.tensor_tensor(best[:], gate[:, 0, :], gate[:, 1, :], ALU.add))
                    link(dve.reciprocal(best[:], best[:]))
                    link(dve.tensor_tensor(gate[:], gate[:], best[:].unsqueeze(1).broadcast_to([P, TOP, NB]), ALU.mult))
                    dve.wait_ge(small_turned, 3)
                    for n in range(2):
                        link(dve.tensor_copy(ln_t[:, n, :], ps_s[:, n, 0:X * KD]))
                    link(dve.tensor_copy(b1_t[:], ps_s[:, 2, 0:X * FH]))

                    def stage(a):
                        s = a.slot(2)
                        wait_slot(dve, tok_sent[s], a, 2, 16 * TOP)
                        dve.tensor_scalar(tok_st[:, s, :], xn[:, ds(a.t, 1), :].rearrange("p b c -> p (b c)"), mean[:, ds(a.t, 1)],
                                          rstd[:, ds(a.t, 1)], ALU.subtract, ALU.mult)
                        dve.tensor_copy(place_st[:, s, :], place_i[:, ds(a.t, 1), :].rearrange("p b n -> p (b n)")).then_inc(tok_staged[s], 1)

                    walk(dve, NB, stage)

                @block.scalar
                def _(act):
                    act.wait_ge(f_var, 1)
                    act.activation(rstd[:], tmp_b[:], ACT.Sqrt).then_inc(f_std, 1)
                    act.wait_ge(f_var, 2)
                    act.activation(rstd[:], tmp_b[:], ACT.Sqrt).then_inc(f_std, 1)
                    with act.Fori(0, NB) as b:
                        for k in range(KD):
                            act.wait_ge(f_turned, b * KD + k + 1)
                            act.copy(tok_t[:, k, ds(b * P, P)], ps_t[:, k, 0:P]).then_inc(f_copied, 1)
                    act.wait_ge(ex_in, 1)
                    act.activation(logits[:], logits[:], ACT.Exp).then_inc(ex_ready, 1)

                @block.tensor
                def _(pe):
                    pe.wait_ge(f_in, 96)
                    for m in range(2):
                        pe.transpose(ps_s[:, m, 0:X * KD], ln_rows[:, m, :], ident[0:X * KD, 0:X * KD]).then_inc(small_turned, 1)
                    pe.transpose(ps_s[:, 2, 0:X * FH], b1_rows[:], ident[0:X * FH, 0:X * FH]).then_inc(small_turned, 1)
                    pe.wait_ge(xf_ready, 1)
                    for b in range(NB):
                        for k in range(KD):
                            if b:
                                pe.wait_ge(f_copied, (b - 1) * KD + k + 1)
                            pe.transpose(ps_t[:, k, 0:P], xn[:, b, k * P:(k + 1) * P], ident[:]).then_inc(f_turned, 1)
                    pe.wait_ge(f_copied, NB * KD)
                    for b in range(NB):
                        for k in range(KD):
                            pe.matmul(ps_l[:, b * X:(b + 1) * X], tok_t[:, k, b * P:(b + 1) * P], wr[:, k, :], start=(k == 0), stop=False)
                        last = pe.matmul(ps_l[:, b * X:(b + 1) * X], ones[0:1, :], br_row[:], start=False, stop=True)
                    last.then_inc(logits_ready, 1)
                    pe.wait_ge(chosen_ready, 1)
                    flat = chosen[:].rearrange("p b e -> p (b e)")
                    pe.matmul(ps_n[:, 0, 0:NB * X], before[:], flat, start=True, stop=True)
                    pe.matmul(ps_n[:, 1, 0:NB * X], ones[:], flat, start=True, stop=True).then_inc(prefix_ready, 1)

            with ExitStack() as ctx:
                w1 = sbuf(ctx, "w1", [P, 2, KD, HID])
                tok = sbuf(ctx, "tok", [P, 4, D])
                x_e = sbuf(ctx, "x_e", [P, 2, KD, P])
                hid = sbuf(ctx, "hid", [P, 2, FH, P])
                y_out = sbuf(ctx, "y_out", [P, 2, D])
                ps_t = psum(ctx, "ps_te", [P, 2, 512])
                ps_h = psum(ctx, "ps_h", [P, 2, 2, 512])
                ps_y = psum(ctx, "ps_y", [P, 2, 512])
                tok_in = sems(*[f"tok_in{n}" for n in range(4)])
                w1_in = sems("w1_in0", "w1_in1")
                y_stored = sems("y_stored0", "y_stored1")
                tok_turned, xe_ready, h_ready, hid_ready, y_ready, y_copied = sems(
                    "tok_turned", "xe_ready", "h_ready", "hid_ready", "y_ready", "y_copied")
                block = ctx.enter_context(nc.Block())

                @block.sync
                def _(sp):
                    def load(a):
                        s = a.slot(4)
                        wait_done(sp, tok_turned, a, 4)
                        sp.dma_start(tok[:, s, :], sorted_dram[ds(a.t * P, P), :]).then_inc(tok_in[s], 16)
                        e = sp.value_load(expert_i[0:1, ds(a.t, 1)], min_val=0, max_val=X - 1)
                        if a.c >= 2:
                            sp.wait_ge(h_ready, a.t * 2 - 2)
                        sp.dma_start(w1[:, a.slot(2)], W1[ds(e, 1), :, :].rearrange("o (k p) h -> p (o k) h", p=P)).then_inc(w1_in[a.slot(2)], 16)

                    walk(sp, XT, load)

                @block.gpsimd
                def _(pool):
                    def store(a):
                        h = a.slot(2)
                        pool.wait_ge(y_copied, a.t + 1)
                        pool.dma_start(expert_out_dram[ds(a.t * P, P), :], y_out[:, h, :]).then_inc(y_stored[h], 16)

                    walk(pool, XT, store)
                    pool.wait_ge(y_stored[0], 16 * (XT - XT // 2))
                    pool.wait_ge(y_stored[1], 16 * (XT // 2))

                @block.vector
                def _(dve):
                    def scale(a):
                        h = a.slot(2)
                        e = dve.value_load(expert_i[0:1, ds(a.t, 1)], min_val=0, max_val=X - 1)
                        wait_done(dve, tok_turned, a)
                        if a.c >= 2:
                            dve.wait_ge(h_ready, a.t * 2 - 2)
                        for k in range(KD):
                            last = dve.tensor_scalar(x_e[:, h, k, :], ps_t[:, h, k * P:(k + 1) * P], ln_t[:, 0, ds(e * KD + k, 1)],
                                                     ln_t[:, 1, ds(e * KD + k, 1)], ALU.mult, ALU.add)
                        last.then_inc(xe_ready, 1)

                    def copy_y(a):
                        h = a.slot(2)
                        wait_done(dve, y_ready, a)
                        wait_slot(dve, y_stored[h], a, 2, 16)
                        dve.tensor_copy(y_out[:, h, :], ps_y[:, h, 0:D]).then_inc(y_copied, 1)

                    def step(a):
                        scale(a)
                        if a.c >= 2:
                            copy_y(a + -2)

                    walk(dve, XT, step)
                    copy_y(At(0, XT - 2))
                    copy_y(At(0, XT - 1))

                @block.scalar
                def _(act):
                    def gelu(a):
                        h = a.slot(2)
                        e = act.value_load(expert_i[0:1, ds(a.t, 1)], min_val=0, max_val=X - 1)
                        wait_done(act, y_ready, a, 2)
                        for f in range(FH):
                            if f % 4 == 0:
                                act.wait_ge(h_ready, a.t * 2 + f // 4 + 1)
                            act.activation(hid[:, h, f, :], ps_h[:, h, f // 4, f % 4 * P:(f % 4 + 1) * P], ACT.Gelu,
                                           bias=b1_t[:, ds(e * FH + f, 1)]).then_inc(hid_ready, 1)

                    walk(act, XT, gelu)

                @block.tensor
                def _(pe):
                    def turn_tok(a):
                        h = a.slot(2)
                        pe.wait_ge(tok_in[a.slot(4)], (a.turn(4) + 1) * 16)
                        wait_done(pe, xe_ready, a, 2)
                        for k in range(KD):
                            last = pe.transpose(ps_t[:, h, k * P:(k + 1) * P], tok[:, a.slot(4), k * P:(k + 1) * P], ident[:])
                        last.then_inc(tok_turned, 1)

                    def first(a):
                        h = a.slot(2)
                        wait_done(pe, xe_ready, a)
                        pe.wait_ge(w1_in[h], (a.turn(2) + 1) * 16)
                        if a.c >= 2:
                            pe.wait_ge(hid_ready, a.t * FH - FH)
                        for f in range(FH):
                            for k in range(KD):
                                last = pe.matmul(ps_h[:, h, f // 4, f % 4 * P:(f % 4 + 1) * P], w1[:, h, k, f * P:(f + 1) * P], x_e[:, h, k, :],
                                                 start=(k == 0), stop=(k == KD - 1))
                            if f % 4 == 3:
                                last.then_inc(h_ready, 1)

                    def second(a):
                        h = a.slot(2)
                        e = pe.value_load(expert_i[0:1, ds(a.t, 1)], min_val=0, max_val=X - 1)
                        wait_done(pe, y_copied, a, 2)
                        for f in range(FH):
                            pe.wait_ge(hid_ready, a.t * FH + f + 1)
                            pe.matmul(ps_y[:, h, 0:D], hid[:, h, f, :], w2[:, ds(e, 1), f, :].rearrange("p o c -> p (o c)"), start=(f == 0), stop=False)
                        pe.matmul(ps_y[:, h, 0:D], ones[0:1, :], b2_row[:, ds(e, 1), :].rearrange("o e c -> o (e c)"), start=False,
                                  stop=True).then_inc(y_ready, 1)

                    def step(a):
                        if a.c == 0:
                            turn_tok(a)
                        if a.c + 1 < XT:
                            turn_tok(a + 1)
                        first(a)
                        if a.c:
                            second(a + -1)

                    walk(pe, XT, step)
                    second(At(0, XT - 1))

            with ExitStack() as ctx:
                got = sbuf(ctx, "got", [P, 4, TOP, D])
                get_st = sbuf(ctx, "get_st", [P, 4, TOP], I32)
                got_in = sems(*[f"got_in{n}" for n in range(4)])
                get_staged, got_added, out_done = sems("get_staged", "got_added", "out_done")
                block = ctx.enter_context(nc.Block())

                @block.gpsimd
                def _(pool):
                    def get(a):
                        s = a.slot(4)
                        pool.wait_ge(get_staged, a.t + 1)
                        if a.c >= 4:
                            pool.wait_ge(got_added, a.t * TOP - 6)
                        pool.sem_inc(pool_turn, 1)
                        for n in range(TOP):
                            pool.indirect_dma_start(got[:, s, n, :], None, expert_out_dram[:, :],
                                                    bass.IndirectOffsetOnAxis(ap=get_st[:, s, n:n + 1], axis=0)).then_inc(got_in[s], 16)

                    walk(pool, NB, get)

                @block.vector
                def _(dve):
                    def stage(a):
                        s = a.slot(4)
                        wait_slot(dve, got_in[s], a, 4, 16 * TOP)
                        dve.tensor_copy(get_st[:, s, :], place_i[:, ds(a.t, 1), :].rearrange("p b n -> p (b n)")).then_inc(get_staged, 1)

                    def add(a):
                        s = a.slot(4)
                        dve.wait_ge(got_in[s], (a.turn(4) + 1) * 16 * TOP)
                        row = res[:, ds(a.t, 1), :].rearrange("p b c -> p (b c)")
                        for n in range(TOP):
                            dve.scalar_tensor_tensor(row, got[:, s, n, :], gate[:, n, ds(a.t, 1)], row, ALU.mult, ALU.add).then_inc(got_added, 1)
                            dve.wait_ge(got_added, a.t * TOP + n + 1)

                    def step(a):
                        add(a)
                        if not isinstance(a.t, int) or a.t + 4 < NB:
                            stage(a + 4)

                    for t in range(4):
                        stage(At(0, t))
                    walk(dve, NB, step)

                @block.sync
                def _(sp):
                    sp.wait_ge(got_added, NB * TOP)
                    sp.dma_start(out[0:d.FULL * P, :].rearrange("(b p) c -> p b c", p=P), res[:, 0:d.FULL, :]).then_inc(out_done, 16)
                    sp.dma_start(out[d.FULL * P:N, :], res[0:d.TAIL, d.FULL, :]).then_inc(out_done, 16)
                    sp.wait_ge(out_done, 32)


_INS = ['x', 'src', 'dst', 'edge_attr_5', 'node_type_19', 'L0_gnn_Wk', 'L0_gnn_bk', 'L0_gnn_Wq', 'L0_gnn_bq',
        'L0_gnn_Wv', 'L0_gnn_bv', 'L0_gnn_Wa', 'L0_gnn_ba', 'L0_gnn_gamma', 'L0_gnn_beta', 'L0_gnn_w_time',
        'L0_gnn_b_time', 'L0_ffn_Wr', 'L0_ffn_br', 'L0_ffn_ln_g', 'L0_ffn_ln_b', 'L0_ffn_W1', 'L0_ffn_b1',
        'L0_ffn_W2', 'L0_ffn_b2']


def kernel(**inputs):
    import numpy as _np
    import concourse.bacc as _bacc
    from concourse import mybir as _mybir
    from concourse.bass_utils import run_bass_kernel_spmd as _run

    nc = _bacc.Bacc("TRN2", target_bir_lowering=False, num_devices=1)
    arrays, args = {}, []
    for name in _INS:
        a = _np.ascontiguousarray(inputs[name])
        arrays[f"in_{name}"] = a
        args.append(nc.dram_tensor(f"in_{name}", a.shape, _mybir.dt.from_np(a.dtype), kind="ExternalInput").ap())
    args.append(nc.dram_tensor("out_x", inputs["x"].shape, _mybir.dt.float32, kind="ExternalOutput").ap())
    gnn_ffn_kernel(nc, *args)
    r = _run(nc, [arrays], core_ids=[0])
    return r.results[0]["out_x"]
```

```python
from contextlib import ExitStack

import concourse.bass as bass
from concourse import mybir

F32 = mybir.dt.float32
I32 = mybir.dt.int32
BF16 = mybir.dt.bfloat16
ALU = mybir.AluOpType
ACT = mybir.ActivationFunctionType
AX = mybir.AxisListType.X

P = 128
TWO_PI = 6.283185307179586
SIN_SCALE = 6.283185
MAGIC = 12582912.0
BIG = 1.0e30
RESET = -2.0e38
LN_EPS = 1e-5


class Chain:

    def __init__(self, eng, sem, base=0):
        self.eng, self.sem, self.base, self.n = eng, sem, base, 0

    def __call__(self, ins):
        self.n += 1
        ins.then_inc(self.sem, 1)
        self.eng.wait_ge(self.sem, self.base + self.n)


class At:

    def __init__(self, i, c):
        self.i, self.c, self.t = i, c, i * 4 + c

    def slot(self, k):
        return self.c % k

    def turn(self, k):
        return self.i * (4 // k) + self.c // k

    def __add__(self, n):
        return At(self.i, self.c + n)


def walk(eng, steps, step):
    for t in range(min(4, steps)):
        step(At(0, t))
    loops = (steps - 5) // 4
    with eng.Fori(0, loops) as i:
        for u in range(4):
            step(At(i, 4 + u))
    for t in range(4 + 4 * loops, steps):
        step(At(0, t))


def wait_slot(eng, sem, a, slots, by=1):
    if a.c >= slots:
        eng.wait_ge(sem, a.turn(slots) * by)


def wait_done(eng, sem, a, back=0):
    if a.c >= back:
        eng.wait_ge(sem, a.t + (1 - back))


class Dims:

    def __init__(self, x, src, Wk, Wa, w_time, W1):
        self.N, self.D = x.shape
        self.E = src.shape[0]
        self.T, _, self.PROJ = Wk.shape
        self.TD = w_time.shape[0]
        self.KD = self.D // P
        self.H = 4
        self.DK = (self.D - self.TD) // self.H
        self.LAST = self.PROJ - 3 * self.DK
        self.NB = -(-self.N // P)
        self.NP = self.NB * P
        self.FULL = self.N // P
        self.TAIL = self.N - self.FULL * P
        self.C = 8
        self.EC = -(-self.E // (P * self.C)) * self.C
        self.EFULL = self.E // self.EC
        self.ETAIL = self.E - self.EFULL * self.EC
        self.KB = 2 * self.NB
        self.G = 4
        self.R = 4
        rows = 2 * self.EC * P // self.G + self.KB * P
        self.RT = -(-rows // (P * self.R)) * self.R
        self.NR = self.RT * P
        self.QKV = 2 * self.PROJ + self.DK
        self.MSG = self.D + self.H
        self.X, _, self.HID = W1.shape
        self.TOP = 2
        self.XT = self.TOP * self.NB + self.X - 1
        self.TT = self.NB + self.T - 1


class Groups:

    def __init__(self, sbuf, ctx, tag, blocks, groups, tiles):
        self.blocks, self.groups, self.tiles = blocks, groups, tiles
        self.block_tot = sbuf(ctx, "block_tot_" + tag, [P, blocks, groups])
        self.block_upto = sbuf(ctx, "block_upto_" + tag, [P, blocks, groups])
        self.row_of = sbuf(ctx, "row_of_" + tag, [P, blocks, groups])
        self.tiles_i = sbuf(ctx, "tiles_i_" + tag, [P, groups], I32)
        self.tiles_f = sbuf(ctx, "tiles_f_" + tag, [P, groups])
        self.tiles_upto = sbuf(ctx, "tiles_upto_" + tag, [P, groups])
        self.first_row = sbuf(ctx, "first_row_" + tag, [P, groups])
        self.past = sbuf(ctx, "past_" + tag, [P, tiles, groups])

    def place(self, dve, link, ps_n, ones, lane, of_tile):
        NB, X, XT = self.blocks, self.groups, self.tiles
        flat = lambda t: t[:].rearrange("p b e -> p (b e)")
        link(dve.tensor_copy(flat(self.block_tot), ps_n[:, 1, 0:NB * X]))
        for e in range(X):
            last = dve.tensor_tensor_scan(self.block_upto[:, :, e], ones[:, 0:NB], self.block_tot[:, :, e], 0.0, ALU.mult, ALU.add)
        link(last)
        link(dve.tensor_scalar(self.tiles_i[:], self.block_upto[:, NB - 1, :], float(P - 1), None, ALU.add))
        link(dve.tensor_scalar(self.tiles_i[:], self.tiles_i[:], P.bit_length() - 1, None, ALU.arith_shift_right))
        link(dve.tensor_copy(self.tiles_f[:], self.tiles_i[:]))
        link(dve.tensor_tensor_scan(self.tiles_upto[:], ones[:, 0:X], self.tiles_f[:], 0.0, ALU.mult, ALU.add))
        link(dve.tensor_tensor(self.first_row[:], self.tiles_upto[:], self.tiles_f[:], ALU.subtract))
        link(dve.tensor_scalar(self.first_row[:], self.first_row[:], float(P), None, ALU.mult))
        link(dve.tensor_tensor(self.row_of[:], self.block_upto[:], self.block_tot[:], ALU.subtract))
        link(dve.tensor_tensor(flat(self.row_of), flat(self.row_of), ps_n[:, 0, 0:NB * X], ALU.add))
        link(dve.tensor_tensor(self.row_of[:], self.row_of[:], self.first_row[:].unsqueeze(1).broadcast_to([P, NB, X]), ALU.add))
        link(dve.tensor_tensor(self.past[:], lane[:, 0:XT].unsqueeze(2).broadcast_to([P, XT, X]),
                               self.tiles_upto[:].unsqueeze(1).broadcast_to([P, XT, X]), ALU.is_ge))
        link(dve.tensor_reduce(of_tile[:], self.past[:], AX, ALU.add))
        link(dve.tensor_scalar(of_tile[:], of_tile[:], float(X - 1), None, ALU.min))


def gnn_ffn_kernel(nc, x, src, dst, edge_attr, node_type, Wk, bk, Wq, bq, Wv, bv, Wa, ba, gamma, beta,
                   w_time, b_time, Wr, br, ln_g, ln_b, W1, b1, W2, b2, out):
    d = Dims(x, src, Wk, Wa, w_time, W1)
    N, D, E, T, KD, NB, NPAD = d.N, d.D, d.E, d.T, d.KD, d.NB, d.NP
    PROJ, TD, H, DK, LAST = d.PROJ, d.TD, d.H, d.DK, d.LAST
    G, R, RT, NR, KB, EC, C = d.G, d.R, d.RT, d.NR, d.KB, d.EC, d.C
    ds = bass.ds

    KVW = 2 * PROJ + TD
    kv_dram = nc.dram_tensor("kv_table", (1 + NPAD, KVW), F32).ap()
    q_dram = nc.dram_tensor("q_table", (NPAD, DK), F32).ap()
    keyrow_dram = nc.dram_tensor("key_rows", (2 * EC, P), F32).ap()
    lorow_dram = nc.dram_tensor("lo_rows", (2 * EC, P), F32).ap()
    rec_dram = nc.dram_tensor("edge_records", (NR * G, 4), F32).ap()
    starts_dram = nc.dram_tensor("row_starts", (NR + P, 1 + DK), F32).ap()
    part_dram = nc.dram_tensor("row_messages", (NR, d.MSG), F32).ap()
    xn_dram = nc.dram_tensor("normalized_x", (NPAD, D), F32).ap()
    typed_x_dram = nc.dram_tensor("nodes_by_type", (d.TT * P, D), F32).ap()
    typed_kvq_dram = nc.dram_tensor("kvq_by_type", (d.TT * P, KVW + DK), F32).ap()
    typed_out_dram = nc.dram_tensor("typed_out", (d.TT * P, D), F32).ap()
    sorted_dram = nc.dram_tensor("tokens_by_expert", (d.XT * P, D), F32).ap()
    expert_out_dram = nc.dram_tensor("expert_out", (d.XT * P, D), F32).ap()
    wk_dram = nc.dram_tensor("row_weights", (NR, H + 1), F32).ap()

    top = ExitStack()
    with top:
        def sbuf(ctx, name, shape, dt=F32):
            return ctx.enter_context(nc.sbuf_tensor(name, shape, dt))

        def psum(ctx, name, shape, dt=F32):
            return ctx.enter_context(nc.psum_tensor(name, shape, dt))

        in_use = []

        def sems(*names):
            made = [nc.alloc_semaphore(name=n) for n in names]
            in_use.extend(made)
            return made

        def clear_sems():
            nc.clear_and_free_semaphores(list(in_use))
            in_use.clear()
            nc.all_engine_barrier()

        pool_turn = nc.alloc_semaphore(name="pool_turn")

        xn = sbuf(top, "xn", [P, NB, D])
        res = sbuf(top, "res", [P, NB, D])
        ident = sbuf(top, "ident", [P, P])
        ones = sbuf(top, "ones", [P, P])
        before = sbuf(top, "before", [P, P])
        after = sbuf(top, "after", [P, P])
        lane = sbuf(top, "lane", [P, 2 * P])
        lane_col = sbuf(top, "lane_col", [P, 1])
        magic = sbuf(top, "magic", [P, 1])
        type_rows = sbuf(top, "type_rows", [NB, P], I32)
        type_row = sbuf(top, "type_row", [P, NB], I32)
        tile_type = sbuf(top, "tile_type", [P, d.TT])
        tile_type_i = sbuf(top, "tile_type_i", [P, d.TT], I32)
        stats = sbuf(top, "stats", [P, NB, 6])
        mean = sbuf(top, "mean", [P, NB])
        rstd = sbuf(top, "rstd", [P, NB])
        tmp_a = sbuf(top, "tmp_a", [P, NB])
        tmp_b = sbuf(top, "tmp_b", [P, NB])

        def layer_norm_stats(dve, act_in, act_out, link, source, turn):
            for b in range(NB):
                last = dve.bn_stats(stats[:, b, :], source[:, b, :])
            link(last)
            link(dve.tensor_tensor(mean[:], stats[:, :, 1], stats[:, :, 4], ALU.add))
            link(dve.tensor_tensor(tmp_a[:], stats[:, :, 1], stats[:, :, 4], ALU.subtract))
            link(dve.tensor_tensor(tmp_b[:], stats[:, :, 2], stats[:, :, 5], ALU.add))
            link(dve.tensor_scalar(mean[:], mean[:], 0.5, None, ALU.mult))
            link(dve.tensor_tensor(tmp_a[:], tmp_a[:], tmp_a[:], ALU.mult))
            link(dve.tensor_scalar(tmp_a[:], tmp_a[:], 0.25, LN_EPS, ALU.mult, ALU.add))
            dve.scalar_tensor_tensor(tmp_b[:], tmp_b[:], 1.0 / D, tmp_a[:], ALU.mult, ALU.add).then_inc(act_in, 1)
            dve.wait_ge(act_out, turn)
            link(dve.reciprocal(rstd[:], rstd[:]))

        def normalize(dve, dst_t, source, ready=None):
            for b in range(NB):
                last = dve.tensor_scalar(dst_t[:, b, :], source[:, b, :], mean[:, b:b + 1], rstd[:, b:b + 1],
                                         ALU.subtract, ALU.mult)
                if ready is not None:
                    last.then_inc(ready, 1)
            return last

        TT = d.TT
        with ExitStack() as ctx:
            wcat = sbuf(ctx, "wcat", [P, T * KD, d.QKV])
            wq_st = sbuf(ctx, "wq_st", [P, T * KD, PROJ])
            bcat = sbuf(ctx, "bcat", [T, d.QKV])
            bq_st = sbuf(ctx, "bq_st", [T, PROJ])
            zeros = sbuf(ctx, "zeros_x", [P, D])
            groups = Groups(sbuf, ctx, "type", NB, T, TT)
            type_f = sbuf(ctx, "type_f", [NB, P])
            type_t = sbuf(ctx, "type_t", [P, NB])
            is_type = sbuf(ctx, "is_type", [P, NB, T])
            row_f = sbuf(ctx, "row_f", [P, NB])
            nodes = sbuf(ctx, "nodes", [P, 4, D])
            x_t = sbuf(ctx, "x_t", [P, 2, KD, P])
            chosen_t = sbuf(ctx, "chosen_t", [T, 2, P])
            qkv = sbuf(ctx, "qkv", [P, 2, KVW + DK])
            ps_t = psum(ctx, "ps_t", [P, 2, 512])
            ps_n = psum(ctx, "ps_nt", [P, 2, 512])
            ps_qkv = psum(ctx, "ps_qkv", [P, 2, 512])
            zeroed, consts, type_in, type_turned, type_ready, is_ready, counted = sems(
                "zeroed", "consts", "type_in", "type_turned", "type_ready", "is_ready", "types_counted")
            x_in, wq_in, w_in, filled, var_ready, std_ready, const_chain, dve_chain = sems(
                "x_in", "wq_in", "w_in", "filled", "var_ready", "std_ready", "const_chain", "dve_chain")
            xn_ready, x_sent, q_folded, turned, xt_ready, qkv_ready, qkv_copied = sems(
                "xn_ready", "x_sent", "q_folded", "turned", "xt_ready", "qkv_ready", "qkv_copied")
            xn_saved, = sems("xn_saved")
            node_in = sems(*[f"node_in{n}" for n in range(4)])
            qkv_stored = sems("qkv_stored0", "qkv_stored1")
            block = ctx.enter_context(nc.Block())

            @block.sync
            def _(sp):
                sp.wait_ge(zeroed, 3)
                sp.dma_start(type_rows[0:d.FULL, :], node_type[0:d.FULL * P].rearrange("(b p) -> b p", p=P)).then_inc(type_in, 16)
                sp.dma_start(type_rows[d.FULL:NB, 0:d.TAIL], node_type[d.FULL * P:N].rearrange("(o p) -> o p", o=1)).then_inc(type_in, 16)
                sp.dma_start(res[:, 0:d.FULL, :], x[0:d.FULL * P, :].rearrange("(b p) c -> p b c", p=P)).then_inc(x_in, 16)
                sp.dma_start(res[0:d.TAIL, d.FULL, :], x[d.FULL * P:N, :]).then_inc(x_in, 16)
                sp.dma_start(typed_x_dram.rearrange("(t p) c -> p t c", p=P), zeros[:].unsqueeze(1).broadcast_to([P, TT, D])).then_inc(filled, 16)
                sp.dma_start(wq_st[:], Wq.rearrange("t (k p) c -> p (t k) c", p=P)).then_inc(wq_in, 16)
                sp.dma_start(bq_st[:], bq).then_inc(wq_in, 16)
                sp.dma_start(wcat[:, :, 0:PROJ], Wk.rearrange("t (k p) c -> p (t k) c", p=P)).then_inc(w_in, 16)
                sp.dma_start(wcat[:, :, PROJ:2 * PROJ], Wv.rearrange("t (k p) c -> p (t k) c", p=P)).then_inc(w_in, 16)
                sp.dma_start(bcat[:, 0:PROJ], bk).then_inc(w_in, 16)
                sp.dma_start(bcat[:, PROJ:2 * PROJ], bv).then_inc(w_in, 16)
                sp.wait_ge(x_sent, 16 * NB)
                sp.dma_start(xn_dram.rearrange("(b p) c -> p b c", p=P), xn[:]).then_inc(xn_saved, 16)

                def load(a):
                    wait_done(sp, turned, a, 4)
                    sp.dma_start(nodes[:, a.slot(4), :], typed_x_dram[ds(a.t * P, P), :]).then_inc(node_in[a.slot(4)], 16)

                walk(sp, TT, load)
                sp.wait_ge(xn_saved, 16)

            @block.gpsimd
            def _(pool):
                pool.memset(type_rows[:], 0).then_inc(zeroed, 1)
                pool.memset(zeros[:], 0.0).then_inc(zeroed, 1)
                pool.memset(res[:, d.FULL:NB, :], 0.0).then_inc(zeroed, 1)
                pool.memset(qkv[:, :, PROJ:PROJ + TD], 0.0).then_inc(const_chain, 1)
                pool.iota(lane[:], [[1, 2 * P]], base=0, channel_multiplier=0,
                          allow_small_or_imprecise_dtypes=True).then_inc(const_chain, 1)
                pool.iota(lane_col[:], [[0, 1]], base=0, channel_multiplier=1,
                          allow_small_or_imprecise_dtypes=True).then_inc(const_chain, 1)
                pool.wait_ge(const_chain, 3)
                pool.memset(ones[:], 1.0).then_inc(consts, 1)
                pool.tensor_scalar(ident[:], lane[:, 0:P], lane_col[:, 0:1], None, ALU.is_equal).then_inc(consts, 1)
                pool.tensor_scalar(before[:], lane[:, 0:P], lane_col[:, 0:1], None, ALU.is_gt).then_inc(consts, 1)
                pool.tensor_scalar(after[:], lane[:, 0:P], lane_col[:, 0:1], None, ALU.is_lt).then_inc(consts, 1)
                pool.memset(magic[:], MAGIC)
                pool.wait_ge(filled, 16)
                for b in range(NB):
                    pool.wait_ge(xn_ready, b + 1)
                    pool.sem_inc(pool_turn, 1)
                    pool.indirect_dma_start(typed_x_dram[:, :], bass.IndirectOffsetOnAxis(ap=type_row[:, b:b + 1], axis=0),
                                            xn[:, b, :], None).then_inc(x_sent, 16)

                def store(a):
                    h = a.slot(2)
                    pool.wait_ge(qkv_copied, a.t + 1)
                    pool.dma_start(typed_kvq_dram[ds(a.t * P, P), :], qkv[:, h, :]).then_inc(qkv_stored[h], 16)

                walk(pool, TT, store)
                pool.wait_ge(qkv_stored[0], 16 * (TT - TT // 2))
                pool.wait_ge(qkv_stored[1], 16 * (TT // 2))

            @block.vector
            def _(dve):
                link = Chain(dve, dve_chain)
                dve.wait_ge(type_in, 32)
                dve.tensor_copy(type_f[:], type_rows[:]).then_inc(type_ready, 1)
                dve.wait_ge(consts, 4)
                dve.wait_ge(type_turned, 1)
                link(dve.tensor_copy(type_t[:], ps_t[:, 0, 0:NB]))
                dve.tensor_tensor(is_type[:], type_t[:].unsqueeze(2).broadcast_to([P, NB, T]),
                                  lane[:, 0:T].unsqueeze(1).broadcast_to([P, NB, T]), ALU.is_equal).then_inc(is_ready, 1)
                dve.wait_ge(x_in, 32)
                layer_norm_stats(dve, var_ready, std_ready, link, res, 1)
                dve.wait_ge(counted, 1)
                groups.place(dve, link, ps_n, ones, lane, tile_type)
                link(dve.tensor_copy(tile_type_i[:], tile_type[:]))
                link(dve.tensor_tensor(is_type[:], is_type[:], groups.row_of[:], ALU.mult))
                link(dve.tensor_reduce(row_f[:], is_type[:], AX, ALU.add))
                link(dve.tensor_copy(type_row[:], row_f[:]))
                normalize(dve, xn, res, xn_ready)
                dve.wait_ge(wq_in, 32)
                for wt, wst in ((wcat[:, :, 2 * PROJ:d.QKV], wq_st[:, :, :]),
                                (bcat[:, 2 * PROJ:d.QKV], bq_st[:, :])):
                    cut = (lambda t, a, b: t[:, :, a:b]) if len(wt.shape) == 3 else (lambda t, a, b: t[:, a:b])
                    link(dve.tensor_tensor(wt, cut(wst, 0, DK), cut(wst, DK, 2 * DK), ALU.add))
                    link(dve.tensor_tensor(wt, wt, cut(wst, 2 * DK, 3 * DK), ALU.add))
                    link(dve.tensor_tensor(cut(wt, 0, LAST), cut(wt, 0, LAST), cut(wst, 3 * DK, PROJ), ALU.add))
                dve.sem_inc(q_folded, 1)

                def copy_x(a):
                    h = a.slot(2)
                    wait_done(dve, qkv_ready, a, 2)
                    dve.tensor_copy(chosen_t[:, h, :], lane_col[0:T, 0:1].broadcast_to([T, P]))
                    wait_done(dve, turned, a)
                    dve.tensor_copy(x_t[:, h].rearrange("p k c -> p (k c)"), ps_t[:, h, 0:D]).then_inc(xt_ready, 1)
                    dve.wait_ge(xt_ready, a.t * 2 + 1)
                    dve.tensor_scalar(chosen_t[:, h, :], chosen_t[:, h, :], tile_type[0:T, ds(a.t, 1)], None, ALU.is_equal).then_inc(xt_ready, 1)

                walk(dve, TT, copy_x)

            @block.scalar
            def _(act):
                act.wait_ge(var_ready, 1)
                act.activation(rstd[:], tmp_b[:], ACT.Sqrt).then_inc(std_ready, 1)

                def copy_qkv(a):
                    h = a.slot(2)
                    wait_done(act, qkv_ready, a)
                    wait_slot(act, qkv_stored[h], a, 2, 16)
                    act.copy(qkv[:, h, 0:PROJ], ps_qkv[:, h, 0:PROJ])
                    act.copy(qkv[:, h, PROJ + TD:], ps_qkv[:, h, PROJ:d.QKV]).then_inc(qkv_copied, 1)

                walk(act, TT, copy_qkv)

            @block.tensor
            def _(pe):
                pe.wait_ge(consts, 4)
                pe.wait_ge(type_ready, 1)
                pe.transpose(ps_t[:, 0, 0:NB], type_f[:], ident[0:NB, 0:NB]).then_inc(type_turned, 1)
                pe.wait_ge(is_ready, 1)
                pe.matmul(ps_n[:, 0, 0:NB * T], before[:], is_type[:].rearrange("p b t -> p (b t)"), start=True, stop=True)
                pe.matmul(ps_n[:, 1, 0:NB * T], ones[:], is_type[:].rearrange("p b t -> p (b t)"), start=True, stop=True).then_inc(counted, 1)

                def turn_node(a):
                    h = a.slot(2)
                    pe.wait_ge(node_in[a.slot(4)], (a.turn(4) + 1) * 16)
                    if a.c >= 2:
                        pe.wait_ge(xt_ready, a.t * 2 - 2)
                    for k in range(KD):
                        last = pe.transpose(ps_t[:, h, k * P:(k + 1) * P], nodes[:, a.slot(4), k * P:(k + 1) * P], ident[:])
                    last.then_inc(turned, 1)

                def project(a):
                    h = a.slot(2)
                    ty = pe.value_load(tile_type_i[0:1, ds(a.t, 1)], min_val=0, max_val=T - 1)
                    pe.wait_ge(xt_ready, a.t * 2 + 2)
                    wait_done(pe, qkv_copied, a, 2)
                    for k in range(KD):
                        pe.matmul(ps_qkv[:, h, 0:d.QKV], x_t[:, h, k, :], wcat[:, ds(ty * KD + k, 1), :].rearrange("p o c -> p (o c)"),
                                  start=(k == 0), stop=False)
                    pe.matmul(ps_qkv[:, h, 0:d.QKV], chosen_t[:, h, :], bcat[:], start=False, stop=True).then_inc(qkv_ready, 1)

                def step(a):
                    if not isinstance(a.t, int) or a.t + 1 < TT:
                        turn_node(a + 1)
                    if isinstance(a.t, int) and a.t == 0:
                        pe.wait_ge(w_in, 64)
                        pe.wait_ge(q_folded, 1)
                    project(a)

                turn_node(At(0, 0))
                walk(pe, TT, step)

        clear_sems()
        row_base = sbuf(top, "row_base", [P, KB])

        NC = 2 * EC // C
        rows = ExitStack()
        marks = sbuf(rows, "marks", [P, RT])
        marks_next = sbuf(rows, "marks_next", [P, RT])
        key_of = sbuf(rows, "key_of", [P, RT])
        q_all = sbuf(rows, "q_all", [P, RT, 1 + DK])
        edges = ExitStack()
        with edges:
            rec = sbuf(edges, "rec", [P, 2 * EC, 4])
            key_f = sbuf(edges, "key_f", [P, 2 * EC])
            lo_f = sbuf(edges, "lo_f", [P, 2 * EC])
            hi_f = sbuf(edges, "hi_f", [P, 2 * EC])
            start = sbuf(edges, "start", [P, NB, 1 + DK])

            with ExitStack() as ctx:
                zero_row = sbuf(ctx, "zero_row", [1, KVW])
                kvq = sbuf(ctx, "kvq", [P, 4, KVW + DK])
                ends = [sbuf(ctx, "src_i", [P, EC], I32), sbuf(ctx, "dst_i", [P, EC], I32)]
                attr = sbuf(ctx, "attr", [P, EC, edge_attr.shape[1]])
                key_i = sbuf(ctx, "key_i", [P, 2 * EC], I32)
                lo_i = sbuf(ctx, "lo_i", [P, 2 * EC], I32)
                hi_i = sbuf(ctx, "hi_i", [P, 2 * EC], I32)
                ZW = NR * G * 4 // P
                zeros = sbuf(ctx, "zeros", [P, ZW])
                filled = (rec_dram, starts_dram, sorted_dram)
                fills = sum(-(-(t.shape[0] // P * t.shape[1]) // ZW) for t in filled)
                zeros_b = sbuf(ctx, "zeros_b", [P, P], BF16)
                TC = 104
                NTC = 2 * EC // TC
                rows_sb = sbuf(ctx, "rows_sb", [TC, 2, NTC, P])
                lane_b = sbuf(ctx, "lane_b", [P, P], BF16)
                lo_hot = sbuf(ctx, "lo_hot", [P, 2, C, P], BF16)
                hi_hot = sbuf(ctx, "hi_hot", [P, 2, C, KB], BF16)
                cnt_i = sbuf(ctx, "cnt_i", [P, KB], I32)
                rows_f = sbuf(ctx, "rows_f", [P, KB])
                totals = sbuf(ctx, "totals", [P, KB])
                upto = sbuf(ctx, "upto", [P, KB])
                within = sbuf(ctx, "within", [P, KB])
                ps_row = psum(ctx, "ps_row", [P, 2, 512])
                ps_cnt = psum(ctx, "ps_cnt", [P, 512])
                ps_pre = psum(ctx, "ps_pre", [P, 2, 512])
                e_clear, e_in, keys_ready, lanes_ready, e_chain = sems("e_clear", "e_in", "keys_ready", "lanes_ready", "e_chain")
                row_tp, row_copied, rows_out, zeros_out = sems("row_tp", "row_copied", "rows_out", "zeros_out")
                hot_ready, cnt_ready, rows_ready, pre_ready = sems("hot_ready", "cnt_ready", "rows_ready", "pre_ready")
                hot_used = sems("hot_used0", "hot_used1")
                kvq_in = sems(*[f"kvq_in{n}" for n in range(4)])
                kvq_out = sems(*[f"kvq_out{n}" for n in range(4)])
                zero_out, q_kept = sems("zero_out", "q_kept")
                block = ctx.enter_context(nc.Block())

                @block.sync
                def _(sp):
                    sp.wait_ge(e_clear, 3)
                    for t, a in ((ends[0][:], src.rearrange("(n o) -> n o", o=1)),
                                 (ends[1][:], dst.rearrange("(n o) -> n o", o=1)),
                                 (attr[:].rearrange("p c a -> p (c a)"), edge_attr)):
                        sp.dma_start(t[0:d.EFULL, :], a[0:d.EFULL * EC, :].rearrange("(p c) a -> p (c a)", p=d.EFULL)).then_inc(e_in, 16)
                        sp.dma_start(t[d.EFULL:P, 0:d.ETAIL * a.shape[1]],
                                     a[d.EFULL * EC:E, :].rearrange("(p c) a -> p (c a)", p=1)).then_inc(e_in, 16)
                    sp.wait_ge(e_clear, 4)
                    for dram in filled:
                        flat = dram.rearrange("(p c) w -> p (c w)", p=P)
                        for at in range(0, flat.shape[1], ZW):
                            n = min(ZW, flat.shape[1] - at)
                            sp.dma_start(flat[:, at:at + n], zeros[:, 0:n]).then_inc(zeros_out, 16)
                    sp.wait_ge(row_copied, 2 * NTC)
                    for n, t in enumerate((keyrow_dram, lorow_dram)):
                        sp.dma_start(t.rearrange("(b r) c -> r b c", r=TC), rows_sb[:, n, :, :]).then_inc(rows_out, 16)
                    sp.dma_start(kv_dram[0:1, :], zero_row[:]).then_inc(zero_out, 16)
                    for b in range(NB):
                        sp.wait_ge(kvq_in[b % 4], 16 * (b // 4 + 1))
                        sp.dma_start(kv_dram[b * P + 1:b * P + 1 + P, :], kvq[:, b % 4, 0:KVW]).then_inc(kvq_out[b % 4], 16)
                        sp.dma_start(q_dram[b * P:b * P + P, :], kvq[:, b % 4, KVW:]).then_inc(kvq_out[b % 4], 16)
                    for s in range(4):
                        sp.wait_ge(kvq_out[s], 32 * len(range(s, NB, 4)))
                    sp.wait_ge(zeros_out, 16 * fills)
                    sp.wait_ge(rows_out, 32)
                    sp.wait_ge(zero_out, 16)

                @block.gpsimd
                def _(pool):
                    pool.memset(ends[0][:], N).then_inc(e_clear, 1)
                    pool.memset(ends[1][:], N).then_inc(e_clear, 1)
                    pool.memset(attr[:], 0.0).then_inc(e_clear, 1)
                    pool.memset(zero_row[:], 0.0)
                    pool.memset(start[:, :, 0:1], 1.0)
                    pool.memset(zeros[:], 0.0).then_inc(e_clear, 1)
                    for b in range(NB):
                        if b >= 4:
                            pool.wait_ge(kvq_out[b % 4], 32 * (b // 4))
                            pool.wait_ge(q_kept, b - 3)
                        pool.sem_inc(pool_turn, 1)
                        pool.indirect_dma_start(kvq[:, b % 4, :], None, typed_kvq_dram[:, :],
                                                bass.IndirectOffsetOnAxis(ap=type_row[:, b:b + 1], axis=0)).then_inc(kvq_in[b % 4], 16)

                @block.vector
                def _(dve):
                    link = Chain(dve, e_chain)
                    link(dve.memset(zeros_b[:], 0.0))
                    link(dve.tensor_copy(lane_b[:], lane[:, 0:P]))
                    dve.wait_ge(e_in, 96)
                    for way in range(2):
                        cols = slice(way * EC, (way + 1) * EC)
                        link(dve.tensor_scalar(rec[:, cols, 0], ends[way][:], 1.0, None, ALU.add))
                        link(dve.tensor_scalar(key_i[:, cols], ends[1 - way][:], float(way * NPAD), None, ALU.add))
                    dve.tensor_copy(key_f[:], key_i[:]).then_inc(keys_ready, 1)
                    link(dve.tensor_scalar(lo_i[:], key_i[:], P - 1, None, ALU.bitwise_and))
                    link(dve.tensor_scalar(hi_i[:], key_i[:], 7, None, ALU.arith_shift_right))
                    dve.tensor_copy(lo_f[:], lo_i[:]).then_inc(lanes_ready, 1)
                    link(dve.tensor_copy(hi_f[:], hi_i[:]))
                    dve.wait_ge(lanes_ready, 1)

                    def compare(a):
                        s = a.slot(2)
                        wait_slot(dve, hot_used[s], a, 2)
                        dve.tensor_tensor(lo_hot[:, s], lane_b[:].unsqueeze(1).broadcast_to([P, C, P]),
                                          lo_f[:, ds(a.t * C, C)].unsqueeze(2).broadcast_to([P, C, P]),
                                          ALU.is_equal).then_inc(hot_ready, 1)
                        dve.tensor_tensor(hi_hot[:, s], lane_b[:, 0:KB].unsqueeze(1).broadcast_to([P, C, KB]),
                                          hi_f[:, ds(a.t * C, C)].unsqueeze(2).broadcast_to([P, C, KB]),
                                          ALU.is_equal).then_inc(hot_ready, 1)

                    walk(dve, NC, compare)
                    dve.wait_ge(cnt_ready, 1)
                    link(dve.tensor_copy(cnt_i[:], ps_cnt[:, 0:KB]))
                    link(dve.tensor_scalar(cnt_i[:], cnt_i[:], float(G - 1), None, ALU.add))
                    link(dve.tensor_scalar(cnt_i[:], cnt_i[:], G.bit_length() - 1, None, ALU.arith_shift_right))
                    dve.tensor_scalar(rows_f[:], cnt_i[:], 1.0, None, ALU.max).then_inc(rows_ready, 1)
                    dve.wait_ge(pre_ready, 1)
                    link(dve.tensor_copy(totals[:], ps_pre[:, 1, 0:KB]))
                    link(dve.tensor_copy(within[:], ps_pre[:, 0, 0:KB]))
                    link(dve.tensor_tensor_scan(upto[:], ones[:, 0:KB], totals[:], 0.0, ALU.mult, ALU.add))
                    link(dve.tensor_tensor(upto[:], upto[:], totals[:], ALU.subtract))
                    link(dve.tensor_tensor(row_base[:], upto[:], within[:], ALU.add))

                @block.scalar
                def _(act):
                    act.wait_ge(e_in, 96)
                    for way, words in enumerate(((0, 1, 2), (0, 2, 1))):
                        for w, a in enumerate(words):
                            act.activation(rec[:, way * EC:(way + 1) * EC, 1 + w], attr[:, :, a], ACT.Ln, bias=1.0)
                    for n in range(2 * NTC):
                        act.wait_ge(row_tp, n + 1)
                        act.copy(rows_sb[:, n // NTC, n % NTC, :], ps_row[0:TC, n % 2, 0:P]).then_inc(row_copied, 1)
                    for b in range(NB):
                        act.wait_ge(kvq_in[b % 4], 16 * (b // 4 + 1))
                        act.copy(start[:, b, 1:], kvq[:, b % 4, KVW:]).then_inc(q_kept, 1)

                @block.tensor
                def _(pe):
                    pe.wait_ge(keys_ready, 1)
                    pe.wait_ge(lanes_ready, 1)
                    for n in range(2 * NTC):
                        if n >= 2:
                            pe.wait_ge(row_copied, n - 1)
                        t = (key_f, lo_f)[n // NTC]
                        pe.transpose(ps_row[0:TC, n % 2, 0:P], t[:, n % NTC * TC:(n % NTC + 1) * TC], ident[:]).then_inc(row_tp, 1)
                    pe.wait_ge(hot_ready, 1)
                    pe.matmul(ps_cnt[:, 0:KB], zeros_b[:], lane_b[:, 0:KB], start=True, stop=False, skip_group_check=True)

                    def count(a):
                        s = a.slot(2)
                        pe.wait_ge(hot_ready, a.t * 2 + 2)
                        for j in range(C):
                            last = pe.matmul(ps_cnt[:, 0:KB], lo_hot[:, s, j, :], hi_hot[:, s, j, :], start=False,
                                             stop=False, skip_group_check=True)
                        last.then_inc(hot_used[s], 1)

                    walk(pe, NC, count)
                    pe.matmul(ps_cnt[:, 0:KB], zeros_b[:], lane_b[:, 0:KB], start=False, stop=True,
                              skip_group_check=True).then_inc(cnt_ready, 1)
                    pe.wait_ge(rows_ready, 1)
                    pe.matmul(ps_pre[:, 0, 0:KB], before[:], rows_f[:], start=True, stop=True)
                    pe.matmul(ps_pre[:, 1, 0:KB], ones[:], rows_f[:], start=True, stop=True).then_inc(pre_ready, 1)

            with ExitStack() as ctx:
                key_row = sbuf(ctx, "key_row", [P, 2, C, P])
                lo_row = sbuf(ctx, "lo_row", [P, 2, C, P])
                lo_hot_t = sbuf(ctx, "lo_hot_t", [P, 2, C, P])
                lo_hot = sbuf(ctx, "lo_hot2", [P, 2, C, P])
                hi_hot = sbuf(ctx, "hi_hot2", [P, 2, C, KB])
                same = sbuf(ctx, "same", [P, C, P])
                picked = sbuf(ctx, "picked", [P, C, KB])
                rank = sbuf(ctx, "rank", [P, 2, C])
                seen = sbuf(ctx, "seen", [P, C])
                place = sbuf(ctx, "place", [P, 4, C], I32)
                rec_st = sbuf(ctx, "rec_st", [P, 4, C, 4])
                base_g = sbuf(ctx, "base_g", [P, KB])
                so_far = sbuf(ctx, "so_far", [P, 2, KB])
                base_i = sbuf(ctx, "base_i", [P, KB], I32)
                mark_st = sbuf(ctx, "mark_st", [P, NB], I32)
                low_rows = sbuf(ctx, "low_rows", [P, 1])
                going_on = sbuf(ctx, "going_on", [P, RT])
                first_key = sbuf(ctx, "lane_key", [P, 1])
                first_i = sbuf(ctx, "lane_key_i", [P, 1], I32)
                first_q = sbuf(ctx, "lane_q", [P, DK])
                ps_low = psum(ctx, "ps_low", [P, 512])
                ps_sofar = psum(ctx, "ps_sofar", [P, 512])
                ps_pick = psum(ctx, "ps_pick", [P, 2, 512])
                row_in = sems("row_in0", "row_in1")
                rows_used = sems("rows_used0", "rows_used1")
                pick_ready = sems("pick_ready0", "pick_ready1")
                sent = sems(*[f"sent{n}" for n in range(4)])
                QL = 4
                KEYS_AT = NC - 4
                place_ready, q_in, q_chain, counted, low_ready, first_ready_q, first_q_in = sems(
                    "place_ready", "q_in", "q_chain", "counted", "low_ready", "first_ready_q", "first_q_in")
                hots_ready, base_ready, added, sofar_ready, p_chain, rec_staged = sems(
                    "hots_ready", "base_ready", "added", "sofar_ready", "p_chain", "rec_staged")
                mark_staged, marks_out, base_i_ready = sems("mark_staged", "marks_out", "base_i_ready")
                block = ctx.enter_context(nc.Block())

                @block.sync
                def _(sp):
                    def load(a):
                        s = a.slot(2)
                        wait_slot(sp, rows_used[s], a, 2, C)
                        for t, dram in ((key_row, keyrow_dram), (lo_row, lorow_dram)):
                            sp.dma_start(t[:, s].rearrange("p j e -> p (j e)"),
                                         dram[ds(a.t * C, C), :].rearrange("(o j) e -> o (j e)", o=1)
                                         .broadcast_to([P, C * P])).then_inc(row_in[s], 16)

                    walk(sp, NC, load)

                @block.gpsimd
                def _(pool):
                    with pool.Fori(0, 2) as way:
                        pool.wait_ge(mark_staged, way + 1)
                        pool.sem_inc(pool_turn, 1)
                        for b in range(NB):
                            pool.indirect_dma_start(starts_dram[:, :], bass.IndirectOffsetOnAxis(ap=mark_st[:, b:b + 1], axis=0),
                                                    start[:, b, :], None).then_inc(marks_out, 16)

                    def send(a):
                        s = a.slot(4)
                        if isinstance(a.t, int) and a.t == KEYS_AT:
                            pool.wait_ge(first_ready_q, 1)
                            pool.sem_inc(pool_turn, 1)
                            pool.indirect_dma_start(first_q[:], None, q_dram[:, :],
                                                    bass.IndirectOffsetOnAxis(ap=first_i[:, 0:1], axis=0)).then_inc(first_q_in, 16)
                        pool.wait_ge(place_ready, a.t + 1)
                        pool.wait_ge(rec_staged, a.t + 1)
                        pool.sem_inc(pool_turn, 1)
                        for j in range(C):
                            pool.indirect_dma_start(rec_dram[:, :], bass.IndirectOffsetOnAxis(ap=place[:, s, j:j + 1], axis=0),
                                                    rec_st[:, s, j, :], None).then_inc(sent[s], 16)

                    walk(pool, NC, send)
                    for s in range(4):
                        pool.wait_ge(sent[s], 16 * C * (NC // 4))
                    pool.wait_ge(marks_out, 16 * KB)

                @block.vector
                def _(dve):
                    dve.tensor_scalar(base_g[:], row_base[:], float(G), None, ALU.mult).then_inc(base_ready, 1)
                    dve.tensor_copy(base_i[:], row_base[:]).then_inc(base_i_ready, 1)
                    dve.wait_ge(base_i_ready, 1)
                    for way in range(2):
                        if way:
                            dve.wait_ge(marks_out, 16 * NB)
                        dve.tensor_copy(mark_st[:], base_i[:, way * NB:(way + 1) * NB]).then_inc(mark_staged, 1)

                    def compare(a):
                        s, last = a.slot(2), a + -1
                        dve.wait_ge(row_in[s], (a.turn(2) + 1) * 32)
                        wait_slot(dve, pick_ready[s], a, 2)
                        dve.tensor_scalar(lo_hot_t[:, s], lo_row[:, s], lane_col[:, 0:1], None, ALU.is_equal).then_inc(hots_ready, 1)
                        dve.tensor_tensor(lo_hot[:, s], lane[:, 0:P].unsqueeze(1).broadcast_to([P, C, P]),
                                          lo_f[:, ds(a.t * C, C)].unsqueeze(2).broadcast_to([P, C, P]),
                                          ALU.is_equal).then_inc(hots_ready, 1)
                        dve.tensor_tensor(hi_hot[:, s], lane[:, 0:KB].unsqueeze(1).broadcast_to([P, C, KB]),
                                          hi_f[:, ds(a.t * C, C)].unsqueeze(2).broadcast_to([P, C, KB]),
                                          ALU.is_equal).then_inc(hots_ready, 1)
                        if a.c:
                            dve.wait_ge(rows_used[last.slot(2)], (last.turn(2) + 1) * C)
                        wait_done(dve, place_ready, a, 2)
                        for j in range(C):
                            dve.scalar_tensor_tensor(same[:, j], key_row[:, s, j, :], key_f[:, ds(a.t * C + j, 1)], after[:],
                                                     ALU.is_equal, ALU.mult, accum_out=rank[:, s, j:j + 1]).then_inc(rows_used[s], 1)

                    def settle(a):
                        s = a.slot(2)
                        link = Chain(dve, p_chain, a.t * 2)
                        dve.wait_ge(pick_ready[s], a.turn(2) + 1)
                        link(dve.tensor_tensor(picked[:], ps_pick[:, s, 0:C * KB].rearrange("p (j b) -> p j b", j=C), hi_hot[:, s], ALU.mult))
                        wait_done(dve, place_ready, a, 1)
                        link(dve.tensor_reduce(seen[:], picked[:], AX, ALU.add))
                        dve.wait_ge(rows_used[s], (a.turn(2) + 1) * C)
                        wait_slot(dve, sent[a.slot(4)], a, 4, 16 * C)
                        dve.tensor_tensor(place[:, a.slot(4)], seen[:], rank[:, s], ALU.add).then_inc(place_ready, 1)

                    def find_keys():
                        link = Chain(dve, q_chain)
                        dve.wait_ge(q_in, 16 * (1 + QL))
                        link(dve.tensor_copy(marks[:], q_all[:, :, 0]))
                        link(dve.tensor_copy(marks_next[:, 0:RT - 1], marks[:, 1:RT]))
                        link(dve.tensor_tensor_scan(key_of[:], ones[:, 0:1].broadcast_to([P, RT]), marks[:], 0.0, ALU.mult, ALU.add))
                        dve.tensor_copy(low_rows[:], key_of[:, RT - 1:RT]).then_inc(counted, 1)
                        dve.wait_ge(low_ready, 1)
                        dve.wait_ge(counted, 1)
                        link(dve.tensor_scalar(low_rows[:], ps_low[:, 0:1], -1.0, None, ALU.add))
                        link(dve.tensor_scalar(key_of[:], key_of[:], low_rows[:, 0:1], None, ALU.add))
                        link(dve.tensor_scalar(first_key[:], key_of[:, 0:1], float(NPAD), float(-NPAD), ALU.is_ge, ALU.mult))
                        dve.tensor_tensor(first_i[:], first_key[:], key_of[:, 0:1], ALU.add).then_inc(first_ready_q, 1)
                        link(dve.tensor_scalar(going_on[:], marks[:], -1.0, 1.0, ALU.mult, ALU.add))

                    def step(a):
                        if not isinstance(a.t, int) or a.t + 1 < NC:
                            compare(a + 1)
                        settle(a)
                        if isinstance(a.t, int) and a.t == KEYS_AT:
                            find_keys()

                    compare(At(0, 0))
                    walk(dve, NC, step)
                    dve.wait_ge(first_q_in, 16)
                    for c in range(DK):
                        col = q_all[:, :, 1 + c]
                        dve.tensor_tensor_scan(col, going_on[:], col, first_q[:, c:c + 1], ALU.mult, ALU.add)

                @block.scalar
                def _(act):
                    act.wait_ge(added, 1)
                    act.copy(so_far[:, 0, :], ps_sofar[:, 0:KB]).then_inc(sofar_ready, 1)

                    def copy_counts(a):
                        if isinstance(a.t, int) and a.t == 3:
                            act.wait_ge(marks_out, 16 * KB)
                            for n in range(QL):
                                cut = slice(n * RT // QL, (n + 1) * RT // QL)
                                act.dma_start(q_all[:, cut, :], starts_dram[0:NR, :].rearrange("(p i) c -> p i c", p=P)[:, cut, :]).then_inc(q_in, 16)
                            act.dma_start(marks_next[:, RT - 1:RT], starts_dram[1:NR + 1, :].rearrange("(p i) c -> p i c", p=P)[:, RT - 1, 0:1], allow_slow_non_contiguous=True).then_inc(q_in, 16)
                        wait_slot(act, sent[a.slot(4)], a, 4, 16 * C)
                        act.copy(rec_st[:, a.slot(4)], rec[:, ds(a.t * C, C), :]).then_inc(rec_staged, 1)
                        for j in range(C):
                            act.wait_ge(added, a.t * C + j + 2)
                            act.copy(so_far[:, (j + 1) % 2, :], ps_sofar[:, 0:KB]).then_inc(sofar_ready, 1)

                    walk(act, NC, copy_counts)

                @block.tensor
                def _(pe):
                    pe.wait_ge(base_ready, 1)
                    pe.matmul(ps_sofar[:, 0:KB], ident[:], base_g[:], start=True, stop=False, skip_group_check=True).then_inc(added, 1)

                    def count(a):
                        s = a.slot(2)
                        pe.wait_ge(hots_ready, a.t * 3 + 3)
                        wait_done(pe, place_ready, a, 2)
                        for j in range(C):
                            pe.wait_ge(sofar_ready, a.t * C + j + 1)
                            pe.matmul(ps_sofar[:, 0:KB], lo_hot[:, s, j, :], hi_hot[:, s, j, :], start=False, stop=False,
                                      skip_group_check=True).then_inc(added, 1)
                            last = pe.matmul(ps_pick[:, s, j * KB:(j + 1) * KB], lo_hot_t[:, s, j, :], so_far[:, j % 2, :],
                                             start=True, stop=True)
                        last.then_inc(pick_ready[s], 1)
                        if isinstance(a.t, int) and a.t == KEYS_AT + 1:
                            pe.wait_ge(counted, 1)
                            pe.matmul(ps_low[:, 0:1], before[:], low_rows[:], start=True, stop=True).then_inc(low_ready, 1)

                    walk(pe, NC, count)

        row_max = sbuf(rows, "row_max", [P, RT, H])
        with ExitStack() as ctx:
            AHEAD = 10
            rec = sbuf(ctx, "rec_rows", [P, RT + AHEAD, G * 4])
            gidx = sbuf(ctx, "gidx", [P, RT + R, G], I32)
            mask = sbuf(ctx, "mask", [P, RT, G])
            w_row = sbuf(ctx, "w_row", [1, TD])
            b_row = sbuf(ctx, "b_row", [1, 3, TD])
            time_w = sbuf(ctx, "time_w", [G * 4, G * 3 * TD])
            idx_st = sbuf(ctx, "idx_st", [P, R, G], I32)
            rec_st = sbuf(ctx, "rec_row_st", [P, R, G * 4])
            rec_t = sbuf(ctx, "rec_t", [G * 4, 2, P])
            turns = sbuf(ctx, "turns", [P, 2, G * 3 * TD])
            phase = sbuf(ctx, "phase", [P, 4, G * 3 * TD])
            emb = sbuf(ctx, "emb", [P, 4, G * 3 * TD])
            kv = sbuf(ctx, "kv", [P, R, G, 2 * H * DK])
            q_emb = sbuf(ctx, "q_emb", [P, 2, G, DK])
            prod = sbuf(ctx, "prod", [P, G, H * DK])
            q_sum = sbuf(ctx, "q_sum", [P, G, DK])
            att = sbuf(ctx, "att", [P, G, H])
            att_m = sbuf(ctx, "att_m", [P, G + 1, H])
            drop = sbuf(ctx, "drop", [P, 2, G, H])
            msg = xn[:].rearrange("p b c -> p (b c)")[:, 0:R * G * d.MSG].rearrange("p (s g c) -> p s g c", s=R, g=G)
            msg_out = sbuf(ctx, "msg_out", [P, 2, d.MSG])
            ps_rt = psum(ctx, "ps_rt", [P, 2, 512])
            ps_turns = psum(ctx, "ps_turns", [P, 2, 512])
            ps_sum = psum(ctx, "ps_sum", [P, 2, 512])
            r_clear, r_in, r_chain, w_in2, w_scaled, w_clear, w_placed = sems(
                "r_clear", "r_in", "r_chain", "w_in2", "w_scaled", "w_clear", "w_placed")
            rows_set, = sems("rows_set")
            staged, rt_turned, rt_copied, turns_ready, rounded, phase_ready = sems(
                "staged", "rt_turned", "rt_copied", "turns_ready", "rounded", "phase_ready")
            rec_ready, sines_done = sems("rec_ready", "sines_done")
            emb_ready, weight_ready, sum_ready, sum_copied, q_summed = sems(
                "emb_ready", "weight_ready", "sum_ready", "sum_copied", "q_summed")
            scored, reduced, masked, topped, dropped = sems("scored", "reduced", "masked", "topped", "dropped")
            msg_ready = sems(*[f"msg_ready{n}" for n in range(R)])
            kv_in = sems(*[f"kv_in{n}" for n in range(R)])
            msg_stored = sems("msg_stored0", "msg_stored1")
            block = ctx.enter_context(nc.Block())

            @block.sync
            def _(sp):
                sp.dma_start(rec[:, 0:RT, :].rearrange("p i w -> p (i w)"),
                             rec_dram.rearrange("(p i) w -> p (i w)", p=P)).then_inc(r_in, 16)
                sp.dma_start(w_row[:], w_time.rearrange("(o n) -> o n", o=1)).then_inc(w_in2, 16)
                for n in range(3):
                    sp.dma_start(b_row[:, n, :], b_time.rearrange("(o n) -> o n", o=1)).then_inc(w_in2, 16)
                sp.wait_ge(w_scaled, 2)
                sp.wait_ge(w_clear, 1)
                for g in range(G):
                    at = g * 3 * TD
                    sp.dma_start(time_w[g * 4:g * 4 + 1, at:at + 3 * TD], b_row[:].rearrange("p n t -> p (n t)")).then_inc(w_placed, 16)
                    for n in range(3):
                        sp.dma_start(time_w[g * 4 + 1 + n:g * 4 + 2 + n, at + n * TD:at + (n + 1) * TD], w_row[:]).then_inc(w_placed, 16)

                def store(a):
                    sp.wait_ge(sum_copied, a.t + 1)
                    sp.dma_start(part_dram.rearrange("(p i) c -> p i c", p=P)[:, ds(a.t, 1), :].rearrange("p i c -> p (i c)"),
                                 msg_out[:, a.slot(2), :]).then_inc(msg_stored[a.slot(2)], 16)

                walk(sp, RT, store)
                for n in range(2):
                    sp.wait_ge(msg_stored[n], 16 * (RT // 2))

            @block.gpsimd
            def _(pool):
                pool.memset(rec[:, RT:, :], 0.0).then_inc(r_clear, 1)
                pool.memset(gidx[:, RT:, :], 0).then_inc(r_clear, 1)
                pool.memset(time_w[:], 0.0).then_inc(w_clear, 1)
                pool.memset(q_emb[:, :, :, 0:LAST], 0.0).then_inc(r_clear, 1)
                pool.memset(att_m[:, G, :], -BIG / 10).then_inc(r_clear, 1)

                def gather(a):
                    s = a.slot(R)
                    pool.wait_ge(staged, a.t + 1)
                    wait_slot(pool, msg_ready[s], a, R)
                    pool.sem_inc(pool_turn, 1)
                    for g in range(G):
                        pool.indirect_dma_start(kv[:, s, g, 0:KVW], None, kv_dram[:, :],
                                                bass.IndirectOffsetOnAxis(ap=idx_st[:, s, g:g + 1], axis=0)).then_inc(kv_in[s], 16)

                walk(pool, RT, gather)

            @block.vector
            def _(dve):
                link = Chain(dve, r_chain)
                dve.wait_ge(w_in2, 64)
                dve.tensor_scalar(w_row[:], w_row[:], 1.0 / TWO_PI, None, ALU.mult).then_inc(w_scaled, 1)
                dve.tensor_scalar(b_row[:], b_row[:], 1.0 / TWO_PI, 0.25, ALU.mult, ALU.add).then_inc(w_scaled, 1)
                dve.wait_ge(r_in, 16)
                dve.wait_ge(r_clear, 4)
                words = rec[:, 0:RT, :].rearrange("p i (g w) -> p i g w", w=4)[:, :, :, 0]
                link(dve.tensor_copy(gidx[:, 0:RT, :], words))
                link(dve.tensor_scalar(words, words, 1.0, None, ALU.min))
                dve.tensor_scalar(mask[:], words, -1.0, BIG, ALU.add, ALU.mult).then_inc(rows_set, 1)

                def find_phase(a):
                    wait_done(dve, rounded, a)
                    wait_slot(dve, sines_done, a, 4)
                    h = a.slot(2)
                    dve.scalar_tensor_tensor(phase[:, a.slot(4)], turns[:, h], MAGIC, ps_turns[:, h, 0:G * 3 * TD],
                                             ALU.subtract, ALU.subtract).then_inc(phase_ready, 1)

                def step(a):
                    s = a.slot(R)
                    wait_done(dve, emb_ready, a)
                    wait_done(dve, scored, a, 1)
                    add_q(a)
                    if a.c:
                        mask_att(a + -1)
                    late = a.c % 4 == 3
                    if not late:
                        find_phase(a + 5)
                    if a.c:
                        find_top(a + -1)
                    dve.wait_ge(kv_in[s], (a.turn(R) + 1) * 16 * G)
                    wait_done(dve, q_summed, a)
                    dve.tensor_tensor(prod[:].rearrange("p g (h c) -> p g h c", h=H),
                                      kv[:, s, :, 0:H * DK].rearrange("p g (h c) -> p g h c", h=H),
                                      q_sum[:].unsqueeze(2).broadcast_to([P, G, H, DK]), ALU.mult).then_inc(scored, 1)
                    if a.c:
                        subtract_top(a + -1)
                    if late:
                        find_phase(a + 5)
                    wait_done(dve, scored, a)
                    dve.tensor_reduce(att[:], prod[:].rearrange("p g (h c) -> p g h c", h=H), AX, ALU.add).then_inc(reduced, 1)
                    if a.c:
                        weigh(a + -1)

                def add_q(a):
                    dve.tensor_tensor(q_sum[:], q_emb[:, a.slot(2)], q_all[:, ds(a.t, 1), 1:].broadcast_to([P, G, DK]),
                                      ALU.add).then_inc(q_summed, 1)

                def mask_att(a):
                    wait_done(dve, reduced, a)
                    wait_done(dve, dropped, a, 1)
                    dve.tensor_tensor(att_m[:, 0:G, :], att[:], mask[:, ds(a.t, 1), :].rearrange("p i g -> p (i g)").unsqueeze(2)
                                      .broadcast_to([P, G, H]), ALU.add).then_inc(masked, 1)

                def top_of(a):
                    return row_max[:, ds(a.t, 1), :].rearrange("p i h -> p (i h)")

                def find_top(a):
                    wait_done(dve, masked, a)
                    dve.tensor_reduce(top_of(a), att_m[:].rearrange("p g h -> p h g"), AX, ALU.max).then_inc(topped, 1)

                def subtract_top(a):
                    wait_done(dve, topped, a)
                    wait_done(dve, weight_ready, a, 2)
                    dve.tensor_tensor(drop[:, a.slot(2)], att_m[:, 0:G, :], top_of(a).unsqueeze(1).broadcast_to([P, G, H]),
                                      ALU.subtract).then_inc(dropped, 1)

                def weigh(a):
                    s = a.slot(R)
                    wait_done(dve, weight_ready, a)
                    dve.tensor_tensor(msg[:, s, :, 0:H * DK].rearrange("p g (h c) -> p g h c", h=H),
                                      kv[:, s, :, H * DK:].rearrange("p g (h c) -> p g h c", h=H),
                                      msg[:, s, :, D:].unsqueeze(3).broadcast_to([P, G, H, DK]), ALU.mult).then_inc(msg_ready[s], 1)

                for t in range(5):
                    find_phase(At(0, t))
                walk(dve, RT, step)
                last = At(0, RT - 1)
                mask_att(last)
                find_top(last)
                subtract_top(last)
                weigh(last)

            @block.scalar
            def _(act):
                def stage(a):
                    wait_slot(act, kv_in[a.slot(R)], a, R, 16 * G)
                    act.copy(idx_st[:, a.slot(R), :], gidx[:, ds(a.t, 1), :].rearrange("p i g -> p (i g)")).then_inc(staged, 1)

                def stage_rec(a):
                    wait_done(act, rt_turned, a, 4)
                    act.copy(rec_st[:, a.slot(4), :], rec[:, ds(a.t, 1), :].rearrange("p i g -> p (i g)")).then_inc(rec_ready, 1)

                def copy_rt(a):
                    wait_done(act, rt_turned, a)
                    wait_done(act, turns_ready, a, 2)
                    act.copy(rec_t[:, a.slot(2), :], ps_rt[0:G * 4, a.slot(2), 0:P]).then_inc(rt_copied, 1)

                def round_turns(a):
                    wait_done(act, turns_ready, a)
                    wait_done(act, phase_ready, a, 2)
                    act.activation(turns[:, a.slot(2)], ps_turns[:, a.slot(2), 0:G * 3 * TD], ACT.Identity,
                                   bias=magic[:, 0:1]).then_inc(rounded, 1)

                def sines(a):
                    wait_done(act, phase_ready, a + 3)
                    if a.c >= 4:
                        act.wait_ge(emb_ready, a.t)
                    act.activation(emb[:].rearrange("p s c -> p (s c)"), phase[:].rearrange("p s c -> p (s c)"), ACT.Sin,
                                   scale=-SIN_SCALE).then_inc(sines_done, 1)

                def embed(a):
                    s, h = a.slot(R), a.slot(2)
                    act.wait_ge(sines_done, a.turn(4) + 1)
                    wait_done(act, sum_ready, a, R)
                    at = emb[:, a.slot(4)].rearrange("p (g n t) -> p n g t", g=G, n=3)
                    act.copy(msg[:, s, :, H * DK:D], at[:, 0])
                    wait_done(act, q_summed, a, 2)
                    act.copy(q_emb[:, h, :, LAST:], at[:, 2])
                    act.wait_ge(kv_in[s], (a.turn(R) + 1) * 16 * G)
                    act.copy(kv[:, s].rearrange("p g (n c) -> p g n c", n=2)[:, :, :, PROJ:],
                             at[:, 1].unsqueeze(2).broadcast_to([P, G, 2, TD])).then_inc(emb_ready, 1)

                def exps(a):
                    wait_done(act, dropped, a)
                    act.activation(msg[:, a.slot(R), :, D:], drop[:, a.slot(2)], ACT.Exp, scale=float(DK) ** -0.5).then_inc(weight_ready, 1)

                def copy_sum(a):
                    wait_done(act, sum_ready, a)
                    wait_slot(act, msg_stored[a.slot(2)], a, 2, 16)
                    act.copy(msg_out[:, a.slot(2), :], ps_sum[:, a.slot(2), 0:d.MSG]).then_inc(sum_copied, 1)

                def step(a):
                    exps(a)
                    stage(a + 4)
                    if not isinstance(a.t, int) or a.t + 2 < RT:
                        embed(a + 2)
                    round_turns(a + 7)
                    if a.c % 4 == 1:
                        sines(a + 3)
                    stage_rec(a + 10)
                    copy_rt(a + 8)
                    if a.c >= 2:
                        copy_sum(a + -2)

                act.wait_ge(rows_set, 1)
                for t in range(4):
                    stage(At(0, t))
                    stage_rec(At(0, t))
                for t in range(8):
                    copy_rt(At(0, t))
                    if t < 6:
                        stage_rec(At(0, t + 4))
                    if t:
                        round_turns(At(0, t - 1))
                    if t == 5:
                        sines(At(0, 0))
                for t in range(2):
                    embed(At(0, t))
                walk(act, RT, step)
                copy_sum(At(0, RT - 2))
                copy_sum(At(0, RT - 1))

            @block.tensor
            def _(pe):
                pe.wait_ge(w_placed, 16 * G * 4)

                def turn_rec(a):
                    wait_done(pe, rec_ready, a)
                    wait_done(pe, rt_copied, a, 2)
                    pe.transpose(ps_rt[0:G * 4, a.slot(2), 0:P], rec_st[:, a.slot(4), :], ident[:]).then_inc(rt_turned, 1)

                def multiply(a):
                    wait_done(pe, rt_copied, a)
                    wait_done(pe, phase_ready, a, 2)
                    pe.matmul(ps_turns[:, a.slot(2), 0:G * 3 * TD], rec_t[:, a.slot(2), :], time_w[:], start=True,
                              stop=True).then_inc(turns_ready, 1)

                def add_up(a):
                    pe.wait_ge(msg_ready[a.slot(R)], a.turn(R) + 1)
                    wait_done(pe, sum_copied, a, 2)
                    for g in range(G):
                        last = pe.matmul(ps_sum[:, a.slot(2), 0:d.MSG], ident[:], msg[:, a.slot(R), g, :], start=(g == 0), stop=(g == G - 1))
                    last.then_inc(sum_ready, 1)

                def step(a):
                    multiply(a + 7)
                    turn_rec(a + 9)
                    if a.c:
                        add_up(a + -1)

                for t in range(9):
                    turn_rec(At(0, t))
                    if t >= 2:
                        multiply(At(0, t - 2))
                walk(pe, RT, step)
                add_up(At(0, RT - 1))

        nodes = ExitStack()
        wa = sbuf(nodes, "wa", [P, T * KD, D])
        wa_of = wa[:].rearrange("p (t k) c -> p t k c", k=KD)
        wa_more = xn[:].rearrange("p b c -> p (b c)")[:, 0:T * D].rearrange("p (t c) -> p t c", t=T)

        with ExitStack() as ctx:
            fall = sbuf(ctx, "fall", [P, 2, RT])
            lane_fall = sbuf(ctx, "lane_fall", [P, 2])
            flow = sbuf(ctx, "flow", [P, 2, H, RT])
            ends_of = sbuf(ctx, "ends_of", [P, 2, 2, H])
            across = sbuf(ctx, "across", [H, 2, P + 1])
            across_in = sbuf(ctx, "across_in", [H, 2, 2, P])
            carry = sbuf(ctx, "carry", [P, 2, H])
            below = sbuf(ctx, "below", [P, RT, H])
            share = sbuf(ctx, "share", [P, RT, H + 1])
            ps_lane = psum(ctx, "ps_lane", [P, 4, 512])
            s_chain, lanes_set, lanes_turned, carry_set, carry_turned, below_ready, share_ready, share_out = sems(
                "s_chain", "lanes_set", "lanes_turned", "carry_set", "carry_turned", "below_ready", "share_ready", "share_out")
            wa_in, wa_folded = sems("wa_in", "wa_folded")
            block = ctx.enter_context(nc.Block())

            @block.gpsimd
            def _(pool):
                for k in range(KD):
                    pool.dma_start(wa_of[:, :, k, :], Wa[:, k * P:(k + 1) * P, :].rearrange("t p c -> p t c")).then_inc(wa_in, 16)
                pool.dma_start(wa_more, Wa[:, D:D + P, :].rearrange("t p c -> p t c")).then_inc(wa_in, 16)
                pool.wait_ge(wa_in, 16 * (KD + 1))

            @block.vector
            def _(dve):
                link = Chain(dve, s_chain)
                link(dve.tensor_scalar(fall[:, 0], marks[:], RESET, None, ALU.mult))
                link(dve.tensor_scalar(fall[:, 1], marks_next[:], RESET, None, ALU.mult))
                link(dve.tensor_reduce(lane_fall[:], fall[:], AX, ALU.min))
                link(dve.memset(across[:], RESET / 2))
                for n in range(2):
                    order = slice(None, None, -1) if n else slice(None)
                    edge = 0 if n else RT - 1

                    def scan(start):
                        for h in range(H):
                            src_t = flow[:, 0, h, order] if n else row_max[:, :, h]
                            last = dve.tensor_tensor_scan(flow[:, n, h, order], fall[:, n, order], src_t, start(h), ALU.add, ALU.max)
                        link(last)

                    scan(lambda h: RESET / 2)
                    link(dve.tensor_copy(ends_of[:, n, 0, :], flow[:, n, :, edge]))
                    dve.tensor_copy(ends_of[:, n, 1, :], lane_fall[:, n:n + 1].broadcast_to([P, H])).then_inc(lanes_set, 1)
                    dve.wait_ge(lanes_turned, n + 1)
                    for w in range(2):
                        link(dve.tensor_copy(across_in[:, n, w, :], ps_lane[0:H, w, 0:P]))
                    kept = across[:, n, 0:P][:, order] if n else across[:, n, 1:P + 1]
                    dve.tensor_tensor_scan(kept, across_in[:, n, 1, order], across_in[:, n, 0, order], RESET / 2,
                                           ALU.add, ALU.max).then_inc(carry_set, 1)
                    dve.wait_ge(carry_turned, n + 1)
                    link(dve.tensor_copy(carry[:, n, :], ps_lane[:, 2, 0:H]))
                    scan(lambda h: carry[:, n, h:h + 1])
                dve.tensor_tensor(below[:], row_max[:], flow[:, 1].rearrange("p h i -> p i h"), ALU.subtract).then_inc(below_ready, 1)
                dve.tensor_copy(share[:, :, H], key_of[:]).then_inc(share_ready, 1)

            @block.tensor
            def _(pe):
                for n in range(2):
                    pe.wait_ge(lanes_set, n + 1)
                    for w in range(2):
                        last = pe.transpose(ps_lane[0:H, w, 0:P], ends_of[:, n, w, :], ident[:])
                    last.then_inc(lanes_turned, 1)
                    pe.wait_ge(carry_set, n + 1)
                    pe.transpose(ps_lane[:, 2, 0:H], across[:, n, 1:P + 1] if n else across[:, n, 0:P], ident[0:H, 0:H]).then_inc(carry_turned, 1)

            @block.scalar
            def _(act):
                act.wait_ge(below_ready, 1)
                act.activation(share[:, :, 0:H], below[:], ACT.Exp, scale=float(DK) ** -0.5).then_inc(share_ready, 1)

            @block.sync
            def _(sp):
                sp.wait_ge(share_ready, 2)
                sp.dma_start(wk_dram.rearrange("(p i) c -> p (i c)", p=P), share[:].rearrange("p i c -> p (i c)")).then_inc(share_out, 16)
                sp.wait_ge(share_out, 16)

        with nodes:
            agg = sbuf(nodes, "agg", [P, NB, D])
            with ExitStack() as ctx:
                acc = q_all[:].rearrange("p i c -> p (i c)")[:, 0:(KB + 1) * d.MSG].rearrange("p (b c) -> p b c", c=d.MSG)
                first_key = sbuf(ctx, "first_key", [1, RT])
                first_i = sbuf(ctx, "first_i", [1, RT], I32)
                block_i = sbuf(ctx, "block_i", [1, RT], I32)
                block_key = sbuf(ctx, "block_key", [1, RT])
                block_key_bc = sbuf(ctx, "block_key_bc", [P, RT])
                part = sbuf(ctx, "part", [P, 4, 2, d.MSG])
                wk = sbuf(ctx, "wk", [P, 4, 2, H + 1])
                key_hot = sbuf(ctx, "key_hot", [P, 4, 2, 2 * P])
                total = sbuf(ctx, "total", [P, KB, H])
                ps_bc = psum(ctx, "ps_bc", [P, 512])
                ps_key = psum(ctx, "ps_key", [P, 2, 2, 512])
                k_in, k_chain, first_ready, bc_ready, acc_clear = sems("k_in", "k_chain", "first_ready", "bc_ready", "acc_clear")
                sums_ready, rows_placed = sems("sums_ready", "rows_placed")
                part_in = sems(*[f"part_in{n}" for n in range(4)])
                part_ready, key_summed, key_added, tile_chain = sems("part_ready", "key_summed", "key_added", "tile_chain")
                block = ctx.enter_context(nc.Block())

                def wait_slot_pair(eng, sem, a):
                    if a.c >= 4:
                        eng.wait_ge(sem, a.t * 2 - 6)

                @block.sync
                def _(sp):
                    sp.dma_start(first_key[:], wk_dram.rearrange("(i p) c -> c p i", p=P)[H:H + 1, 0, :],
                                 allow_slow_non_contiguous=True).then_inc(k_in, 16)

                    def load(a):
                        s = a.slot(4)
                        wait_slot_pair(sp, key_summed, a)
                        for t, dram in ((part, part_dram), (wk, wk_dram)):
                            sp.dma_start(t[:, s], dram[ds(a.t * 2 * P, 2 * P), :].rearrange("(n p) c -> p n c", p=P)).then_inc(part_in[s], 16)

                    walk(sp, RT // 2, load)

                @block.gpsimd
                def _(pool):
                    pool.memset(acc, 0.0).then_inc(acc_clear, 1)

                    def weigh_sums(a):
                        s = a.slot(4)
                        pool.wait_ge(part_in[s], (a.turn(4) + 1) * 32)
                        pool.tensor_tensor(part[:, s, :, D:], part[:, s, :, D:], wk[:, s, :, 0:H], ALU.mult).then_inc(sums_ready, 1)
                        if isinstance(a.t, int) and a.t == 3:
                            pool.wait_ge(wa_folded, 1)
                            pool.dma_start(wa_more, Wa[:, D + P:D + 2 * P, :].rearrange("t p c -> p t c")).then_inc(wa_in, 16)

                    walk(pool, RT // 2, weigh_sums)

                @block.scalar
                def _(act):
                    def weigh(a):
                        s = a.slot(4)
                        act.wait_ge(part_in[s], (a.turn(4) + 1) * 32)
                        for n in range(2):
                            for h in range(H):
                                cols = part[:, s, n, h * DK:(h + 1) * DK]
                                last = act.activation(cols, cols, ACT.Copy, scale=wk[:, s, n, h:h + 1])
                            last.then_inc(part_ready, 1)

                    walk(act, RT // 2, weigh)

                @block.vector
                def _(dve):
                    link = Chain(dve, k_chain)
                    dve.wait_ge(k_in, 16)
                    link(dve.tensor_copy(first_i[:], first_key[:]))
                    link(dve.tensor_scalar(block_i[:], first_i[:], 7, None, ALU.arith_shift_right))
                    dve.tensor_scalar(block_key[:], block_i[:], float(P), None, ALU.mult).then_inc(first_ready, 1)
                    dve.wait_ge(bc_ready, 1)
                    link(dve.tensor_copy(block_key_bc[:], ps_bc[:, 0:RT]))
                    dve.wait_ge(acc_clear, 1)

                    def add(a):
                        for n in range(2):
                            t = a.t * 2 + n
                            at = dve.value_load(block_i[0:1, ds(t, 1)], min_val=0, max_val=KB - 1)
                            dve.wait_ge(key_summed, t + 1)
                            if a.c or n:
                                dve.wait_ge(key_added, t)
                            dve.tensor_tensor(acc[:, ds(at, 2), :], acc[:, ds(at, 2), :], ps_key[:, n, :, 0:d.MSG],
                                              ALU.add).then_inc(key_added, 1)

                    def place_rows(a):
                        s = a.slot(4)
                        dve.wait_ge(part_in[s], (a.turn(4) + 1) * 32)
                        wait_slot_pair(dve, key_summed, a)
                        for n in range(2):
                            dve.tensor_scalar(key_hot[:, s, n], lane[:], block_key_bc[:, ds(a.t * 2 + n, 1)], wk[:, s, n, H:H + 1],
                                              ALU.add, ALU.is_equal).then_inc(rows_placed, 1)

                    def step(a):
                        if not isinstance(a.t, int) or a.t + 1 < RT // 2:
                            place_rows(a + 1)
                        add(a)
                        if isinstance(a.t, int) and a.t in (3, RT // 2 - 2):
                            k = int(a.t != 3)
                            dve.wait_ge(wa_in, 16 * (KD + 1 + k))
                            dve.tensor_tensor(wa_of[:, :, k, :], wa_of[:, :, k, :], wa_more, ALU.add).then_inc(wa_folded, 1)

                    place_rows(At(0, 0))
                    walk(dve, RT // 2, step)
                    dve.wait_ge(key_added, RT)
                    dve.wait_ge(wa_folded, KD)
                    link(dve.tensor_scalar(total[:], acc[:, 0:KB, D:], 1e-16, None, ALU.add))
                    link(dve.reciprocal(total[:], total[:]))
                    heads = acc[:, 0:KB, 0:3 * DK].rearrange("p b (h c) -> p b h c", h=3)
                    link(dve.tensor_tensor(heads, heads, total[:, :, 0:3].unsqueeze(3).broadcast_to([P, KB, 3, DK]), ALU.mult))
                    link(dve.tensor_tensor(acc[:, 0:KB, 3 * DK:H * DK], acc[:, 0:KB, 3 * DK:H * DK],
                                           total[:, :, 3:4].broadcast_to([P, KB, DK]), ALU.mult))
                    link(dve.tensor_tensor(agg[:], acc[:, 0:NB, 0:D], acc[:, NB:KB, 0:D], ALU.add))

                @block.tensor
                def _(pe):
                    pe.wait_ge(first_ready, 1)
                    pe.matmul(ps_bc[:, 0:RT], ones[0:1, :], block_key[:], start=True, stop=True).then_inc(bc_ready, 1)

                    def sum_rows(a):
                        s = a.slot(4)
                        wait_done(pe, sums_ready, a)
                        for n in range(2):
                            t = a.t * 2 + n
                            pe.wait_ge(part_ready, t + 1)
                            pe.wait_ge(rows_placed, t + 1)
                            if a.c:
                                pe.wait_ge(key_added, t - 1)
                            for m in range(2):
                                last = pe.matmul(ps_key[:, n, m, 0:d.MSG], key_hot[:, s, n, m * P:(m + 1) * P], part[:, s, n, :],
                                                 start=True, stop=True)
                            last.then_inc(key_summed, 1)

                    walk(pe, RT // 2, sum_rows)

            with ExitStack() as ctx:
                vecs = sbuf(ctx, "vecs", [T, 2, D])
                types = sbuf(ctx, "types", [T, NPAD], I32)
                onehot_st = sbuf(ctx, "onehot_a", [T, 2, P])
                free = q_all[:].rearrange("p i c -> p (i c)")
                nodes = free[:, 0:4 * D].rearrange("p (s c) -> p s c", s=4)
                x_t = free[:, 4 * D:6 * D].rearrange("p (s k c) -> p s k c", s=2, k=KD)
                y_out = free[:, 6 * D:8 * D].rearrange("p (s c) -> p s c", s=2)
                ba_all = free[:, 8 * D:(8 + T) * D].rearrange("p (t c) -> p t c", t=T)
                ps_t = psum(ctx, "ps_ta", [P, 2, 512])
                ps_o = psum(ctx, "ps_o", [P, 2, 512])
                ps_v = psum(ctx, "ps_v", [P, 2, 512])
                vecs_in, ba_in, types_clear, a_sent, a_back = sems("vecs_in", "ba_in", "types_clear", "a_sent", "a_back")
                a_turned, at_ready, y_ready, y_copied = sems("a_turned", "at_ready", "ya_ready", "ya_copied")
                a_chain, a_var, a_std, v_hot, v_ready, v_used = sems("a_chain", "a_var", "a_std", "v_hot", "v_ready", "v_used")
                v_scaled, = sems("v_scaled")
                xn_in, = sems("xn_in")
                a_in = sems(*[f"a_in{n}" for n in range(4)])
                y_stored = sems("ya_stored0", "ya_stored1")
                block = ctx.enter_context(nc.Block())

                @block.gpsimd
                def _(pool):
                    for b in range(NB):
                        pool.indirect_dma_start(typed_x_dram[:, :], bass.IndirectOffsetOnAxis(ap=type_row[:, b:b + 1], axis=0),
                                                agg[:, b, :], None).then_inc(a_sent, 16)
                    pool.memset(types[:], 0).then_inc(types_clear, 1)

                    def store(a):
                        h = a.slot(2)
                        pool.wait_ge(y_copied, a.t + 1)
                        pool.dma_start(typed_out_dram[ds(a.t * P, P), :], y_out[:, h, :]).then_inc(y_stored[h], 16)

                    walk(pool, TT, store)
                    pool.wait_ge(y_stored[0], 16 * (TT - TT // 2))
                    pool.wait_ge(y_stored[1], 16 * (TT // 2))
                    pool.sem_inc(pool_turn, 1)
                    for b in range(NB):
                        pool.indirect_dma_start(agg[:, b, :], None, typed_out_dram[:, :],
                                                bass.IndirectOffsetOnAxis(ap=type_row[:, b:b + 1], axis=0)).then_inc(a_back, 16)

                @block.sync
                def _(sp):
                    sp.dma_start(xn[:], xn_dram.rearrange("(b p) c -> p b c", p=P)).then_inc(xn_in, 16)
                    sp.dma_start(ba_all, ba.rearrange("(o t) c -> o t c", o=1).broadcast_to([P, T, D])).then_inc(ba_in, 16)
                    for n, v in enumerate((gamma, beta)):
                        sp.dma_start(vecs[:, n, :], v).then_inc(vecs_in, 16)
                    sp.wait_ge(types_clear, 1)
                    sp.dma_start(types[:, 0:N], node_type.rearrange("(o n) -> o n", o=1).broadcast_to([T, N])).then_inc(vecs_in, 16)
                    sp.wait_ge(a_sent, 16 * NB)

                    def load(a):
                        wait_done(sp, a_turned, a, 4)
                        sp.dma_start(nodes[:, a.slot(4), :], typed_x_dram[ds(a.t * P, P), :]).then_inc(a_in[a.slot(4)], 16)

                    walk(sp, TT, load)

                @block.scalar
                def _(act):
                    act.wait_ge(a_var, 1)
                    act.activation(rstd[:], tmp_b[:], ACT.Sqrt).then_inc(a_std, 1)

                @block.vector
                def _(dve):
                    link = Chain(dve, a_chain)

                    dve.wait_ge(ba_in, 16)

                    def copy_x(a):
                        h = a.slot(2)
                        wait_done(dve, a_turned, a)
                        wait_done(dve, y_ready, a, 2)
                        dve.tensor_copy(x_t[:, h].rearrange("p k c -> p (k c)"), ps_t[:, h, 0:D]).then_inc(at_ready, 1)

                    def add_bias(a):
                        ty = dve.value_load(tile_type_i[0:1, ds(a.t, 1)], min_val=0, max_val=T - 1)
                        h = a.slot(2)
                        wait_done(dve, y_ready, a)
                        wait_slot(dve, y_stored[h], a, 2, 16)
                        dve.tensor_tensor(y_out[:, h, :], ps_o[:, h, 0:D], ba_all[:, ds(ty, 1), :].rearrange("p o c -> p (o c)"),
                                          ALU.add).then_inc(y_copied, 1)

                    def turn_and_add(a):
                        copy_x(a)
                        if a.c:
                            add_bias(a + -1)

                    walk(dve, TT, turn_and_add)
                    add_bias(At(0, TT - 1))
                    dve.wait_ge(a_back, 16 * NB)
                    dve.wait_ge(xn_in, 16)
                    link(dve.tensor_tensor(agg[:], agg[:], xn[:], ALU.add))
                    layer_norm_stats(dve, a_var, a_std, link, agg, 1)
                    link(normalize(dve, agg, agg))
                    dve.wait_ge(vecs_in, 48)

                    def hot(a):
                        if a.c >= 2:
                            wait_done(dve, v_ready, a, 2)
                        dve.tensor_scalar(onehot_st[:, a.slot(2), :], types[:, ds(a.t * P, P)], lane_col[0:T, 0:1], None, ALU.is_equal).then_inc(v_hot, 1)

                    def node_rows(t, a):
                        return t[:, ds(a.t, 1), :].rearrange("p b c -> p (b c)")

                    def scale(a):
                        wait_done(dve, v_ready, a)
                        dve.tensor_tensor(node_rows(agg, a), node_rows(agg, a), ps_v[:, a.slot(2), 0:D], ALU.mult).then_inc(v_scaled, 1)

                    def shift(a):
                        wait_done(dve, v_scaled, a)
                        dve.tensor_tensor(node_rows(agg, a), node_rows(agg, a), ps_v[:, a.slot(2), D:2 * D], ALU.add).then_inc(v_used, 1)

                    def add_to_x(a):
                        wait_done(dve, v_used, a)
                        dve.tensor_tensor(node_rows(res, a), node_rows(res, a), node_rows(agg, a), ALU.add)

                    def step(a):
                        if not isinstance(a.t, int) or a.t + 1 < NB:
                            hot(a + 1)
                        if a.c >= 1:
                            add_to_x(a + -1)
                        scale(a)
                        shift(a)

                    hot(At(0, 0))
                    walk(dve, NB, step)
                    add_to_x(At(0, NB - 1))

                @block.tensor
                def _(pe):
                    pe.wait_ge(vecs_in, 48)

                    def turn_node(a):
                        h = a.slot(2)
                        pe.wait_ge(a_in[a.slot(4)], (a.turn(4) + 1) * 16)
                        wait_done(pe, at_ready, a, 2)
                        for k in range(KD):
                            last = pe.transpose(ps_t[:, h, k * P:(k + 1) * P], nodes[:, a.slot(4), k * P:(k + 1) * P], ident[:])
                        last.then_inc(a_turned, 1)

                    def project(a):
                        h = a.slot(2)
                        ty = pe.value_load(tile_type_i[0:1, ds(a.t, 1)], min_val=0, max_val=T - 1)
                        wait_done(pe, at_ready, a)
                        wait_done(pe, y_copied, a, 2)
                        for k in range(KD):
                            last = pe.matmul(ps_o[:, h, 0:D], x_t[:, h, k, :], wa[:, ds(ty * KD + k, 1), :].rearrange("p o c -> p (o c)"),
                                             start=(k == 0), stop=(k == KD - 1))
                        last.then_inc(y_ready, 1)

                    def step(a):
                        if not isinstance(a.t, int) or a.t + 1 < TT:
                            turn_node(a + 1)
                        project(a)

                    turn_node(At(0, 0))
                    walk(pe, TT, step)

                    def spread(a):
                        pe.wait_ge(v_hot, a.t + 1)
                        wait_done(pe, v_used, a, 2)
                        pe.matmul(ps_v[:, a.slot(2), 0:2 * D], onehot_st[:, a.slot(2), :], vecs[:, 0:2, :], start=True, stop=True).then_inc(v_ready, 1)

                    walk(pe, NB, spread)

        rows.close()
        clear_sems()
        X, HID, TOP, XT = d.X, d.HID, d.TOP, d.XT
        FH = HID // P
        ffn = ExitStack()
        with ffn:
            gate = sbuf(ffn, "gate", [P, TOP, NB])
            place_i = sbuf(ffn, "place_i", [P, NB + 4, TOP], I32)
            expert_i = sbuf(ffn, "expert_i", [P, XT], I32)
            b1_t = sbuf(ffn, "b1_t", [P, X * FH])
            ln_t = sbuf(ffn, "ln_t", [P, 2, X * KD])
            b2_all = sbuf(ffn, "b2_all", [P, X, D])
            w2 = sbuf(ffn, "w2", [P, X, FH, D])
            with ExitStack() as ctx:
                tok_t = sbuf(ctx, "tok_t", [P, KD, NPAD])
                wr = sbuf(ctx, "wr", [P, KD, X])
                br_row = sbuf(ctx, "br_row", [1, X])
                logits = sbuf(ctx, "logits", [P, NB, X])
                higher = sbuf(ctx, "higher", [P, NB, X, X])
                equal = sbuf(ctx, "equal", [P, NB, X, X])
                earlier = sbuf(ctx, "earlier", [P, X, X])
                order = sbuf(ctx, "order", [P, NB, X])
                chosen = sbuf(ctx, "chosen", [P, NB, X])
                best = sbuf(ctx, "best", [P, NB])
                groups = Groups(sbuf, ctx, "expert", NB, X, XT)
                expert_f = sbuf(ctx, "expert_f", [P, XT])
                pick = sbuf(ctx, "pick", [P, NB, X])
                picked = sbuf(ctx, "picked_e", [P, TOP, NB, X])
                place_f = sbuf(ctx, "place_f", [P, TOP, NB])
                b1_rows = sbuf(ctx, "b1_rows", [X * FH, P])
                ln_rows = sbuf(ctx, "ln_rows", [X * KD, 2, P])
                tok_st = sbuf(ctx, "tok_st", [P, 2, D])
                place_st = sbuf(ctx, "place_st", [P, 2, TOP], I32)
                ps_t = psum(ctx, "ps_tf", [P, 2, 512])
                ps_l = psum(ctx, "ps_l", [P, 512])
                ps_s = psum(ctx, "ps_s", [P, 3, 512])
                ps_n = psum(ctx, "ps_n", [P, 2, 512])
                f_chain, f_var, f_std, xf_ready, f_turned, f_copied, logits_ready = sems(
                    "f_chain", "f_var", "f_std", "xf_ready", "f_turned", "f_copied", "logits_ready")
                f_in, earlier_set, ex_in, ex_ready, small_turned, chosen_ready, prefix_ready, w2_in = sems(
                    "f_in", "earlier_set", "ex_in", "ex_ready", "small_turned", "chosen_ready", "prefix_ready", "w2_in")
                tok_staged = sems("tok_staged0", "tok_staged1")
                tok_sent = sems("tok_sent0", "tok_sent1")
                block = ctx.enter_context(nc.Block())

                @block.sync
                def _(sp):
                    sp.dma_start(wr[:], Wr.rearrange("(k p) e -> p k e", p=P)).then_inc(f_in, 16)
                    sp.dma_start(br_row[:], br.rearrange("(o e) -> o e", o=1)).then_inc(f_in, 16)
                    sp.dma_start(b1_rows[:], b1.rearrange("e (f p) -> (e f) p", p=P)).then_inc(f_in, 16)
                    sp.dma_start(ln_rows[:, 0, :], ln_g.rearrange("e (k p) -> (e k) p", p=P)).then_inc(f_in, 16)
                    sp.dma_start(ln_rows[:, 1, :], ln_b.rearrange("e (k p) -> (e k) p", p=P)).then_inc(f_in, 16)
                    sp.dma_start(b2_all[:], b2.rearrange("(o e) c -> o e c", o=1).broadcast_to([P, X, D])).then_inc(f_in, 16)
                    sp.dma_start(w2[:].rearrange("p e f c -> p (e f) c"), W2.rearrange("e (f p) c -> p (e f) c", p=P)).then_inc(w2_in, 16)
                    sp.wait_ge(w2_in, 16)

                @block.gpsimd
                def _(pool):
                    pool.iota(equal[:, 0], [[1, X], [-1, X]], base=0, channel_multiplier=0,
                              allow_small_or_imprecise_dtypes=True).then_inc(earlier_set, 1)
                    pool.wait_ge(earlier_set, 1)
                    pool.tensor_scalar(earlier[:], equal[:, 0], 0.0, None, ALU.is_gt).then_inc(earlier_set, 1)

                    def send(a):
                        s = a.slot(2)
                        pool.wait_ge(tok_staged[s], a.turn(2) + 1)
                        pool.sem_inc(pool_turn, 1)
                        for n in range(TOP):
                            pool.indirect_dma_start(sorted_dram[:, :], bass.IndirectOffsetOnAxis(ap=place_st[:, s, n:n + 1], axis=0),
                                                    tok_st[:, s, :], None).then_inc(tok_sent[s], 16)

                    walk(pool, NB, send)
                    pool.wait_ge(tok_sent[0], 16 * TOP * (NB - NB // 2))
                    pool.wait_ge(tok_sent[1], 16 * TOP * (NB // 2))

                @block.vector
                def _(dve):
                    link = Chain(dve, f_chain)
                    layer_norm_stats(dve, f_var, f_std, link, res, 1)
                    normalize(dve, xn, res, xf_ready)
                    dve.wait_ge(logits_ready, 1)
                    link(dve.tensor_copy(logits[:].rearrange("p b e -> p (b e)"), ps_l[:, 0:NB * X]))
                    dve.wait_ge(earlier_set, 2)
                    mine = logits[:].unsqueeze(3).broadcast_to([P, NB, X, X])
                    other = logits[:].unsqueeze(2).broadcast_to([P, NB, X, X])
                    link(dve.tensor_tensor(higher[:], other, mine, ALU.is_gt))
                    link(dve.tensor_tensor(equal[:], other, mine, ALU.is_equal))
                    link(dve.tensor_tensor(equal[:], equal[:], earlier[:].unsqueeze(1).broadcast_to([P, NB, X, X]), ALU.mult))
                    link(dve.tensor_tensor(higher[:], higher[:], equal[:], ALU.add))
                    link(dve.tensor_reduce(order[:], higher[:], AX, ALU.add))
                    dve.tensor_scalar(chosen[:], order[:], float(TOP), None, ALU.is_lt).then_inc(chosen_ready, 1)
                    link(dve.tensor_reduce(best[:], logits[:], AX, ALU.max))
                    dve.tensor_tensor(logits[:], logits[:], best[:].unsqueeze(2).broadcast_to([P, NB, X]), ALU.subtract).then_inc(ex_in, 1)
                    layer_norm_stats(dve, f_var, f_std, link, xn, 2)
                    dve.wait_ge(prefix_ready, 1)
                    groups.place(dve, link, ps_n, ones, lane, expert_f)
                    link(dve.tensor_copy(expert_i[:], expert_f[:]))
                    dve.wait_ge(ex_ready, 1)
                    for n in range(TOP):
                        link(dve.tensor_scalar(pick[:], order[:], float(n), None, ALU.is_equal))
                        link(dve.tensor_tensor(picked[:, n], pick[:], groups.row_of[:], ALU.mult))
                        link(dve.tensor_reduce(place_f[:, n, :], picked[:, n], AX, ALU.add))
                        link(dve.tensor_tensor(pick[:], pick[:], logits[:], ALU.mult))
                        link(dve.tensor_reduce(gate[:, n, :], pick[:], AX, ALU.add))
                    link(dve.memset(place_i[:, NB:, :], 0))
                    link(dve.tensor_copy(place_i[:, 0:NB, :], place_f[:].rearrange("p n b -> p b n")))
                    link(dve.tensor_tensor(best[:], gate[:, 0, :], gate[:, 1, :], ALU.add))
                    link(dve.reciprocal(best[:], best[:]))
                    link(dve.tensor_tensor(gate[:], gate[:], best[:].unsqueeze(1).broadcast_to([P, TOP, NB]), ALU.mult))
                    dve.wait_ge(small_turned, 3)
                    for n in range(2):
                        link(dve.tensor_copy(ln_t[:, n, :], ps_s[:, n, 0:X * KD]))
                    link(dve.tensor_copy(b1_t[:], ps_s[:, 2, 0:X * FH]))

                    def stage(a):
                        s = a.slot(2)
                        wait_slot(dve, tok_sent[s], a, 2, 16 * TOP)
                        dve.tensor_scalar(tok_st[:, s, :], xn[:, ds(a.t, 1), :].rearrange("p b c -> p (b c)"), mean[:, ds(a.t, 1)],
                                          rstd[:, ds(a.t, 1)], ALU.subtract, ALU.mult)
                        dve.tensor_copy(place_st[:, s, :], place_i[:, ds(a.t, 1), :].rearrange("p b n -> p (b n)")).then_inc(tok_staged[s], 1)

                    walk(dve, NB, stage)

                @block.scalar
                def _(act):
                    act.wait_ge(f_var, 1)
                    act.activation(rstd[:], tmp_b[:], ACT.Sqrt).then_inc(f_std, 1)

                    def copy_turned(a):
                        wait_done(act, f_turned, a)
                        act.copy(tok_t[:, :, ds(a.t * P, P)], ps_t[:, a.slot(2), 0:D].rearrange("p (k c) -> p k c", k=KD)).then_inc(f_copied, 1)

                    walk(act, NB, copy_turned)
                    act.wait_ge(ex_in, 1)
                    act.activation(logits[:], logits[:], ACT.Exp).then_inc(ex_ready, 1)
                    act.wait_ge(f_var, 2)
                    act.activation(rstd[:], tmp_b[:], ACT.Sqrt).then_inc(f_std, 1)

                @block.tensor
                def _(pe):
                    pe.wait_ge(f_in, 96)
                    for m in range(2):
                        pe.transpose(ps_s[:, m, 0:X * KD], ln_rows[:, m, :], ident[0:X * KD, 0:X * KD]).then_inc(small_turned, 1)
                    pe.transpose(ps_s[:, 2, 0:X * FH], b1_rows[:], ident[0:X * FH, 0:X * FH]).then_inc(small_turned, 1)
                    for b in range(NB + 2):
                        if b < NB:
                            pe.wait_ge(xf_ready, b + 1)
                            if b >= 2:
                                pe.wait_ge(f_copied, b - 1)
                            for k in range(KD):
                                last = pe.transpose(ps_t[:, b % 2, k * P:(k + 1) * P], xn[:, b, k * P:(k + 1) * P], ident[:])
                            last.then_inc(f_turned, 1)
                        if b >= 2:
                            c = b - 2
                            pe.wait_ge(f_copied, c + 1)
                            for k in range(KD):
                                pe.matmul(ps_l[:, c * X:(c + 1) * X], tok_t[:, k, c * P:(c + 1) * P], wr[:, k, :], start=(k == 0), stop=False)
                            last = pe.matmul(ps_l[:, c * X:(c + 1) * X], ones[0:1, :], br_row[:], start=False, stop=True)
                    last.then_inc(logits_ready, 1)
                    pe.wait_ge(chosen_ready, 1)
                    flat = chosen[:].rearrange("p b e -> p (b e)")
                    pe.matmul(ps_n[:, 0, 0:NB * X], before[:], flat, start=True, stop=True)
                    pe.matmul(ps_n[:, 1, 0:NB * X], ones[:], flat, start=True, stop=True).then_inc(prefix_ready, 1)

            with ExitStack() as ctx:
                w1 = sbuf(ctx, "w1", [P, 2, KD, HID])
                tok = sbuf(ctx, "tok", [P, 4, D])
                x_e = sbuf(ctx, "x_e", [P, 2, KD, P])
                hid = sbuf(ctx, "hid", [P, 2, FH, P])
                y_out = sbuf(ctx, "y_out", [P, 2, D])
                ps_t = psum(ctx, "ps_te", [P, 2, 512])
                ps_h = psum(ctx, "ps_h", [P, 2, 2, 512])
                ps_y = psum(ctx, "ps_y", [P, 2, 512])
                tok_in = sems(*[f"tok_in{n}" for n in range(4)])
                w1_in = sems("w1_in0", "w1_in1")
                y_stored = sems("y_stored0", "y_stored1")
                tok_turned, xe_ready, h_ready, hid_ready, y_ready, y_copied = sems(
                    "tok_turned", "xe_ready", "h_ready", "hid_ready", "y_ready", "y_copied")
                block = ctx.enter_context(nc.Block())

                @block.sync
                def _(sp):
                    def load(a):
                        s = a.slot(4)
                        wait_done(sp, tok_turned, a, 4)
                        sp.dma_start(tok[:, s, :], sorted_dram[ds(a.t * P, P), :]).then_inc(tok_in[s], 16)
                        e = sp.value_load(expert_i[0:1, ds(a.t, 1)], min_val=0, max_val=X - 1)
                        if a.c >= 2:
                            sp.wait_ge(h_ready, a.t * 2 - 2)
                        sp.dma_start(w1[:, a.slot(2)], W1[ds(e, 1), :, :].rearrange("o (k p) h -> p (o k) h", p=P)).then_inc(w1_in[a.slot(2)], 16)

                    walk(sp, XT, load)

                @block.gpsimd
                def _(pool):
                    def store(a):
                        h = a.slot(2)
                        pool.wait_ge(y_copied, a.t + 1)
                        pool.dma_start(expert_out_dram[ds(a.t * P, P), :], y_out[:, h, :]).then_inc(y_stored[h], 16)

                    walk(pool, XT, store)
                    pool.wait_ge(y_stored[0], 16 * (XT - XT // 2))
                    pool.wait_ge(y_stored[1], 16 * (XT // 2))

                @block.vector
                def _(dve):
                    def scale(a):
                        h = a.slot(2)
                        e = dve.value_load(expert_i[0:1, ds(a.t, 1)], min_val=0, max_val=X - 1)
                        wait_done(dve, tok_turned, a)
                        if a.c >= 2:
                            dve.wait_ge(h_ready, a.t * 2 - 2)
                        for k in range(KD):
                            last = dve.tensor_scalar(x_e[:, h, k, :], ps_t[:, h, k * P:(k + 1) * P], ln_t[:, 0, ds(e * KD + k, 1)],
                                                     ln_t[:, 1, ds(e * KD + k, 1)], ALU.mult, ALU.add)
                        last.then_inc(xe_ready, 1)

                    def copy_y(a):
                        e = dve.value_load(expert_i[0:1, ds(a.t, 1)], min_val=0, max_val=X - 1)
                        h = a.slot(2)
                        wait_done(dve, y_ready, a)
                        wait_slot(dve, y_stored[h], a, 2, 16)
                        dve.tensor_tensor(y_out[:, h, :], ps_y[:, h, 0:D], b2_all[:, ds(e, 1), :].rearrange("p o c -> p (o c)"),
                                          ALU.add).then_inc(y_copied, 1)

                    def step(a):
                        scale(a)
                        if a.c >= 2:
                            copy_y(a + -2)

                    walk(dve, XT, step)
                    copy_y(At(0, XT - 2))
                    copy_y(At(0, XT - 1))

                @block.scalar
                def _(act):
                    def gelu(a):
                        h = a.slot(2)
                        e = act.value_load(expert_i[0:1, ds(a.t, 1)], min_val=0, max_val=X - 1)
                        wait_done(act, y_ready, a, 2)
                        for f in range(FH):
                            if f % 4 == 0:
                                act.wait_ge(h_ready, a.t * 2 + f // 4 + 1)
                            act.activation(hid[:, h, f, :], ps_h[:, h, f // 4, f % 4 * P:(f % 4 + 1) * P], ACT.Gelu,
                                           bias=b1_t[:, ds(e * FH + f, 1)]).then_inc(hid_ready, 1)

                    walk(act, XT, gelu)

                @block.tensor
                def _(pe):
                    def turn_tok(a):
                        h = a.slot(2)
                        pe.wait_ge(tok_in[a.slot(4)], (a.turn(4) + 1) * 16)
                        wait_done(pe, xe_ready, a, 2)
                        for k in range(KD):
                            last = pe.transpose(ps_t[:, h, k * P:(k + 1) * P], tok[:, a.slot(4), k * P:(k + 1) * P], ident[:])
                        last.then_inc(tok_turned, 1)

                    def first(a):
                        h = a.slot(2)
                        wait_done(pe, xe_ready, a)
                        pe.wait_ge(w1_in[h], (a.turn(2) + 1) * 16)
                        if a.c >= 2:
                            pe.wait_ge(hid_ready, a.t * FH - FH)
                        for f in range(FH):
                            for k in range(KD):
                                last = pe.matmul(ps_h[:, h, f // 4, f % 4 * P:(f % 4 + 1) * P], w1[:, h, k, f * P:(f + 1) * P], x_e[:, h, k, :],
                                                 start=(k == 0), stop=(k == KD - 1))
                            if f % 4 == 3:
                                last.then_inc(h_ready, 1)

                    def second(a):
                        h = a.slot(2)
                        e = pe.value_load(expert_i[0:1, ds(a.t, 1)], min_val=0, max_val=X - 1)
                        wait_done(pe, y_copied, a, 2)
                        for f in range(FH):
                            pe.wait_ge(hid_ready, a.t * FH + f + 1)
                            last = pe.matmul(ps_y[:, h, 0:D], hid[:, h, f, :], w2[:, ds(e, 1), f, :].rearrange("p o c -> p (o c)"),
                                             start=(f == 0), stop=(f == FH - 1))
                        last.then_inc(y_ready, 1)

                    def step(a):
                        if a.c == 0:
                            turn_tok(a)
                        if a.c + 1 < XT:
                            turn_tok(a + 1)
                        first(a)
                        if a.c:
                            second(a + -1)

                    walk(pe, XT, step)
                    second(At(0, XT - 1))

            with ExitStack() as ctx:
                got = sbuf(ctx, "got", [P, 4, TOP, D])
                get_st = sbuf(ctx, "get_st", [P, 4, TOP], I32)
                got_in = sems(*[f"got_in{n}" for n in range(4)])
                get_staged, got_added, out_done = sems("get_staged", "got_added", "out_done")
                block = ctx.enter_context(nc.Block())

                @block.gpsimd
                def _(pool):
                    def get(a):
                        s = a.slot(4)
                        pool.wait_ge(get_staged, a.t + 1)
                        if a.c >= 4:
                            pool.wait_ge(got_added, a.t * TOP - 6)
                        pool.sem_inc(pool_turn, 1)
                        for n in range(TOP):
                            pool.indirect_dma_start(got[:, s, n, :], None, expert_out_dram[:, :],
                                                    bass.IndirectOffsetOnAxis(ap=get_st[:, s, n:n + 1], axis=0)).then_inc(got_in[s], 16)

                    walk(pool, NB, get)

                @block.vector
                def _(dve):
                    def stage(a):
                        s = a.slot(4)
                        wait_slot(dve, got_in[s], a, 4, 16 * TOP)
                        dve.tensor_copy(get_st[:, s, :], place_i[:, ds(a.t, 1), :].rearrange("p b n -> p (b n)")).then_inc(get_staged, 1)

                    def add(a):
                        s = a.slot(4)
                        dve.wait_ge(got_in[s], (a.turn(4) + 1) * 16 * TOP)
                        row = res[:, ds(a.t, 1), :].rearrange("p b c -> p (b c)")
                        for n in range(TOP):
                            dve.scalar_tensor_tensor(row, got[:, s, n, :], gate[:, n, ds(a.t, 1)], row, ALU.mult, ALU.add).then_inc(got_added, 1)
                            dve.wait_ge(got_added, a.t * TOP + n + 1)

                    def step(a):
                        add(a)
                        if not isinstance(a.t, int) or a.t + 4 < NB:
                            stage(a + 4)

                    for t in range(4):
                        stage(At(0, t))
                    walk(dve, NB, step)

                @block.sync
                def _(sp):
                    sp.wait_ge(got_added, NB * TOP)
                    sp.dma_start(out[0:d.FULL * P, :].rearrange("(b p) c -> p b c", p=P), res[:, 0:d.FULL, :]).then_inc(out_done, 16)
                    sp.dma_start(out[d.FULL * P:N, :], res[0:d.TAIL, d.FULL, :]).then_inc(out_done, 16)
                    sp.wait_ge(out_done, 32)


_INS = ['x', 'src', 'dst', 'edge_attr_5', 'node_type_19', 'L0_gnn_Wk', 'L0_gnn_bk', 'L0_gnn_Wq', 'L0_gnn_bq',
        'L0_gnn_Wv', 'L0_gnn_bv', 'L0_gnn_Wa', 'L0_gnn_ba', 'L0_gnn_gamma', 'L0_gnn_beta', 'L0_gnn_w_time',
        'L0_gnn_b_time', 'L0_ffn_Wr', 'L0_ffn_br', 'L0_ffn_ln_g', 'L0_ffn_ln_b', 'L0_ffn_W1', 'L0_ffn_b1',
        'L0_ffn_W2', 'L0_ffn_b2']


def kernel(**inputs):
    import numpy as _np
    import concourse.bacc as _bacc
    from concourse import mybir as _mybir
    from concourse.bass_utils import run_bass_kernel_spmd as _run

    nc = _bacc.Bacc("TRN2", target_bir_lowering=False, num_devices=1)
    arrays, args = {}, []
    for name in _INS:
        a = _np.ascontiguousarray(inputs[name])
        arrays[f"in_{name}"] = a
        args.append(nc.dram_tensor(f"in_{name}", a.shape, _mybir.dt.from_np(a.dtype), kind="ExternalInput").ap())
    args.append(nc.dram_tensor("out_x", inputs["x"].shape, _mybir.dt.float32, kind="ExternalOutput").ap())
    gnn_ffn_kernel(nc, *args)
    r = _run(nc, [arrays], core_ids=[0])
    return r.results[0]["out_x"]
```
